# Optimizing a Trainium2 kernel written in Bass

```python
import numpy as np
import jax
import jax.numpy as jnp

def _softmax(x, axis=-1):
    return jax.nn.softmax(x, axis=axis)

def _gelu(x):
    return jax.nn.gelu(x, approximate=True)

def _silu(x):
    return jax.nn.silu(x)

def _sigmoid(x):
    return jax.nn.sigmoid(x)

def _layernorm(x, axis=-1, eps=1e-05):
    m = jnp.mean(x, axis=axis, keepdims=True)
    v = jnp.var(x, axis=axis, keepdims=True)
    return (x - m) / jnp.sqrt(v + eps)

def _scatter_add(tgt, idx, src, axis=0):
    return tgt.at[idx].add(src)

def _segment_sum(src, seg, n):
    return jax.ops.segment_sum(src, seg, n)
kernel_name = 'mk_gnn_preln_d4_gnn_r32_753740'

def setup_inputs(seed: int=0):
    np.random.seed(seed)
    _w = jnp.asarray

    def _rec_inputs():
        import jax
        import jax.numpy as jnp
        _gk = jax.random.key(seed)
        x = -0.000202 + 1 * jax.random.normal(jax.random.fold_in(_gk, 1), (3125, 128), jnp.float32)
        _s = jax.random.randint(jax.random.fold_in(_gk, 2), (50000,), 0, 3125, jnp.int32)
        _d = jax.random.randint(jax.random.fold_in(_gk, 3), (50000,), 0, 3125, jnp.int32)
        _loop = jnp.arange(3125, dtype=jnp.int32)
        src = jnp.concatenate([_s, _d, _loop])
        dst = jnp.concatenate([_d, _s, _loop])
        _o = jnp.argsort(dst, stable=True)
        src = src[_o]
        dst = dst[_o]
        edge_attr_64 = -9.77346e-05 + 0.999888 * jax.random.normal(jax.random.fold_in(_gk, 11), (103125, 64), jnp.float32)
        edge_type_64 = jax.random.randint(jax.random.fold_in(_gk, 13), (103125,), 0, 64, jnp.int32)
        edge_weight1 = jax.random.uniform(jax.random.fold_in(_gk, 14), (103125, 1), jnp.float32, 0.0, 0.999998)
        node_vec1 = jax.random.uniform(jax.random.fold_in(_gk, 15), (3125, 1), jnp.float32, 0.0, 0.999884)
        return (x, src, dst, edge_attr_64, edge_type_64, edge_weight1, node_vec1)
    x, src, dst, edge_attr_64, edge_type_64, edge_weight1, node_vec1 = _rec_inputs()

    def _L0_gnn_setup():
        import jax, jax.numpy as jnp
        import numpy as np
        N_NODES = 50000
        N_EDGES = 25000
        HIDDEN = 128
        HEADS = 8
        HEAD_DIM = HIDDEN // HEADS
        N_REL = 64
        SCALE = np.sqrt(HEAD_DIM).astype(np.float32)
        key = jax.random.key(seed)
        ks = jax.random.split(key, 12)
        s = 1.0 / np.sqrt(2 * HIDDEN)
        s2 = 1.0 / np.sqrt(HIDDEN)
        return {'node_features': jax.random.normal(ks[0], (N_NODES, HIDDEN), jnp.float32), 'query_embedding': jax.random.normal(ks[1], (1, HIDDEN), jnp.float32), 'relation_embeddings': jax.random.normal(ks[2], (N_REL, HIDDEN), jnp.float32), 'Wq': jax.random.uniform(ks[3], (2 * HIDDEN, HIDDEN), jnp.float32, -s, s), 'bq': jnp.zeros((HIDDEN,), jnp.float32), 'Wk': jax.random.uniform(ks[4], (2 * HIDDEN, HIDDEN), jnp.float32, -s, s), 'bk': jnp.zeros((HIDDEN,), jnp.float32), 'Wv': jax.random.uniform(ks[5], (HIDDEN, HIDDEN), jnp.float32, -s2, s2), 'bv': jnp.zeros((HIDDEN,), jnp.float32), 'Wo': jax.random.uniform(ks[6], (HIDDEN, HIDDEN), jnp.float32, -s2, s2), 'bo': jnp.zeros((HIDDEN,), jnp.float32), 'edge_index': jax.random.randint(ks[7], (2, N_EDGES), 0, N_NODES, jnp.int64), 'edge_type': jax.random.randint(ks[8], (N_EDGES,), 0, N_REL, jnp.int64)}
    _L0_gnn_all = _L0_gnn_setup()
    _L0_gnn_in = {k: v for k, v in _L0_gnn_all.items() if k in ('query_embedding', 'relation_embeddings', 'Wq', 'bq', 'Wk', 'bk', 'Wv', 'bv', 'Wo', 'bo')}
    del _L0_gnn_all

    def _L1_gnn_setup():
        import jax, jax.numpy as jnp
        import numpy as np
        N = 50000
        E = 25000
        F_IN = 128
        DIM_H = 16
        HEADS = 8
        NEG_SLOPE = 0.2

        def gat_conv(x, src, dst, W, a_src, a_dst, b):
            n = x.shape[0]
            H, D = a_src.shape
            h = (x @ W).reshape(n, H, D)
            e_src = jnp.sum(h * a_src, axis=-1)
            e_dst = jnp.sum(h * a_dst, axis=-1)
            e = jax.nn.leaky_relu(e_src[src] + e_dst[dst], NEG_SLOPE)
            m = jax.lax.stop_gradient(jax.ops.segment_max(e, dst, num_segments=n))
            w = jnp.exp(e - m[dst])
            denom = jax.ops.segment_sum(w, dst, num_segments=n)
            alpha = w / (denom[dst] + 1e-16)
            out = jax.ops.segment_sum(h[src] * alpha[:, :, None], dst, num_segments=n)
            return out.reshape(n, H * D) + b
        key = jax.random.key(seed)
        ks = jax.random.split(key, 10)
        p = lambda k, shape: jax.random.normal(k, shape, jnp.float32) * 0.1
        x = jax.random.normal(ks[0], (N, F_IN), jnp.float32)
        edge_index = jax.random.randint(ks[1], (2, E), 0, N, dtype=jnp.int64)
        W1 = p(ks[2], (F_IN, HEADS * DIM_H))
        a_src1 = p(ks[3], (HEADS, DIM_H))
        a_dst1 = p(ks[4], (HEADS, DIM_H))
        b1 = jnp.zeros((HEADS * DIM_H,), jnp.float32)
        W2 = p(ks[5], (HEADS * DIM_H, HEADS * DIM_H))
        a_src2 = p(ks[6], (HEADS, DIM_H))
        a_dst2 = p(ks[7], (HEADS, DIM_H))
        b2 = jnp.zeros((HEADS * DIM_H,), jnp.float32)
        return {'x': x, 'edge_index': edge_index, 'W1': W1, 'a_src1': a_src1, 'a_dst1': a_dst1, 'b1': b1, 'W2': W2, 'a_src2': a_src2, 'a_dst2': a_dst2, 'b2': b2}
    _L1_gnn_all = _L1_gnn_setup()
    _L1_gnn_in = {k: v for k, v in _L1_gnn_all.items() if k in ('W1', 'a_src1', 'a_dst1', 'b1', 'W2', 'a_src2', 'a_dst2', 'b2')}
    del _L1_gnn_all

    def _L2_gnn_setup():
        import jax, jax.numpy as jnp
        import numpy as np
        N_NODES, N_EDGES = (50000, 25000)
        NODE_DIM, EDGE_DIM, HIDDEN, HEADS = (128, 64, 128, 8)
        HEAD_DIM = HIDDEN // HEADS
        key = jax.random.key(seed)
        ks = jax.random.split(key, 24)

        def lin(k, fan_in, fan_out):
            lim = 1.0 / np.sqrt(fan_in)
            kw, kb = jax.random.split(k)
            W = jax.random.uniform(kw, (fan_in, fan_out), jnp.float32, -lim, lim)
            b = jax.random.uniform(kb, (fan_out,), jnp.float32, -lim, lim)
            return (W, b)
        inp = {}
        inp['nodes'] = jax.random.normal(ks[0], (N_NODES, NODE_DIM), jnp.float32)
        inp['edges'] = jax.random.normal(ks[1], (N_EDGES, EDGE_DIM), jnp.float32)
        inp['edge_index'] = jax.random.randint(ks[2], (2, N_EDGES), 0, N_NODES, jnp.int32)
        inp['conservation_scores'] = jax.random.uniform(ks[3], (N_NODES, 1), jnp.float32)
        inp['distances'] = jax.random.uniform(ks[4], (N_EDGES, 1), jnp.float32)
        inp['Wq'], inp['bq'] = lin(ks[5], NODE_DIM, HIDDEN)
        inp['Wk'], inp['bk'] = lin(ks[6], NODE_DIM, HIDDEN)
        inp['Wv'], inp['bv'] = lin(ks[7], NODE_DIM, HIDDEN)
        inp['We'], inp['be'] = lin(ks[8], EDGE_DIM, HEADS)
        inp['Wc1'], inp['bc1'] = lin(ks[9], 1, 32)
        inp['Wc2'], inp['bc2'] = lin(ks[10], 32, HEADS)
        inp['Wd1'], inp['bd1'] = lin(ks[11], 1, 16)
        inp['Wd2'], inp['bd2'] = lin(ks[12], 16, HEADS)
        inp['Wo'], inp['bo'] = lin(ks[13], HIDDEN, NODE_DIM)
        inp['gamma'] = jnp.ones((NODE_DIM,), jnp.float32)
        inp['beta'] = jnp.zeros((NODE_DIM,), jnp.float32)
        return inp
    _L2_gnn_all = _L2_gnn_setup()
    _L2_gnn_in = {k: v for k, v in _L2_gnn_all.items() if k in ('Wq', 'bq', 'Wk', 'bk', 'Wv', 'bv', 'We', 'be', 'Wc1', 'bc1', 'Wc2', 'bc2', 'Wd1', 'bd1', 'Wd2', 'bd2', 'Wo', 'bo', 'gamma', 'beta')}
    del _L2_gnn_all

    def _L3_gnn_setup():
        import jax, jax.numpy as jnp
        import numpy as np
        N_NODES = 3125
        EMB_DIM = 128
        N_EDGES = 50000
        key = jax.random.key(seed)
        k1, k2 = jax.random.split(key)
        edge_index = jax.random.randint(k1, (2, N_EDGES), 0, N_NODES, dtype=jnp.int64 if jax.config.read('jax_enable_x64') else jnp.int32)
        embedding = jax.random.normal(k2, (N_NODES, EMB_DIM), dtype=jnp.float32)
        return {'edge_index': edge_index, 'embedding': embedding}
    _L3_gnn_all = _L3_gnn_setup()
    _L3_gnn_in = {k: v for k, v in _L3_gnn_all.items() if k in ()}
    del _L3_gnn_all
    return {'x': x, 'src': src, 'dst': dst, 'edge_attr_64': edge_attr_64, 'edge_type_64': edge_type_64, 'edge_weight1': edge_weight1, 'node_vec1': node_vec1, 'L0_gnn_query_embedding': _L0_gnn_in['query_embedding'], 'L0_gnn_relation_embeddings': _L0_gnn_in['relation_embeddings'], 'L0_gnn_Wq': _L0_gnn_in['Wq'], 'L0_gnn_bq': _L0_gnn_in['bq'], 'L0_gnn_Wk': _L0_gnn_in['Wk'], 'L0_gnn_bk': _L0_gnn_in['bk'], 'L0_gnn_Wv': _L0_gnn_in['Wv'], 'L0_gnn_bv': _L0_gnn_in['bv'], 'L0_gnn_Wo': _L0_gnn_in['Wo'], 'L0_gnn_bo': _L0_gnn_in['bo'], 'L1_gnn_W1': _L1_gnn_in['W1'], 'L1_gnn_a_src1': _L1_gnn_in['a_src1'], 'L1_gnn_a_dst1': _L1_gnn_in['a_dst1'], 'L1_gnn_b1': _L1_gnn_in['b1'], 'L1_gnn_W2': _L1_gnn_in['W2'], 'L1_gnn_a_src2': _L1_gnn_in['a_src2'], 'L1_gnn_a_dst2': _L1_gnn_in['a_dst2'], 'L1_gnn_b2': _L1_gnn_in['b2'], 'L2_gnn_Wq': _L2_gnn_in['Wq'], 'L2_gnn_bq': _L2_gnn_in['bq'], 'L2_gnn_Wk': _L2_gnn_in['Wk'], 'L2_gnn_bk': _L2_gnn_in['bk'], 'L2_gnn_Wv': _L2_gnn_in['Wv'], 'L2_gnn_bv': _L2_gnn_in['bv'], 'L2_gnn_We': _L2_gnn_in['We'], 'L2_gnn_be': _L2_gnn_in['be'], 'L2_gnn_Wc1': _L2_gnn_in['Wc1'], 'L2_gnn_bc1': _L2_gnn_in['bc1'], 'L2_gnn_Wc2': _L2_gnn_in['Wc2'], 'L2_gnn_bc2': _L2_gnn_in['bc2'], 'L2_gnn_Wd1': _L2_gnn_in['Wd1'], 'L2_gnn_bd1': _L2_gnn_in['bd1'], 'L2_gnn_Wd2': _L2_gnn_in['Wd2'], 'L2_gnn_bd2': _L2_gnn_in['bd2'], 'L2_gnn_Wo': _L2_gnn_in['Wo'], 'L2_gnn_bo': _L2_gnn_in['bo'], 'L2_gnn_gamma': _L2_gnn_in['gamma'], 'L2_gnn_beta': _L2_gnn_in['beta']}

def reference(x, src, dst, edge_attr_64, edge_type_64, edge_weight1, node_vec1, L0_gnn_query_embedding, L0_gnn_relation_embeddings, L0_gnn_Wq, L0_gnn_bq, L0_gnn_Wk, L0_gnn_bk, L0_gnn_Wv, L0_gnn_bv, L0_gnn_Wo, L0_gnn_bo, L1_gnn_W1, L1_gnn_a_src1, L1_gnn_a_dst1, L1_gnn_b1, L1_gnn_W2, L1_gnn_a_src2, L1_gnn_a_dst2, L1_gnn_b2, L2_gnn_Wq, L2_gnn_bq, L2_gnn_Wk, L2_gnn_bk, L2_gnn_Wv, L2_gnn_bv, L2_gnn_We, L2_gnn_be, L2_gnn_Wc1, L2_gnn_bc1, L2_gnn_Wc2, L2_gnn_bc2, L2_gnn_Wd1, L2_gnn_bd1, L2_gnn_Wd2, L2_gnn_bd2, L2_gnn_Wo, L2_gnn_bo, L2_gnn_gamma, L2_gnn_beta):
    import jax
    import jax.numpy as jnp

    def _L0_gnn_ref(node_features, query_embedding, relation_embeddings, Wq, bq, Wk, bk, Wv, bv, Wo, bo, edge_index, edge_type):
        import jax, jax.numpy as jnp
        import numpy as np
        N_NODES = 50000
        N_EDGES = 25000
        HIDDEN = 128
        HEADS = 8
        HEAD_DIM = HIDDEN // HEADS
        N_REL = 64
        SCALE = np.sqrt(HEAD_DIM).astype(np.float32)
        n = node_features.shape[0]
        q_exp = jnp.broadcast_to(query_embedding, (n, HIDDEN))
        nq = jnp.concatenate([node_features, q_exp], axis=-1)
        q = (nq @ Wq + bq).reshape(n, HEADS, HEAD_DIM)
        k = (nq @ Wk + bk).reshape(n, HEADS, HEAD_DIM)
        v = (node_features @ Wv + bv).reshape(n, HEADS, HEAD_DIM)
        src, dst = (edge_index[0], edge_index[1])
        rel_bias = relation_embeddings[edge_type].reshape(-1, HEADS, HEAD_DIM)
        scores = jnp.sum(q[dst] * (k[src] + rel_bias), axis=-1) / SCALE
        seg_max = jax.ops.segment_max(scores, dst, num_segments=n)
        seg_max = jnp.maximum(seg_max, 0.0)
        exp_s = jnp.exp(scores - seg_max[dst])
        seg_sum = jax.ops.segment_sum(exp_s, dst, num_segments=n)
        attn = exp_s / (seg_sum[dst] + 1e-08)
        messages = attn[:, :, None] * v[src]
        out = jax.ops.segment_sum(messages, dst, num_segments=n)
        out = out.reshape(n, HIDDEN)
        return out @ Wo + bo

    def _L1_gnn_ref(x, edge_index, W1, a_src1, a_dst1, b1, W2, a_src2, a_dst2, b2):
        import jax, jax.numpy as jnp
        import numpy as np
        N = 50000
        E = 25000
        F_IN = 128
        DIM_H = 16
        HEADS = 8
        NEG_SLOPE = 0.2

        def gat_conv(x, src, dst, W, a_src, a_dst, b):
            n = x.shape[0]
            H, D = a_src.shape
            h = (x @ W).reshape(n, H, D)
            e_src = jnp.sum(h * a_src, axis=-1)
            e_dst = jnp.sum(h * a_dst, axis=-1)
            e = jax.nn.leaky_relu(e_src[src] + e_dst[dst], NEG_SLOPE)
            m = jax.lax.stop_gradient(jax.ops.segment_max(e, dst, num_segments=n))
            w = jnp.exp(e - m[dst])
            denom = jax.ops.segment_sum(w, dst, num_segments=n)
            alpha = w / (denom[dst] + 1e-16)
            out = jax.ops.segment_sum(h[src] * alpha[:, :, None], dst, num_segments=n)
            return out.reshape(n, H * D) + b
        n = x.shape[0]
        loops = jnp.arange(n, dtype=edge_index.dtype)
        src = jnp.concatenate([edge_index[0], loops])
        dst = jnp.concatenate([edge_index[1], loops])
        h1 = gat_conv(x, src, dst, W1, a_src1, a_dst1, b1)
        h2 = gat_conv(h1, src, dst, W2, a_src2, a_dst2, b2)
        h3 = gat_conv(h2, src, dst, W2, a_src2, a_dst2, b2)
        return jax.nn.log_softmax(h3, axis=1)

    def _L2_gnn_ref(nodes, edges, edge_index, conservation_scores, distances, Wq, bq, Wk, bk, Wv, bv, We, be, Wc1, bc1, Wc2, bc2, Wd1, bd1, Wd2, bd2, Wo, bo, gamma, beta):
        import jax, jax.numpy as jnp
        import numpy as np
        N_NODES, N_EDGES = (50000, 25000)
        NODE_DIM, EDGE_DIM, HIDDEN, HEADS = (128, 64, 128, 8)
        HEAD_DIM = HIDDEN // HEADS
        N = nodes.shape[0]
        src, tgt = (edge_index[0], edge_index[1])
        q = (nodes @ Wq + bq).reshape(N, HEADS, HEAD_DIM)
        k = (nodes @ Wk + bk).reshape(N, HEADS, HEAD_DIM)
        v = (nodes @ Wv + bv).reshape(N, HEADS, HEAD_DIM)
        scores = jnp.einsum('ehd,ehd->eh', q[src], k[tgt]) / np.sqrt(HEAD_DIM)
        scores = scores + edges @ We + be
        cons = jax.nn.sigmoid(jax.nn.relu(conservation_scores @ Wc1 + bc1) @ Wc2 + bc2)
        scores = scores * cons[tgt]
        scores = scores + jax.nn.relu(distances @ Wd1 + bd1) @ Wd2 + bd2
        seg_max = jax.ops.segment_max(scores, tgt, num_segments=N)
        w = jnp.exp(scores - seg_max[tgt])
        seg_sum = jax.ops.segment_sum(w, tgt, num_segments=N)
        weights = w / seg_sum[tgt]
        attended = weights[..., None] * v[tgt]
        agg = jax.ops.segment_sum(attended, tgt, num_segments=N).reshape(N, HIDDEN)
        out = agg @ Wo + bo
        x = nodes + out
        mu = jnp.mean(x, axis=-1, keepdims=True)
        var = jnp.var(x, axis=-1, keepdims=True)
        return (x - mu) / jnp.sqrt(var + 1e-05) * gamma + beta

    def _L3_gnn_ref(edge_index, embedding):
        import jax, jax.numpy as jnp
        import numpy as np
        N_NODES = 3125
        EMB_DIM = 128
        N_EDGES = 50000
        N = embedding.shape[0]
        loop = jnp.arange(N, dtype=edge_index.dtype)
        row = jnp.concatenate([edge_index[0], loop])
        col = jnp.concatenate([edge_index[1], loop])
        deg = jax.ops.segment_sum(jnp.ones_like(row, dtype=embedding.dtype), row, num_segments=N)
        deg_inv_sqrt = jnp.where(deg > 0, jax.lax.rsqrt(jnp.maximum(deg, 1.0)), 0.0)
        norm = deg_inv_sqrt[row] * deg_inv_sqrt[col]
        msgs = norm[:, None] * embedding[row]
        out = jax.ops.segment_sum(msgs, col, num_segments=N)
        return out
    edge_index = jnp.stack([src, dst])
    h = jnp.maximum(_layernorm(x, axis=-1), 0.0)
    x = x + _L0_gnn_ref(h, L0_gnn_query_embedding, L0_gnn_relation_embeddings, L0_gnn_Wq, L0_gnn_bq, L0_gnn_Wk, L0_gnn_bk, L0_gnn_Wv, L0_gnn_bv, L0_gnn_Wo, L0_gnn_bo, edge_index, edge_type_64)
    h = jnp.maximum(_layernorm(x, axis=-1), 0.0)
    x = x + _L1_gnn_ref(h, edge_index, L1_gnn_W1, L1_gnn_a_src1, L1_gnn_a_dst1, L1_gnn_b1, L1_gnn_W2, L1_gnn_a_src2, L1_gnn_a_dst2, L1_gnn_b2)
    h = jnp.maximum(_layernorm(x, axis=-1), 0.0)
    x = x + _L2_gnn_ref(h, edge_attr_64, edge_index, node_vec1, edge_weight1, L2_gnn_Wq, L2_gnn_bq, L2_gnn_Wk, L2_gnn_bk, L2_gnn_Wv, L2_gnn_bv, L2_gnn_We, L2_gnn_be, L2_gnn_Wc1, L2_gnn_bc1, L2_gnn_Wc2, L2_gnn_bc2, L2_gnn_Wd1, L2_gnn_bd1, L2_gnn_Wd2, L2_gnn_bd2, L2_gnn_Wo, L2_gnn_bo, L2_gnn_gamma, L2_gnn_beta)
    h = jnp.maximum(_layernorm(x, axis=-1), 0.0)
    x = x + _L3_gnn_ref(edge_index, h)
    return x

_drawn_inputs = setup_inputs


def setup_inputs(seed=0):
    import zlib

    import numpy as np

    out = dict(_drawn_inputs(seed))
    spreads = {'L0_gnn_bq': (0.0, 2.0),
     'L0_gnn_bk': (0.0, 2.0),
     'L0_gnn_bv': (0.0, 0.492),
     'L0_gnn_bo': (0.0, 0.1),
     'L1_gnn_b1': (0.0, 0.1),
     'L1_gnn_b2': (0.0, 0.1),
     'L2_gnn_gamma': (1.0, 0.2),
     'L2_gnn_beta': (0.0, 0.347)}
    factors = {'edge_attr_64': 200.0,
     'edge_weight1': 200.0,
     'node_vec1': 200.0,
     'L0_gnn_query_embedding': 8.0,
     'L0_gnn_relation_embeddings': 8.0,
     'L0_gnn_Wq': 8.0,
     'L0_gnn_Wk': 8.0,
     'L1_gnn_a_src1': 2.866,
     'L1_gnn_a_dst1': 102.115,
     'L1_gnn_a_src2': 47.638,
     'L1_gnn_a_dst2': 200.0,
     'L2_gnn_Wq': 200.0,
     'L2_gnn_bq': 200.0,
     'L2_gnn_Wk': 200.0,
     'L2_gnn_bk': 200.0,
     'L2_gnn_bv': 5.342,
     'L2_gnn_We': 200.0,
     'L2_gnn_be': 200.0,
     'L2_gnn_Wc1': 200.0,
     'L2_gnn_bc1': 64.0,
     'L2_gnn_Wc2': 200.0,
     'L2_gnn_bc2': 64.0,
     'L2_gnn_Wd1': 200.0,
     'L2_gnn_bd1': 200.0,
     'L2_gnn_Wd2': 200.0,
     'L2_gnn_bd2': 64.0,
     'L2_gnn_bo': 2.765}
    for name, (base, spread) in spreads.items():
        noise = np.random.default_rng([zlib.crc32(name.encode()), seed]).standard_normal(out[name].shape)
        drawn = base * np.exp(spread * noise) if base else spread * noise
        out[name] = jnp.asarray(drawn.astype(out[name].dtype))
    for name, factor in factors.items():
        out[name] = (out[name] * factor).astype(out[name].dtype)
    return out
```

```python
from contextlib import ExitStack

import concourse.bass as bass
from concourse import mybir

ALU = mybir.AluOpType
ACT = mybir.ActivationFunctionType
AX = mybir.AxisListType
F32 = mybir.dt.float32
BF16 = mybir.dt.bfloat16
I32 = mybir.dt.int32
U32 = mybir.dt.uint32

P = 128
HEADS = 8
HALF = 4
SLOTS = 2 * HALF
RUN = 64
RC = RUN // SLOTS
EP = 125
BIG = 1e30
START = -1e29
EPS = 1e-5
KEYCAP = 4000
KEYSTEP = 4096


class Chain:

    def __init__(self, semaphore):
        self.semaphore, self.count = semaphore, 0

    def one(self):
        self.count += 1
        return 1

    def clear(self):
        count, self.count = self.count, 0
        return count


def heads(ap):
    return ap.rearrange("p (h d) -> p h d", h=HEADS)


def program(nc, a, out):
    N, D = a["x"].shape
    E = a["src"].shape[0]
    NB = -(-N // P)
    NPAD = NB * P
    TAIL = N - (NB - 1) * P
    EC = E // EP
    assert EP * EC == E and D == P
    HD = D // HEADS
    ED = a["edge_attr_64"].shape[1]
    CH, HB = 5, 3
    CB, FB = 11, 3
    assert EC % (CH * HB) == 0 and EC % (CB * FB) == 0
    JMAX = E // SLOTS + NB + 2 * RC
    V = HD + 1
    HV = HEADS * V
    W0 = D + HV
    W1 = HV + HEADS
    REC = 2 * HEADS
    TYPES = a["L0_gnn_relation_embeddings"].shape[0]
    SCALE = 1.0 / HD ** 0.5

    with ExitStack() as ctx:
        def sb(name, shape, dt=F32):
            return ctx.enter_context(nc.sbuf_tensor(name, shape, dt))

        made = {}

        def s(name):
            if name not in made:
                made[name] = ctx.enter_context(nc.semaphore(name))
            return made[name]

        def dram(name, shape, dt=F32):
            return nc.dram_tensor(name, shape, dt, kind="Internal").ap()

        rec_id = dram("rec_id", [E + RUN, 2], I32)
        rec_ft = dram("rec_ft", [E + RUN, REC])
        el_idx = dram("el_idx", [JMAX, P, 12], I32)
        el_msk = dram("el_msk", [JMAX, P, SLOTS])
        el_typ = dram("el_typ", [JMAX, P, SLOTS])
        keyrow = dram("keyrow", [NPAD])
        info_d = dram("info_d", [NPAD, 8])
        table = [dram(f"table{n}", [NPAD, w]) for n, w in enumerate([W0, W1, W1, W1, D, D])]

        ident = sb("ident", [P, P])
        ones = sb("ones", [P, P])
        zerob = sb("zerob", [P, P], BF16)
        zero_i = sb("zero_i", [RUN, REC], I32)
        before = sb("before", [P, P])
        iota_r = sb("iota_r", [P, P])
        iota_p = sb("iota_p", [P, 1])
        neg_p = sb("neg_p", [P, 1])
        run_at = sb("run_at", [P, RC])
        node_id = sb("node_id", [P, NB])
        head_of = sb("head_of", [P, HEADS])

        w_l0 = sb("w_l0", [P, 3 * D])
        b_l0 = sb("b_l0", [P, 3 * D])
        w_bot = sb("w_bot", [P, 2 * D])
        qe = sb("qe", [P, 1])
        rel = sb("rel", [TYPES, D])
        wo0 = sb("wo0", [P, D])
        bo0 = sb("bo0", [P, D])
        w_g = [sb(f"w_g{n}", [P, D + REC]) for n in range(2)]
        a_col = sb("a_col", [P, 4])
        a_blk = sb("a_blk", [P, REC])
        b_g = [sb(f"b_g{n}", [P, D]) for n in range(2)]
        w_l2 = sb("w_l2", [P, 3 * D])
        b_l2 = sb("b_l2", [P, 3 * D])
        wo2 = sb("wo2", [P, D])
        bo2 = sb("bo2", [P, D])
        gam = sb("gam", [P, D])
        bet = sb("bet", [P, D])
        we2 = sb("we2", [P, REC])
        wd2 = sb("wd2", [P, 8 * HEADS])
        wd1 = sb("wd1", [P, HD])
        bd1 = sb("bd1", [P, HD])
        b_ft = sb("b_ft", [P, REC])
        wc1 = sb("wc1", [P, 32])
        bc1 = sb("bc1", [P, 32])
        wc2 = sb("wc2", [32, HEADS])
        bc2 = sb("bc2", [P, HEADS])

        xs = sb("xs", [P, NB, D])
        own0 = sb("own0", [P, NB, D])
        own1 = sb("own1", [P, NB, HV + REC])
        own2 = sb("own2", [P, NB, 3 * D])
        cons = sb("cons", [P, NB, HEADS])
        info = sb("info", [P, NB, 8])
        perm = sb("perm", [P, NB], I32)
        permx = sb("permx", [P, NB], I32)
        dis = sb("dis", [P, NB])
        real = sb("real", [P, NB])
        padneg = sb("padneg", [P, NB])
        bounds = sb("bounds", [1, NB + 1], I32)
        rbounds = sb("rbounds", [1, NB + 1], I32)

        st6 = sb("st6", [P, 6])
        mv = sb("mv", [P, 2])
        var = sb("var", [P, 1])
        lnv = sb("lnv", [P, 1])
        rstd = sb("rstd", [P, 1])
        newt = sb("newt", [P, 1])
        hid = sb("hid", [P, D])
        hid_t = sb("hid_t", [P, D])
        den = sb("den", [P, HEADS])
        tmp = sb("tmp", [P, D])
        tmp2 = sb("tmp2", [P, D])
        col = sb("col", [P, 4])
        stage0 = sb("stage0", [P, W0])
        stage1 = sb("stage1", [P, W1])
        stage2 = sb("stage2", [P, D])
        stage_i = sb("stage_i", [P, 1], I32)

        ss = [sb(f"ss{h}", [P, HALF + 1, HEADS]) for h in range(2)]

        bank = [ctx.enter_context(nc.psum_tensor(f"bank{n}", [P, 512], F32)) for n in range(8)]
        ps_t, ps_p, ps_rel = bank[0], bank[1], bank[2:4]

        with ExitStack() as early:
            def eb(name, shape, dt=F32):
                return early.enter_context(nc.sbuf_tensor(name, shape, dt))

            dst_i = eb("dst_i", [EP, EC], I32)
            rec_i = eb("rec_i", [EP, EC, 2], I32)
            src_i = eb("src_i", [EP, EC], I32)
            typ_i = eb("typ_i", [EP, EC], I32)
            int_t = eb("int_t", [EP, EC], I32)
            dst_f = eb("dst_f", [EP, EC])
            lo = [eb(f"lo{n}", [EP, EC]) for n in range(2)]
            hi = [eb(f"hi{n}", [EP, EC]) for n in range(2)]
            oh_lo = [eb(f"oh_lo{k}", [EP, 2, CH, P], BF16) for k in range(HB)]
            oh_hi = [eb(f"oh_hi{k}", [EP, 2, CH, NB], BF16) for k in range(HB)]
            deg = eb("deg", [P, NB])
            tot = eb("tot", [P, NB])
            cum = eb("cum", [P, NB])
            key = eb("key", [P, NB])
            pad_k = eb("pad_k", [P, NB])
            keyall = eb("keyall", [P, NPAD])
            greater = eb("greater", [P, NPAD], BF16)
            rank = eb("rank", [P, NB])
            rank_i = eb("rank_i", [P, NB], I32)
            inf = eb("inf", [P, NB, 8])
            w_t = eb("w_t", [P, D])
            blk_max = eb("blk_max", [NB, 2])
            blk_i = eb("blk_i", [NB, 2], I32)
            bnd_f = eb("bnd_f", [1, 2, NB + 1])
            before_nb = before[0:NB, 0:NB + 1]

            def bc(v, n=P):
                return v.partition_broadcast(n)

            with nc.Block() as block:
                @block.sync
                def _(sp):
                    sp.dma_start(dst_i[:], a["dst"].rearrange("(p c) -> p c", p=EP)).then_inc(s("dst_loaded"), 16)
                    sp.dma_start(src_i[:], a["src"].rearrange("(p c) -> p c", p=EP)).then_inc(s("src_loaded"), 16)
                    sp.dma_start(typ_i[:], a["edge_type_64"].rearrange("(p c) -> p c", p=EP)).then_inc(s("typ_loaded"), 16)
                    n = 0
                    wk, wq = a["L0_gnn_Wk"], a["L0_gnn_Wq"]
                    loads = [
                        (w_l0[:, 0:D], wk[0:D]), (w_l0[:, D:2 * D], a["L0_gnn_Wv"]), (w_l0[:, 2 * D:], wq[0:D]),
                        (w_bot[:, 0:D], wk[D:2 * D]), (w_bot[:, D:], wq[D:2 * D]),
                        (b_l0[:, 0:D], bc(a["L0_gnn_bk"])), (b_l0[:, D:2 * D], bc(a["L0_gnn_bv"])),
                        (b_l0[:, 2 * D:], bc(a["L0_gnn_bq"])),
                        (qe[:], a["L0_gnn_query_embedding"].rearrange("a (p b) -> p (a b)", b=1)),
                        (rel[:], a["L0_gnn_relation_embeddings"]),
                        (wo0[:], a["L0_gnn_Wo"]), (bo0[:], bc(a["L0_gnn_bo"])),
                        (w_g[0][:, 0:D], a["L1_gnn_W1"]), (w_g[1][:, 0:D], a["L1_gnn_W2"]),
                        (b_g[0][:], bc(a["L1_gnn_b1"])), (b_g[1][:], bc(a["L1_gnn_b2"])),
                        (w_l2[:, 0:D], a["L2_gnn_Wk"]), (w_l2[:, D:2 * D], a["L2_gnn_Wv"]), (w_l2[:, 2 * D:], a["L2_gnn_Wq"]),
                        (b_l2[:, 0:D], bc(a["L2_gnn_bk"])), (b_l2[:, D:2 * D], bc(a["L2_gnn_bv"])),
                        (b_l2[:, 2 * D:], bc(a["L2_gnn_bq"])),
                        (wo2[:], a["L2_gnn_Wo"]), (bo2[:], bc(a["L2_gnn_bo"])),
                        (gam[:], bc(a["L2_gnn_gamma"])), (bet[:], bc(a["L2_gnn_beta"])),
                        (wd1[:], bc(a["L2_gnn_Wd1"].rearrange("a b -> (a b)"))), (bd1[:], bc(a["L2_gnn_bd1"])),
                        (b_ft[:, 0:HEADS], bc(a["L2_gnn_be"])), (b_ft[:, HEADS:], bc(a["L2_gnn_bd2"])),
                        (wc1[:], bc(a["L2_gnn_Wc1"].rearrange("a b -> (a b)"))), (bc1[:], bc(a["L2_gnn_bc1"])),
                        (wc2[:], a["L2_gnn_Wc2"]), (bc2[:], bc(a["L2_gnn_bc2"])),
                    ]
                    loads += [(a_col[:, n:n + 1], a[f"L1_gnn_{w}"].rearrange("h (d o) -> (h d) o", o=1))
                              for n, w in enumerate(["a_src1", "a_dst1", "a_src2", "a_dst2"])]
                    for to, of in loads:
                        sp.dma_start(to, of).then_inc(s("weights"), 16)
                        n += 16
                    sp.wait_ge(s("cleared"), 1)
                    for i in range(2):
                        sp.dma_start(we2[i * ED:(i + 1) * ED, i * HEADS:(i + 1) * HEADS], a["L2_gnn_We"]).then_inc(s("weights"), 16)
                        n += 16
                    for i in range(8):
                        sp.dma_start(wd2[i * HD:(i + 1) * HD, i * HEADS:(i + 1) * HEADS], a["L2_gnn_Wd2"]).then_inc(s("weights"), 16)
                        n += 16
                    nv = a["node_vec1"]
                    with nc.allow_non_contiguous_dma(reason="one word per node"):
                        sp.dma_start(inf[:, 0:NB - 1, 4], nv[0:(NB - 1) * P].rearrange("(b p) o -> p (b o)", p=P)).then_inc(s("weights"), 16)
                        sp.dma_start(inf[0:TAIL, NB - 1:NB, 4], nv[(NB - 1) * P:N]).then_inc(s("weights"), 16)
                    n += 32
                    sp.dma_start(rec_id[E:E + RUN], zero_i[:, 0:2]).then_inc(s("weights"), 16)
                    sp.dma_start(rec_ft[E:E + RUN], zero_i[:].bitcast(F32)).then_inc(s("weights"), 16)
                    n += 32
                    sp.wait_ge(s("rec_ready"), 1)
                    sp.sem_inc(s("rec_ready"), -1)
                    sp.dma_start(rec_id[0:E].rearrange("(p c) w -> p c w", p=EP), rec_i[:]).then_inc(s("weights"), 16)
                    n += 16
                    sp.wait_ge(s("key_ready"), 1)
                    sp.sem_inc(s("key_ready"), -1)
                    with nc.allow_non_contiguous_dma(reason="one word per node"):
                        sp.dma_start(keyrow.rearrange("(b p) -> p b", p=P), key[:]).then_inc(s("key_stored"), 16)
                    sp.wait_ge(s("key_stored"), 16)
                    sp.sem_inc(s("key_stored"), -16)
                    sp.dma_start(keyall[:], bc(keyrow)).then_inc(s("keys"), 16)
                    sp.wait_ge(s("weights"), n)
                    sp.sem_inc(s("weights"), -n)
                    sp.sem_inc(s("weights_in"), 2)
                    sp.wait_ge(s("info_stored"), 16 * NB)
                    sp.dma_start(info[:], info_d.rearrange("(b p) w -> p b w", p=P)).then_inc(s("info_in"), 16)

                @block.gpsimd
                def _(pool):
                    ch = Chain(s("pool_chain"))
                    pool.memset(zerob[:], 0.0).then_inc(ch.semaphore, ch.one())
                    pool.memset(zero_i[:], 0).then_inc(ch.semaphore, ch.one())
                    pool.memset(inf[:], 0.0).then_inc(ch.semaphore, ch.one())
                    pool.memset(we2[:], 0.0).then_inc(ch.semaphore, ch.one())
                    pool.memset(wd2[:], 0.0).then_inc(ch.semaphore, ch.one())
                    pool.memset(ones[:], 1.0).then_inc(ch.semaphore, ch.one())
                    pool.memset(before[:], 1.0).then_inc(ch.semaphore, ch.one())
                    pool.memset(head_of[:], 1.0).then_inc(ch.semaphore, ch.one())
                    pool.memset(stage0[:], 1.0).then_inc(ch.semaphore, ch.one())
                    pool.memset(own1[:], 1.0).then_inc(ch.semaphore, ch.one())
                    pool.iota(iota_r[:], [[1, P]], base=0, channel_multiplier=0, allow_small_or_imprecise_dtypes=True).then_inc(ch.semaphore, ch.one())
                    pool.iota(iota_p[:], [[0, 1]], base=0, channel_multiplier=1, allow_small_or_imprecise_dtypes=True).then_inc(ch.semaphore, ch.one())
                    pool.iota(run_at[:], [[SLOTS, RC]], base=0, channel_multiplier=0, allow_small_or_imprecise_dtypes=True).then_inc(ch.semaphore, ch.one())
                    pool.iota(node_id[:], [[P, NB]], base=0, channel_multiplier=1, allow_small_or_imprecise_dtypes=True).then_inc(ch.semaphore, ch.one())
                    for h in range(2):
                        pool.memset(ss[h][:], 1.0).then_inc(ch.semaphore, ch.one())
                    pool.wait_ge(ch.semaphore, ch.count)
                    pool.sem_inc(s("cleared"), 1)
                    pool.affine_select(out=ident[:], in_=ones[:], pattern=[[-1, P]], compare_op=ALU.is_equal,
                                       fill=0.0, base=0, channel_multiplier=1).then_inc(ch.semaphore, ch.one())
                    pool.affine_select(out=before[:], in_=before[:], pattern=[[1, P]], compare_op=ALU.is_gt,
                                       fill=0.0, base=0, channel_multiplier=-1).then_inc(ch.semaphore, ch.one())
                    pool.affine_select(out=head_of[:], in_=head_of[:], pattern=[[-HD, HEADS]], compare_op=ALU.is_ge,
                                       fill=0.0, base=0, channel_multiplier=1).then_inc(ch.semaphore, ch.one())
                    pool.wait_ge(ch.semaphore, ch.count)
                    pool.affine_select(out=head_of[:], in_=head_of[:], pattern=[[HD, HEADS]], compare_op=ALU.is_ge,
                                       fill=0.0, base=HD - 1, channel_multiplier=-1).then_inc(ch.semaphore, ch.one())
                    pool.wait_ge(ch.semaphore, ch.count)
                    pool.sem_inc(s("consts"), 2)
                    pool.wait_ge(ch.semaphore, ch.count)
                    pool.sem_inc(ch.semaphore, -ch.clear())
                    pool.wait_ge(s("rank_ready"), 1)
                    pool.sem_inc(s("rank_ready"), -1)
                    for b in range(NB):
                        pool.indirect_dma_start(info_d, bass.IndirectOffsetOnAxis(ap=rank_i[:, b:b + 1].bitcast(U32), axis=0),
                                                inf[:, b, :], None).then_inc(s("info_stored"), 16)

                @block.vector
                def _(dve):
                    ch = Chain(s("dve_chain"))
                    dve.wait_ge(s("dst_loaded"), 16)
                    dve.sem_inc(s("dst_loaded"), -16)
                    dve.wait_ge(s("consts"), 1)
                    dve.sem_inc(s("consts"), -1)
                    dve.tensor_copy(dst_f[:], dst_i[:]).then_inc(ch.semaphore, ch.one())
                    dve.tensor_scalar(neg_p[:], iota_p[:], -1.0, None, ALU.mult).then_inc(ch.semaphore, ch.one())
                    for n, nodes in enumerate([dst_i, src_i]):
                        if n:
                            dve.wait_ge(s("src_loaded"), 16)
                            dve.sem_inc(s("src_loaded"), -16)
                        dve.tensor_scalar(int_t[:], nodes[:], P - 1, None, ALU.bitwise_and).then_inc(ch.semaphore, ch.one())
                        dve.wait_ge(ch.semaphore, ch.count)
                        dve.tensor_copy(lo[n][:], int_t[:]).then_inc(ch.semaphore, ch.one())
                        dve.wait_ge(ch.semaphore, ch.count)
                        dve.tensor_scalar(int_t[:], nodes[:], 7, None, ALU.logical_shift_right).then_inc(ch.semaphore, ch.one())
                        dve.wait_ge(ch.semaphore, ch.count)
                        dve.tensor_copy(hi[n][:], int_t[:]).then_inc(ch.semaphore, ch.one())
                        dve.wait_ge(ch.semaphore, ch.count)
                    dve.wait_ge(s("typ_loaded"), 16)
                    dve.sem_inc(s("typ_loaded"), -16)
                    dve.tensor_copy(rec_i[:, :, 0], src_i[:]).then_inc(ch.semaphore, ch.one())
                    dve.tensor_copy(rec_i[:, :, 1], typ_i[:]).then_inc(ch.semaphore, ch.one())
                    dve.wait_ge(ch.semaphore, ch.count)
                    dve.sem_inc(s("rec_ready"), 1)
                    dve.wait_ge(ch.semaphore, ch.count)
                    dve.sem_inc(ch.semaphore, -ch.clear())
                    with dve.Fori(0, EC // (CH * HB)) as i:
                        for k in range(HB):
                            c = i * (CH * HB) + k * CH
                            dve.wait_ge(s(f"onehot_free{k}"), 1)
                            dve.sem_inc(s(f"onehot_free{k}"), -1)
                            for n in range(2):
                                dve.tensor_tensor(oh_lo[k][:, n], iota_r[0:EP].unsqueeze(1).broadcast_to([EP, CH, P]),
                                                  lo[n][:, bass.ds(c, CH)].unsqueeze(2).broadcast_to([EP, CH, P]),
                                                  ALU.is_equal).then_inc(s(f"onehot_ready{k}"), 1)
                                dve.tensor_tensor(oh_hi[k][:, n], iota_r[0:EP, 0:NB].unsqueeze(1).broadcast_to([EP, CH, NB]),
                                                  hi[n][:, bass.ds(c, CH)].unsqueeze(2).broadcast_to([EP, CH, NB]),
                                                  ALU.is_equal).then_inc(s(f"onehot_ready{k}"), 1)
                    dve.wait_ge(s("counted"), 1)
                    dve.sem_inc(s("counted"), -1)
                    for k in range(HB):
                        dve.wait_ge(s(f"onehot_free{k}"), 1)
                        dve.sem_inc(s(f"onehot_free{k}"), -1)
                    dve.tensor_copy(deg[:], bank[4][:, 0:NB]).then_inc(ch.semaphore, ch.one())
                    dve.tensor_copy(inf[:, :, 2], bank[4][:, 0:NB]).then_inc(ch.semaphore, ch.one())
                    dve.tensor_copy(inf[:, :, 3], bank[5][:, 0:NB]).then_inc(ch.semaphore, ch.one())
                    dve.tensor_copy(inf[:, :, 0], node_id[:]).then_inc(ch.semaphore, ch.one())
                    dve.tensor_scalar(pad_k[:], node_id[:], float(N), -float(KEYSTEP), ALU.is_ge, ALU.mult).then_inc(ch.semaphore, ch.one())
                    dve.wait_ge(ch.semaphore, ch.count)
                    dve.sem_inc(s("deg_ready"), 1)
                    dve.tensor_scalar(key[:], deg[:], float(KEYCAP), float(KEYSTEP), ALU.min, ALU.mult).then_inc(ch.semaphore, ch.one())
                    dve.wait_ge(ch.semaphore, ch.count)
                    dve.tensor_tensor(key[:], key[:], pad_k[:], ALU.add).then_inc(ch.semaphore, ch.one())
                    dve.wait_ge(ch.semaphore, ch.count)
                    dve.tensor_tensor(key[:], key[:], node_id[:], ALU.subtract).then_inc(ch.semaphore, ch.one())
                    dve.wait_ge(ch.semaphore, ch.count)
                    dve.tensor_scalar(key[:], key[:], float(NPAD), None, ALU.add).then_inc(ch.semaphore, ch.one())
                    dve.wait_ge(ch.semaphore, ch.count)
                    dve.sem_inc(s("key_ready"), 1)
                    dve.wait_ge(s("sums_ready"), 1)
                    dve.sem_inc(s("sums_ready"), -1)
                    dve.tensor_copy(tot[:], bank[6][:, NB:2 * NB]).then_inc(ch.semaphore, ch.one())
                    dve.wait_ge(ch.semaphore, ch.count)
                    dve.tensor_tensor_scan(cum[:], ones[:, 0:NB], tot[:], 0.0, ALU.mult, ALU.add).then_inc(ch.semaphore, ch.one())
                    dve.wait_ge(ch.semaphore, ch.count)
                    dve.tensor_tensor(cum[:], cum[:], tot[:], ALU.subtract).then_inc(ch.semaphore, ch.one())
                    dve.wait_ge(ch.semaphore, ch.count)
                    dve.tensor_tensor(inf[:, :, 1], cum[:], bank[6][:, 0:NB], ALU.add).then_inc(ch.semaphore, ch.one())
                    dve.wait_ge(ch.semaphore, ch.count)
                    dve.wait_ge(s("keys"), 16)
                    dve.sem_inc(s("keys"), -16)
                    with dve.Fori(0, NB) as b:
                        dve.tensor_scalar(greater[:], keyall[:], key[:, bass.ds(b, 1)], 0.0, ALU.is_gt, ALU.add,
                                          accum_out=rank[:, bass.ds(b, 1)]).then_inc(s("ranked"), 1)
                        dve.wait_ge(s("ranked"), 1)
                        dve.sem_inc(s("ranked"), -1)
                    dve.tensor_copy(rank_i[:], rank[:]).then_inc(ch.semaphore, ch.one())
                    dve.wait_ge(ch.semaphore, ch.count)
                    dve.wait_ge(s("weights_in"), 2)
                    dve.sem_inc(s("rank_ready"), 1)
                    for n in range(2):
                        if n:
                            dve.wait_ge(s("a_used"), 1)
                            dve.sem_inc(s("a_used"), -1)
                        dve.tensor_scalar(a_blk[:, 0:HEADS], head_of[:], a_col[:, 2 * n:2 * n + 1], None, ALU.mult).then_inc(ch.semaphore, ch.one())
                        dve.tensor_scalar(a_blk[:, HEADS:], head_of[:], a_col[:, 2 * n + 1:2 * n + 2], None, ALU.mult).then_inc(ch.semaphore, ch.one())
                        dve.wait_ge(ch.semaphore, ch.count)
                        dve.sem_inc(s("a_ready"), 1)
                        dve.wait_ge(s("wt_psum"), 1)
                        dve.sem_inc(s("wt_psum"), -1)
                        dve.tensor_copy(w_t[:], bank[0][:, 0:D]).then_inc(s("wt_ready"), 1)
                        dve.wait_ge(s("wa_ready"), 1)
                        dve.sem_inc(s("wa_ready"), -1)
                        dve.tensor_copy(w_g[n][:, D:], bank[1][:, 0:REC]).then_inc(ch.semaphore, ch.one())
                        dve.wait_ge(ch.semaphore, ch.count)
                        dve.sem_inc(s("a_used"), 1)
                    dve.wait_ge(s("a_used"), 1)
                    dve.sem_inc(s("a_used"), -1)
                    dve.wait_ge(s("query_ready"), 1)
                    dve.sem_inc(s("query_ready"), -1)
                    dve.tensor_tensor(b_l0[:, 0:D], b_l0[:, 0:D], bank[7][:, 0:D], ALU.add).then_inc(ch.semaphore, ch.one())
                    dve.tensor_tensor(b_l0[:, 2 * D:], b_l0[:, 2 * D:], bank[7][:, D:2 * D], ALU.add).then_inc(ch.semaphore, ch.one())
                    dve.wait_ge(ch.semaphore, ch.count)
                    dve.wait_ge(s("info_in"), 16)
                    dve.sem_inc(s("info_in"), -16)
                    dve.tensor_copy(perm[:], info[:, :, 0]).then_inc(ch.semaphore, ch.one())
                    dve.tensor_scalar(permx[:], info[:, :, 0], float(N - 1), None, ALU.min).then_inc(ch.semaphore, ch.one())
                    dve.tensor_scalar(real[:], info[:, :, 0], float(N), None, ALU.is_lt).then_inc(ch.semaphore, ch.one())
                    dve.wait_ge(ch.semaphore, ch.count)
                    dve.tensor_scalar(padneg[:], real[:], -1.0, BIG, ALU.add, ALU.mult).then_inc(ch.semaphore, ch.one())
                    dve.tensor_scalar(dis[:], info[:, :, 3], 1.0, None, ALU.add).then_inc(ch.semaphore, ch.one())
                    dve.wait_ge(ch.semaphore, ch.count)
                    dve.tensor_copy(deg[:], info[:, :, 2]).then_inc(ch.semaphore, ch.one())
                    dve.wait_ge(ch.semaphore, ch.count)
                    dve.sem_inc(s("degp_ready"), 1)
                    dve.wait_ge(s("degt_ready"), 1)
                    dve.sem_inc(s("degt_ready"), -1)
                    dve.tensor_reduce(blk_max[:, 0:1], bank[0][0:NB, 0:P], AX.X, ALU.max).then_inc(ch.semaphore, ch.one())
                    dve.wait_ge(ch.semaphore, ch.count)
                    dve.tensor_scalar(blk_max[:, 1:2], blk_max[:, 0:1], float(RUN - 1), None, ALU.add).then_inc(ch.semaphore, ch.one())
                    dve.wait_ge(ch.semaphore, ch.count)
                    dve.tensor_scalar(blk_max[:, 0:1], blk_max[:, 0:1], float(SLOTS - 1), None, ALU.add).then_inc(ch.semaphore, ch.one())
                    dve.wait_ge(ch.semaphore, ch.count)
                    dve.tensor_copy(blk_i[:], blk_max[:]).then_inc(ch.semaphore, ch.one())
                    dve.wait_ge(ch.semaphore, ch.count)
                    dve.tensor_scalar(blk_i[:, 0:1], blk_i[:, 0:1], SLOTS.bit_length() - 1, None, ALU.logical_shift_right).then_inc(ch.semaphore, ch.one())
                    dve.tensor_scalar(blk_i[:, 1:2], blk_i[:, 1:2], RUN.bit_length() - 1, None, ALU.logical_shift_right).then_inc(ch.semaphore, ch.one())
                    dve.wait_ge(ch.semaphore, ch.count)
                    dve.tensor_copy(blk_max[:], blk_i[:]).then_inc(ch.semaphore, ch.one())
                    dve.wait_ge(ch.semaphore, ch.count)
                    dve.tensor_scalar(blk_max[:], blk_max[:], 1.0, None, ALU.max).then_inc(ch.semaphore, ch.one())
                    dve.wait_ge(ch.semaphore, ch.count)
                    dve.sem_inc(s("blk_ready"), 1)
                    dve.wait_ge(s("bnd_ready"), 1)
                    dve.sem_inc(s("bnd_ready"), -1)
                    dve.tensor_copy(bounds[:], bank[6][0:1, 0:NB + 1]).then_inc(ch.semaphore, ch.one())
                    dve.tensor_copy(rbounds[:], bank[6][0:1, 32:32 + NB + 1]).then_inc(ch.semaphore, ch.one())
                    dve.wait_ge(ch.semaphore, ch.count)
                    dve.sem_inc(s("dis_arg"), 1)
                    dve.wait_ge(s("dis_exp"), 1)
                    dve.sem_inc(s("dis_exp"), -1)
                    dve.tensor_tensor(cum[:], tot[:], tot[:], ALU.mult).then_inc(ch.semaphore, ch.one())
                    dve.wait_ge(ch.semaphore, ch.count)
                    dve.tensor_tensor(cum[:], cum[:], dis[:], ALU.mult).then_inc(ch.semaphore, ch.one())
                    dve.wait_ge(ch.semaphore, ch.count)
                    dve.tensor_scalar(cum[:], cum[:], -0.5, 1.5, ALU.mult, ALU.add).then_inc(ch.semaphore, ch.one())
                    dve.wait_ge(ch.semaphore, ch.count)
                    dve.tensor_tensor(dis[:], tot[:], cum[:], ALU.mult).then_inc(ch.semaphore, ch.one())
                    dve.wait_ge(ch.semaphore, ch.count)
                    dve.tensor_tensor(dis[:], dis[:], real[:], ALU.mult).then_inc(ch.semaphore, ch.one())
                    dve.wait_ge(ch.semaphore, ch.count)
                    dve.sem_inc(ch.semaphore, -ch.clear())

                @block.scalar
                def _(act):
                    act.wait_ge(s("dis_arg"), 1)
                    act.sem_inc(s("dis_arg"), -1)
                    act.activation(cum[:], dis[:], ACT.Ln).then_inc(s("act_chain"), 1)
                    act.wait_ge(s("act_chain"), 1)
                    act.sem_inc(s("act_chain"), -1)
                    act.activation(tot[:], cum[:], ACT.Exp, scale=-0.5).then_inc(s("dis_exp"), 1)

                @block.tensor
                def _(pe):
                    for k in range(HB):
                        pe.sem_inc(s(f"onehot_free{k}"), 1)
                    pe.wait_ge(s("consts"), 1)
                    pe.sem_inc(s("consts"), -1)
                    for n in range(2):
                        pe.matmul(bank[4 + n][:, 0:NB], zerob[:], zerob[:, 0:NB], start=True, stop=False, skip_group_check=True)
                    with pe.Fori(0, EC // (CH * HB)) as i:
                        for k in range(HB):
                            pe.wait_ge(s(f"onehot_ready{k}"), 4)
                            pe.sem_inc(s(f"onehot_ready{k}"), -4)
                            for c in range(CH):
                                for n in range(2):
                                    last = pe.matmul(bank[4 + n][:, 0:NB], oh_lo[k][:, n, c], oh_hi[k][:, n, c],
                                                     start=False, stop=False, skip_group_check=True)
                            last.then_inc(s(f"onehot_free{k}"), 1)
                    for n in range(2):
                        last = pe.matmul(bank[4 + n][:, 0:NB], zerob[:], zerob[:, 0:NB], start=False, stop=True, skip_group_check=True)
                    last.then_inc(s("counted"), 1)
                    pe.wait_ge(s("deg_ready"), 1)
                    pe.sem_inc(s("deg_ready"), -1)
                    pe.matmul(bank[6][:, 0:NB], before[:], deg[:], start=True, stop=True)
                    pe.matmul(bank[6][:, NB:2 * NB], ones[:], deg[:], start=True, stop=True).then_inc(s("sums_ready"), 1)
                    pe.wait_ge(s("weights_in"), 2)
                    for n in range(2):
                        pe.wait_ge(s("a_ready"), 1)
                        pe.sem_inc(s("a_ready"), -1)
                        pe.transpose(bank[0][:, 0:D], w_g[n][:, 0:D], ident[:]).then_inc(s("wt_psum"), 1)
                        pe.wait_ge(s("wt_ready"), 1)
                        pe.sem_inc(s("wt_ready"), -1)
                        pe.matmul(bank[1][:, 0:REC], w_t[:], a_blk[:], start=True, stop=True).then_inc(s("wa_ready"), 1)
                    pe.matmul(bank[7][:, 0:2 * D], qe[:].broadcast_to([P, P]), w_bot[:], start=True, stop=True).then_inc(s("query_ready"), 1)
                    pe.wait_ge(s("degp_ready"), 1)
                    pe.sem_inc(s("degp_ready"), -1)
                    pe.transpose(bank[0][0:NB, 0:P], deg[:], ident[:]).then_inc(s("degt_ready"), 1)
                    pe.wait_ge(s("blk_ready"), 1)
                    pe.sem_inc(s("blk_ready"), -1)
                    pe.matmul(bank[6][0:1, 0:NB + 1], blk_max[:, 0:1], before_nb, start=True, stop=True)
                    pe.matmul(bank[6][0:1, 32:32 + NB + 1], blk_max[:, 1:2], before_nb, start=True, stop=True).then_inc(s("bnd_ready"), 1)

        with ExitStack() as mid:
            def eb(name, shape, dt=F32):
                return mid.enter_context(nc.sbuf_tensor(name, shape, dt))

            attr = [eb(f"attr{k}", [EP, CB * ED]) for k in range(FB)]
            dist = eb("dist", [EP, EC])
            hdn = eb("hdn", [EP, CB, HD])
            a_t = eb("a_t", [P, 6, EP])
            h_t = eb("h_t", [P, 2, EP])
            fts = [eb(f"fts{k}", [EP, CB, REC]) for k in range(FB)]
            pairs = CB // 2
            groups = [(g, min(8, CB - g)) for g in range(0, CB, 8)]
            rows = a["edge_attr_64"].rearrange("(p c) f -> p (c f)", p=EP)
            frows = rec_ft[0:E].rearrange("(p c) f -> p c f", p=EP)

            def at(bk, i):
                return bk[i // 4][:, (i % 4) * EP:(i % 4 + 1) * EP]

            with nc.Block() as block:
                @block.sync
                def _(sp):
                    sp.dma_start(dist[:], a["edge_weight1"].rearrange("(p c) o -> p (c o)", p=EP)).then_inc(s("dist_in"), 16)
                    with sp.Fori(0, EC // (CB * FB)) as i:
                        for k in range(FB):
                            sp.wait_ge(s(f"attr_free{k}"), 1)
                            sp.sem_inc(s(f"attr_free{k}"), -1)
                            sp.dma_start(attr[k][:], rows[:, bass.ds((i * FB + k) * (CB * ED), CB * ED)]).then_inc(s(f"attr_in{k}"), 16)

                @block.gpsimd
                def _(pool):
                    for k in range(FB):
                        pool.sem_inc(s(f"attr_free{k}"), 1)
                        pool.sem_inc(s(f"fts_free{k}"), 1)
                    with pool.Fori(0, EC // (CB * FB)) as i:
                        for k in range(FB):
                            pool.wait_ge(s(f"fts_ready{k}"), 1)
                            pool.sem_inc(s(f"fts_ready{k}"), -1)
                            pool.dma_start(frows[:, bass.ds((i * FB + k) * CB, CB)], fts[k][:]).then_inc(s("fts_stored"), 16)
                            pool.wait_ge(s("fts_stored"), 16 * (i * FB + k + 1))
                            pool.sem_inc(s(f"fts_free{k}"), 1)

                @block.tensor
                def _(pe):
                    pe.sem_inc(s("ft_psum_free"), 1)
                    with pe.Fori(0, EC // (CB * FB)) as i:
                        for k in range(FB):
                            pe.wait_ge(s(f"attr_in{k}"), 16)
                            pe.sem_inc(s(f"attr_in{k}"), -16)
                            for n in range(pairs):
                                pe.transpose(at(bank[0:2], n), attr[k][:, n * 2 * ED:(n + 1) * 2 * ED], ident[0:EP, 0:EP])
                            pe.transpose(at(bank[0:2], pairs)[0:ED], attr[k][:, pairs * 2 * ED:], ident[0:EP, 0:EP]).then_inc(s("attr_t"), 1)
                            pe.wait_ge(s("hdn_ready"), 1)
                            pe.sem_inc(s("hdn_ready"), -1)
                            for n, (c, m) in enumerate(groups):
                                last = pe.transpose(at(bank[2:3], n)[0:m * HD], hdn[:, c:c + m].rearrange("p c d -> p (c d)"),
                                                    ident[0:EP, 0:EP])
                            last.then_inc(s("hdn_t"), 1)
                            pe.wait_ge(s("t_copied"), 2)
                            pe.sem_inc(s("t_copied"), -2)
                            pe.wait_ge(s("ft_psum_free"), 1)
                            pe.sem_inc(s("ft_psum_free"), -1)
                            o = bank[3][0:EP, 0:CB * REC].rearrange("p (c f) -> p c f", f=REC)
                            for n in range(pairs):
                                pe.matmul(o[:, 2 * n:2 * n + 2, 0:HEADS], a_t[:, n], we2[:].rearrange("p (c h) -> p c h", c=2), start=True, stop=True)
                            pe.matmul(o[:, 2 * pairs:, 0:HEADS], a_t[0:ED, pairs], we2[0:ED, 0:HEADS].unsqueeze(1), start=True, stop=True)
                            for n, (c, m) in enumerate(groups):
                                last = pe.matmul(o[:, c:c + m, HEADS:], h_t[0:m * HD, n],
                                                 wd2[0:m * HD, 0:m * HEADS].rearrange("p (c h) -> p c h", c=m), start=True, stop=True)
                            last.then_inc(s("ft_ready"), 1)

                @block.scalar
                def _(act):
                    with act.Fori(0, EC // (CB * FB)) as i:
                        for k in range(FB):
                            act.wait_ge(s("attr_t"), 1)
                            act.sem_inc(s("attr_t"), -1)
                            act.activation(a_t[:, 0:4].rearrange("p n e -> p (n e)"), bank[0][:, 0:4 * EP], ACT.Copy)
                            act.activation(a_t[:, 4], bank[1][:, 0:EP], ACT.Copy)
                            act.activation(a_t[0:ED, 5], bank[1][0:ED, EP:2 * EP], ACT.Copy).then_inc(s("t_copied"), 1)
                            act.wait_ge(s("hdn_t"), 1)
                            act.sem_inc(s("hdn_t"), -1)
                            act.activation(h_t[:, 0], bank[2][:, 0:EP], ACT.Copy)
                            act.activation(h_t[0:groups[1][1] * HD, 1], bank[2][0:groups[1][1] * HD, EP:2 * EP], ACT.Copy).then_inc(s("t_copied"), 1)

                @block.vector
                def _(dve):
                    ch = Chain(s("dve_chain"))
                    dve.wait_ge(s("dist_in"), 16)
                    dve.sem_inc(s("dist_in"), -16)
                    with dve.Fori(0, EC // (CB * FB)) as i:
                        for k in range(FB):
                            c = (i * FB + k) * CB
                            dve.tensor_tensor(hdn[:], dist[:, bass.ds(c, CB)].unsqueeze(2).broadcast_to([EP, CB, HD]),
                                              wd1[0:EP].unsqueeze(1).broadcast_to([EP, CB, HD]), ALU.mult).then_inc(ch.semaphore, ch.one())
                            dve.wait_ge(ch.semaphore, ch.count)
                            dve.tensor_tensor(hdn[:], hdn[:], bd1[0:EP].unsqueeze(1).broadcast_to([EP, CB, HD]), ALU.add).then_inc(ch.semaphore, ch.one())
                            dve.wait_ge(ch.semaphore, ch.count)
                            dve.tensor_scalar(hdn[:], hdn[:], 0.0, None, ALU.max).then_inc(s("hdn_ready"), 1)
                            dve.wait_ge(s("ft_ready"), 1)
                            dve.sem_inc(s("ft_ready"), -1)
                            dve.sem_inc(s(f"attr_free{k}"), 1)
                            dve.wait_ge(s(f"fts_free{k}"), 1)
                            dve.sem_inc(s(f"fts_free{k}"), -1)
                            dve.tensor_tensor(fts[k][:], bank[3][0:EP, 0:CB * REC].rearrange("p (c f) -> p c f", f=REC),
                                              b_ft[0:EP].unsqueeze(1).broadcast_to([EP, CB, REC]), ALU.add).then_inc(ch.semaphore, ch.one())
                            dve.wait_ge(ch.semaphore, ch.count)
                            dve.sem_inc(s(f"fts_ready{k}"), 1)
                            dve.sem_inc(s("ft_psum_free"), 1)
                        dve.wait_ge(ch.semaphore, ch.count)
                        dve.sem_inc(ch.semaphore, -ch.clear())

        def block_range(engine, b, table=bounds, most=JMAX):
            return (engine.value_load(table[0:1, bass.ds(b, 1)], min_val=0, max_val=most),
                    engine.value_load(table[0:1, bass.ds(b + 1, 1)], min_val=1, max_val=most))

        with ExitStack() as mid:
            def eb(name, shape, dt=F32):
                return mid.enter_context(nc.sbuf_tensor(name, shape, dt))

            left = eb("left", [P, 1])
            at_f = eb("at_f", [P, 1])
            at_c = eb("at_c", [P, 1])
            at_i = eb("at_i", [P, 1], I32)
            rec = eb("rec", [P, RUN, 2], I32)
            src_f = eb("src_f", [P, RUN])
            has = eb("has", [P, RUN])
            iota64 = iota_r[:, 0:RUN]
            el_i = eb("el_i", [P, RC, 12], I32)
            el_m = eb("el_m", [P, RC, SLOTS])
            el_t = eb("el_t", [P, RC, SLOTS])

            with nc.Block() as block:
                @block.gpsimd
                def _(pool):
                    with pool.Fori(0, NB) as b:
                        start, end = block_range(pool, b, rbounds)
                        with pool.Fori(start, end) as r:
                            pool.wait_ge(s("run_ready"), 1)
                            pool.sem_inc(s("run_ready"), -1)
                            pool.indirect_dma_start(rec[:].rearrange("p s w -> p (s w)"), None, rec_id,
                                                    bass.IndirectOffsetOnAxis(ap=at_i[:].bitcast(U32), axis=0)).then_inc(s("run_in"), 16)
                    for b in range(NB):
                        pool.indirect_dma_start(xs[:, b, :], None, a["x"],
                                                bass.IndirectOffsetOnAxis(ap=permx[:, b:b + 1].bitcast(U32), axis=0)).then_inc(s("x_in"), 16)
                    pool.wait_ge(s("x_in"), 16 * NB)

                @block.vector
                def _(dve):
                    ch = Chain(s("dve_chain"))
                    dve.memset(el_i[:], 0).then_inc(s("dve_chain"), 1)
                    dve.wait_ge(s("dve_chain"), 1)
                    dve.sem_inc(s("dve_chain"), -1)
                    with dve.Fori(0, NB) as b:
                        start, end = block_range(dve, b, rbounds)
                        dve.tensor_copy(left[:], info[:, bass.ds(b, 1), 2]).then_inc(ch.semaphore, ch.one())
                        dve.tensor_copy(at_f[:], info[:, bass.ds(b, 1), 1]).then_inc(ch.semaphore, ch.one())
                        dve.wait_ge(ch.semaphore, ch.count)
                        dve.sem_inc(ch.semaphore, -ch.clear())
                        with dve.Fori(start, end) as r:
                            dve.tensor_scalar(at_c[:], at_f[:], float(E), None, ALU.min).then_inc(ch.semaphore, ch.one())
                            dve.wait_ge(ch.semaphore, ch.count)
                            dve.tensor_copy(at_i[:], at_c[:]).then_inc(ch.semaphore, ch.one())
                            dve.tensor_scalar(has[:], iota64, left[:], None, ALU.is_lt).then_inc(ch.semaphore, ch.one())
                            dve.wait_ge(ch.semaphore, ch.count)
                            dve.sem_inc(s("run_ready"), 1)
                            dve.wait_ge(s("el_free"), 1)
                            dve.sem_inc(s("el_free"), -1)
                            dve.tensor_scalar(el_i[:, :, SLOTS], run_at[:], at_c[:], float(E), ALU.add, ALU.min).then_inc(ch.semaphore, ch.one())
                            dve.tensor_scalar(el_m[:].rearrange("p c s -> p (c s)"), has[:], -1.0, BIG, ALU.add, ALU.mult).then_inc(ch.semaphore, ch.one())
                            dve.wait_ge(s("run_in"), 16 * r + 16)
                            dve.tensor_copy(el_t[:].rearrange("p c s -> p (c s)"), rec[:, :, 1]).then_inc(ch.semaphore, ch.one())
                            dve.tensor_copy(src_f[:], rec[:, :, 0]).then_inc(ch.semaphore, ch.one())
                            dve.wait_ge(ch.semaphore, ch.count)
                            dve.scalar_tensor_tensor(src_f[:], src_f[:], -float(NPAD - 1), has[:], ALU.add, ALU.mult).then_inc(ch.semaphore, ch.one())
                            dve.wait_ge(ch.semaphore, ch.count)
                            dve.tensor_scalar(el_i[:, :, 0:SLOTS], src_f[:].rearrange("p (c s) -> p c s", s=SLOTS),
                                              float(NPAD - 1), None, ALU.add).then_inc(ch.semaphore, ch.one())
                            dve.tensor_scalar(left[:], left[:], -float(RUN), None, ALU.add).then_inc(ch.semaphore, ch.one())
                            dve.tensor_scalar(at_f[:], at_f[:], float(RUN), None, ALU.add).then_inc(ch.semaphore, ch.one())
                            dve.wait_ge(ch.semaphore, ch.count)
                            dve.sem_inc(s("el_ready"), 1)
                            dve.wait_ge(ch.semaphore, ch.count)
                            dve.sem_inc(ch.semaphore, -ch.clear())
                    dve.wait_ge(s("el_free"), 1)
                    dve.sem_inc(s("el_free"), -1)

                @block.sync
                def _(sp):
                    sp.sem_inc(s("el_free"), 1)
                    with sp.Fori(0, NB) as b:
                        start, end = block_range(sp, b, bounds, JMAX - RC)
                        with sp.Fori(start, end, RC) as j:
                            sp.wait_ge(s("el_ready"), 1)
                            sp.sem_inc(s("el_ready"), -1)
                            sp.dma_start(el_idx[bass.ds(j, RC)].rearrange("j p s -> p j s"), el_i[:]).then_inc(s("el_stored"), 16)
                            sp.dma_start(el_msk[bass.ds(j, RC)].rearrange("j p s -> p j s"), el_m[:]).then_inc(s("el_stored"), 16)
                            sp.dma_start(el_typ[bass.ds(j, RC)].rearrange("j p s -> p j s"), el_t[:]).then_inc(s("el_stored"), 16)
                            sp.wait_ge(s("el_stored"), 48)
                            sp.sem_inc(s("el_stored"), -48)
                            sp.sem_inc(s("el_free"), 1)

        idx = [sb(f"idx{h}", [P, HALF], I32) for h in range(2)]
        first = sb("first", [P, 2], I32)
        msk = sb("msk", [P, SLOTS])
        typ = sb("typ", [TYPES, P * SLOTS])
        typ_d = sb("typ_d", [TYPES, P * SLOTS])
        onehot = sb("onehot", [TYPES, P, SLOTS])
        feat = sb("feat", [P, SLOTS, REC])
        sc = [sb(f"sc{h}", [P, HALF + 1, HEADS]) for h in range(2)]
        sh = sb("sh", [P, HALF + 1, HEADS])
        wt = sb("wt", [P, HALF + 1, HEADS])
        sw = sb("sw", [P, HALF + 1, HEADS])
        kk = sb("kk", [P, HALF, D])
        prod = sb("prod", [P, HALF + 1, HV])
        g0 = [sb(f"g0{h}", [P, HALF + 1, W0]) for h in range(2)]
        g1 = [sb(f"g1{h}", [P, HALF + 1, W1]) for h in range(2)]
        g2 = [sb(f"g2{h}", [P, HALF + 1, D]) for h in range(2)]

        def dve_layernorm(dve, ch, x, to, relu=True):
            dve.bn_stats(st6[:], x).then_inc(ch.semaphore, ch.one())
            dve.wait_ge(ch.semaphore, ch.count)
            dve.bn_aggr(mv[:], st6[:]).then_inc(ch.semaphore, ch.one())
            dve.wait_ge(ch.semaphore, ch.count)
            dve.tensor_scalar(var[:], mv[:, 1:2], EPS, None, ALU.add).then_inc(ch.semaphore, ch.one())
            dve.wait_ge(ch.semaphore, ch.count)
            dve.sem_inc(s("var_ready"), 1)
            dve.wait_ge(s("rstd_ready"), 1)
            dve.sem_inc(s("rstd_ready"), -1)
            dve.tensor_tensor(newt[:], rstd[:], rstd[:], ALU.mult).then_inc(ch.semaphore, ch.one())
            dve.wait_ge(ch.semaphore, ch.count)
            dve.tensor_tensor(newt[:], newt[:], var[:], ALU.mult).then_inc(ch.semaphore, ch.one())
            dve.wait_ge(ch.semaphore, ch.count)
            dve.tensor_scalar(newt[:], newt[:], -0.5, 1.5, ALU.mult, ALU.add).then_inc(ch.semaphore, ch.one())
            dve.wait_ge(ch.semaphore, ch.count)
            dve.tensor_tensor(newt[:], newt[:], rstd[:], ALU.mult).then_inc(ch.semaphore, ch.one())
            dve.wait_ge(ch.semaphore, ch.count)
            dve.tensor_scalar(to, x, mv[:, 0:1], newt[:], ALU.subtract, ALU.mult).then_inc(ch.semaphore, ch.one())
            dve.wait_ge(ch.semaphore, ch.count)
            if relu:
                dve.tensor_scalar(to, to, 0.0, None, ALU.max).then_inc(ch.semaphore, ch.one())
                dve.wait_ge(ch.semaphore, ch.count)

        def act_layernorm(act):
            act.wait_ge(s("var_ready"), 1)
            act.sem_inc(s("var_ready"), -1)
            act.activation(lnv[:], var[:], ACT.Ln).then_inc(s("act_chain"), 1)
            act.wait_ge(s("act_chain"), 1)
            act.sem_inc(s("act_chain"), -1)
            act.activation(rstd[:], lnv[:], ACT.Exp, scale=-0.5).then_inc(s("rstd_ready"), 1)

        def pe_project(pe, w, n):
            pe.wait_ge(s("hid_ready"), 1)
            pe.sem_inc(s("hid_ready"), -1)
            pe.transpose(ps_t[:, 0:P], hid[:], ident[:]).then_inc(s("hid_turned"), 1)
            pe.wait_ge(s("hid_t_ready"), 1)
            pe.sem_inc(s("hid_t_ready"), -1)
            pe.matmul(ps_p[:, 0:n], hid_t[:], w, start=True, stop=True).then_inc(s("projected"), 1)

        def act_project(act):
            act.wait_ge(s("hid_turned"), 1)
            act.sem_inc(s("hid_turned"), -1)
            act.activation(hid_t[:], ps_t[:, 0:P], ACT.Copy).then_inc(s("hid_t_ready"), 1)

        def dve_project(dve, ch):
            dve.wait_ge(ch.semaphore, ch.count)
            dve.sem_inc(s("hid_ready"), 1)
            dve.wait_ge(s("projected"), 1)
            dve.sem_inc(s("projected"), -1)

        def dve_table(dve, ch, b, number):
            dve.tensor_copy(stage_i[:], perm[:, bass.ds(b, 1)]).then_inc(ch.semaphore, ch.one())
            dve.wait_ge(ch.semaphore, ch.count)
            dve.sem_inc(s("table_ready"), 1)

        def blk(t, b, c0, c1):
            return t[:, bass.ds(b, 1), c0:c1].rearrange("p o c -> p (o c)")

        def wait_table_stored(dve, stores_before, b):
            dve.wait_ge(s("table_stored"), 16 * (stores_before + b))

        scattered = [0]

        def dve_to_l0(dve, ch, b, wait):
            dve_layernorm(dve, ch, blk(xs, b, 0, D), hid[:])
            dve_project(dve, ch)
            wait()
            dve.tensor_tensor(stage0[:, 0:D], ps_p[:, 0:D], b_l0[:, 0:D], ALU.add).then_inc(ch.semaphore, ch.one())
            dve.tensor_tensor(stage0[:, D:].rearrange("p (h v) -> p h v", h=HEADS)[:, :, 0:HD],
                              heads(ps_p[:, D:2 * D]), heads(b_l0[:, D:2 * D]), ALU.add).then_inc(ch.semaphore, ch.one())
            dve.tensor_tensor(blk(own0, b, 0, D), ps_p[:, 2 * D:3 * D], b_l0[:, 2 * D:], ALU.add).then_inc(ch.semaphore, ch.one())
            dve.wait_ge(ch.semaphore, ch.count)
            dve.tensor_scalar(blk(own0, b, 0, D), blk(own0, b, 0, D), SCALE, None, ALU.mult).then_inc(ch.semaphore, ch.one())
            dve_table(dve, ch, b, 0)
            dve.memset(hid[:], 0.0).then_inc(ch.semaphore, ch.one())
            dve.tensor_scalar(tmp[:, 0:32], wc1[:], info[:, bass.ds(b, 1), 4], None, ALU.mult).then_inc(ch.semaphore, ch.one())
            dve.wait_ge(ch.semaphore, ch.count)
            dve.tensor_tensor(tmp[:, 0:32], tmp[:, 0:32], bc1[:], ALU.add).then_inc(ch.semaphore, ch.one())
            dve.wait_ge(ch.semaphore, ch.count)
            dve.tensor_scalar(hid[:, 0:32], tmp[:, 0:32], 0.0, None, ALU.max).then_inc(ch.semaphore, ch.one())
            dve.wait_ge(ch.semaphore, ch.count)
            dve_project(dve, ch)
            dve.tensor_tensor(tmp[:, 0:HEADS], ps_p[:, 0:HEADS], bc2[:], ALU.add).then_inc(ch.semaphore, ch.one())
            dve.wait_ge(ch.semaphore, ch.count)
            dve.tensor_scalar(tmp[:, HEADS:2 * HEADS], tmp[:, 0:HEADS], 0.0, None, ALU.is_ge).then_inc(ch.semaphore, ch.one())
            dve.scalar_tensor_tensor(den[:], tmp[:, 0:HEADS], -1.0, tmp[:, 0:HEADS], ALU.mult, ALU.max).then_inc(ch.semaphore, ch.one())
            dve.wait_ge(ch.semaphore, ch.count)
            dve.sem_inc(s("cons_arg"), 1)
            dve.wait_ge(s("cons_exp"), 1)
            dve.sem_inc(s("cons_exp"), -1)
            dve.tensor_tensor(tmp[:, HEADS:2 * HEADS], tmp[:, HEADS:2 * HEADS], tmp2[:, 0:HEADS], ALU.max).then_inc(ch.semaphore, ch.one())
            dve.tensor_scalar(den[:], tmp2[:, 0:HEADS], 1.0, None, ALU.add).then_inc(ch.semaphore, ch.one())
            dve.wait_ge(ch.semaphore, ch.count)
            dve.reciprocal(den[:], den[:]).then_inc(ch.semaphore, ch.one())
            dve.wait_ge(ch.semaphore, ch.count)
            dve.tensor_tensor(cons[:, bass.ds(b, 1), :].rearrange("p o c -> p (o c)"), den[:], tmp[:, HEADS:2 * HEADS], ALU.mult).then_inc(ch.semaphore, ch.one())
            dve.wait_ge(ch.semaphore, ch.count)

        def act_to_l0(act):
            act_layernorm(act)
            act_project(act)
            act_project(act)
            act.wait_ge(s("cons_arg"), 1)
            act.sem_inc(s("cons_arg"), -1)
            act.activation(tmp2[:, 0:HEADS], den[:], ACT.Exp, scale=-1.0).then_inc(s("cons_exp"), 1)

        def pe_to_l0(pe):
            pe_project(pe, w_l0[:], 3 * D)
            pe.wait_ge(s("hid_ready"), 1)
            pe.sem_inc(s("hid_ready"), -1)
            pe.transpose(ps_t[:, 0:P], hid[:], ident[:]).then_inc(s("hid_turned"), 1)
            pe.wait_ge(s("hid_t_ready"), 1)
            pe.sem_inc(s("hid_t_ready"), -1)
            pe.matmul(ps_p[:, 0:HEADS], hid_t[0:32], wc2[:], start=True, stop=True).then_inc(s("projected"), 1)

        def dve_to_conv(dve, ch, b, wait, number):
            dve_project(dve, ch)
            dve.tensor_copy(blk(own1, b, 0, HV).rearrange("p (h v) -> p h v", h=HEADS)[:, :, 0:HD], heads(ps_p[:, 0:D])).then_inc(ch.semaphore, ch.one())
            dve.tensor_copy(blk(own1, b, HV, HV + REC), ps_p[:, D:D + REC]).then_inc(ch.semaphore, ch.one())
            dve.wait_ge(ch.semaphore, ch.count)
            wait()
            dve.tensor_scalar(stage1[:, HV:W1], blk(own1, b, HV, W1), padneg[:, bass.ds(b, 1)], None, ALU.add).then_inc(ch.semaphore, ch.one())
            dve.tensor_copy(stage1[:, 0:HV], blk(own1, b, 0, HV)).then_inc(ch.semaphore, ch.one())
            dve_table(dve, ch, b, number)

        def dve_softmax_mean(dve, ch, state, eps):
            by_head = state.rearrange("p (h v) -> p h v", h=HEADS)
            dve.tensor_scalar(den[:], by_head[:, :, HD], eps, None, ALU.add).then_inc(ch.semaphore, ch.one())
            dve.wait_ge(ch.semaphore, ch.count)
            dve.reciprocal(den[:], den[:]).then_inc(ch.semaphore, ch.one())
            dve.wait_ge(ch.semaphore, ch.count)
            dve.tensor_tensor(heads(tmp[:]), by_head[:, :, 0:HD], den[:].unsqueeze(2).broadcast_to([P, HEADS, HD]), ALU.mult).then_inc(ch.semaphore, ch.one())
            dve.wait_ge(ch.semaphore, ch.count)

        def after_l0(dve, ch, b, wait):
            dve_softmax_mean(dve, ch, g0[0][:, HALF, D:W0], 1e-8)
            dve.tensor_copy(hid[:], tmp[:]).then_inc(ch.semaphore, ch.one())
            dve.wait_ge(ch.semaphore, ch.count)
            dve_project(dve, ch)
            dve.tensor_tensor(tmp[:], ps_p[:, 0:D], bo0[:], ALU.add).then_inc(ch.semaphore, ch.one())
            dve.wait_ge(ch.semaphore, ch.count)
            dve.tensor_tensor(blk(xs, b, 0, D), blk(xs, b, 0, D), tmp[:], ALU.add).then_inc(ch.semaphore, ch.one())
            dve.wait_ge(ch.semaphore, ch.count)
            dve_layernorm(dve, ch, blk(xs, b, 0, D), hid[:])
            dve_to_conv(dve, ch, b, wait, 1)

        def after_conv(n):
            def run(dve, ch, b, wait):
                dve_softmax_mean(dve, ch, g1[0][:, HALF, 0:HV], 1e-16)
                if n < 2:
                    dve.tensor_tensor(hid[:], tmp[:], b_g[min(n, 1)][:], ALU.add).then_inc(ch.semaphore, ch.one())
                    dve.wait_ge(ch.semaphore, ch.count)
                    dve_to_conv(dve, ch, b, wait, n + 2)
                    return
                dve.tensor_tensor(tmp[:], tmp[:], b_g[1][:], ALU.add).then_inc(ch.semaphore, ch.one())
                dve.wait_ge(ch.semaphore, ch.count)
                dve.tensor_reduce(col[:, 0:1], tmp[:], AX.X, ALU.max).then_inc(ch.semaphore, ch.one())
                dve.wait_ge(ch.semaphore, ch.count)
                dve.tensor_scalar(tmp[:], tmp[:], col[:, 0:1], None, ALU.subtract).then_inc(ch.semaphore, ch.one())
                dve.wait_ge(ch.semaphore, ch.count)
                dve.sem_inc(s("logits_ready"), 1)
                dve.wait_ge(s("log_sum"), 1)
                dve.sem_inc(s("log_sum"), -1)
                dve.tensor_scalar(tmp[:], tmp[:], col[:, 2:3], None, ALU.subtract).then_inc(ch.semaphore, ch.one())
                dve.wait_ge(ch.semaphore, ch.count)
                dve.tensor_tensor(blk(xs, b, 0, D), blk(xs, b, 0, D), tmp[:], ALU.add).then_inc(ch.semaphore, ch.one())
                dve.wait_ge(ch.semaphore, ch.count)
                dve_layernorm(dve, ch, blk(xs, b, 0, D), hid[:])
                dve.tensor_copy(blk(own2, b, 2 * D, 3 * D), hid[:]).then_inc(ch.semaphore, ch.one())
                dve.wait_ge(ch.semaphore, ch.count)
                dve_project(dve, ch)
                wait()
                dve.tensor_tensor(blk(own2, b, 0, 2 * D), ps_p[:, 0:2 * D], b_l2[:, 0:2 * D], ALU.add).then_inc(ch.semaphore, ch.one())
                dve.tensor_tensor(stage2[:], ps_p[:, 2 * D:3 * D], b_l2[:, 2 * D:], ALU.add).then_inc(ch.semaphore, ch.one())
                dve.wait_ge(ch.semaphore, ch.count)
                dve.tensor_scalar(blk(own2, b, 0, D), blk(own2, b, 0, D), SCALE, None, ALU.mult).then_inc(ch.semaphore, ch.one())
                dve_table(dve, ch, b, 4)
            return run

        def act_after_conv3(act):
            act.wait_ge(s("logits_ready"), 1)
            act.sem_inc(s("logits_ready"), -1)
            act.activation(tmp2[:], tmp[:], ACT.Exp, accum_out=col[:, 1:2]).then_inc(s("act_chain"), 1)
            act.wait_ge(s("act_chain"), 1)
            act.sem_inc(s("act_chain"), -1)
            act.activation(col[:, 2:3], col[:, 1:2], ACT.Ln).then_inc(s("log_sum"), 1)
            act_layernorm(act)
            act_project(act)

        def after_l2(dve, ch, b, wait):
            dve.tensor_scalar(den[:], ss[0][:, HALF, :], 1e-30, None, ALU.max).then_inc(ch.semaphore, ch.one())
            dve.wait_ge(ch.semaphore, ch.count)
            dve.reciprocal(den[:], den[:]).then_inc(ch.semaphore, ch.one())
            dve.wait_ge(ch.semaphore, ch.count)
            dve.tensor_tensor(den[:], den[:], ss[0][:, HALF, :], ALU.mult).then_inc(ch.semaphore, ch.one())
            dve.wait_ge(ch.semaphore, ch.count)
            dve.tensor_tensor(heads(hid[:]), heads(blk(own2, b, D, 2 * D)), den[:].unsqueeze(2).broadcast_to([P, HEADS, HD]), ALU.mult).then_inc(ch.semaphore, ch.one())
            dve.wait_ge(ch.semaphore, ch.count)
            dve_project(dve, ch)
            dve.tensor_tensor(tmp[:], ps_p[:, 0:D], bo2[:], ALU.add).then_inc(ch.semaphore, ch.one())
            dve.wait_ge(ch.semaphore, ch.count)
            dve.tensor_tensor(tmp[:], tmp[:], blk(own2, b, 2 * D, 3 * D), ALU.add).then_inc(ch.semaphore, ch.one())
            dve.wait_ge(ch.semaphore, ch.count)
            dve_layernorm(dve, ch, tmp[:], hid[:], relu=False)
            dve.tensor_tensor(tmp[:], hid[:], gam[:], ALU.mult).then_inc(ch.semaphore, ch.one())
            dve.wait_ge(ch.semaphore, ch.count)
            dve.tensor_tensor(tmp[:], tmp[:], bet[:], ALU.add).then_inc(ch.semaphore, ch.one())
            dve.wait_ge(ch.semaphore, ch.count)
            dve.tensor_tensor(blk(xs, b, 0, D), blk(xs, b, 0, D), tmp[:], ALU.add).then_inc(ch.semaphore, ch.one())
            dve.wait_ge(ch.semaphore, ch.count)
            dve_layernorm(dve, ch, blk(xs, b, 0, D), hid[:])
            wait()
            dve.tensor_scalar(stage2[:], hid[:], dis[:, bass.ds(b, 1)], None, ALU.mult).then_inc(ch.semaphore, ch.one())
            dve.wait_ge(ch.semaphore, ch.count)
            dve.tensor_copy(blk(own0, b, 0, D), stage2[:]).then_inc(ch.semaphore, ch.one())
            dve_table(dve, ch, b, 5)

        def after_l3(dve, ch, b, wait):
            dve.tensor_scalar(tmp[:], g2[0][:, HALF, :], dis[:, bass.ds(b, 1)], None, ALU.mult).then_inc(ch.semaphore, ch.one())
            dve.wait_ge(ch.semaphore, ch.count)
            wait()
            dve.tensor_tensor(stage2[:], blk(xs, b, 0, D), tmp[:], ALU.add).then_inc(ch.semaphore, ch.one())
            dve_table(dve, ch, b, 6)

        def slots(ap, shape):
            return ap.unsqueeze(1).broadcast_to(shape)

        H1 = HALF + 1

        def dve_maximum(dve, ch, h):
            new = sc[1 - h][:, HALF, :]
            dve.tensor_reduce(new, sc[h][:].rearrange("p s h -> p h s"), AX.X, ALU.max).then_inc(ch.semaphore, ch.one())
            dve.wait_ge(ch.semaphore, ch.count)
            dve.tensor_tensor(sh[:], sc[h][:], slots(new, [P, H1, HEADS]), ALU.subtract).then_inc(ch.semaphore, ch.one())
            dve.wait_ge(ch.semaphore, ch.count)
            dve.sem_inc(s("shifted"), 1)
            dve.wait_ge(s("exped"), 1)
            dve.sem_inc(s("exped"), -1)

        def dve_weigh(dve, ch, h, g, c0):
            dve.tensor_tensor(prod[:].rearrange("p s (h v) -> p s h v", h=HEADS),
                              g[h][:, :, c0:c0 + HV].rearrange("p s (h v) -> p s h v", h=HEADS),
                              wt[:].unsqueeze(3).broadcast_to([P, H1, HEADS, V]), ALU.mult).then_inc(ch.semaphore, ch.one())
            dve.wait_ge(ch.semaphore, ch.count)
            dve.sem_inc(s(f"rows_free{h}"), 1)
            dve.tensor_reduce(g[1 - h][:, HALF, c0:c0 + HV], prod[:].rearrange("p s c -> p c s"), AX.X, ALU.add).then_inc(ch.semaphore, ch.one())
            dve.wait_ge(ch.semaphore, ch.count)

        def half_l0(dve, ch, b, h, j):
            dve.wait_ge(s(f"rel_ready{h}"), 1)
            dve.sem_inc(s(f"rel_ready{h}"), -1)
            if h == 1:
                dve.sem_inc(s("onehot_free"), 1)
            dve.tensor_tensor(kk[:], g0[h][:, 0:HALF, 0:D], ps_rel[h][:].rearrange("p (s d) -> p s d", d=D), ALU.add).then_inc(ch.semaphore, ch.one())
            dve.wait_ge(ch.semaphore, ch.count)
            dve.sem_inc(s(f"rel_free{h}"), 1)
            dve.tensor_tensor(kk[:], kk[:], slots(blk(own0, b, 0, D), [P, HALF, D]), ALU.mult).then_inc(ch.semaphore, ch.one())
            dve.wait_ge(ch.semaphore, ch.count)
            dve.tensor_reduce(sc[h][:, 0:HALF, :], kk[:].rearrange("p s (h d) -> p s h d", h=HEADS), AX.X, ALU.add).then_inc(ch.semaphore, ch.one())
            dve.wait_ge(ch.semaphore, ch.count)
            if h == 0:
                dve.wait_ge(s("msk_in"), 16)
                dve.sem_inc(s("msk_in"), -16)
            dve.tensor_tensor(sc[h][:, 0:HALF, :], sc[h][:, 0:HALF, :],
                              msk[:, h * HALF:(h + 1) * HALF].unsqueeze(2).broadcast_to([P, HALF, HEADS]), ALU.add).then_inc(ch.semaphore, ch.one())
            dve.wait_ge(ch.semaphore, ch.count)
            if h == 1:
                dve.sem_inc(s("msk_free"), 1)
            dve_maximum(dve, ch, h)
            dve_weigh(dve, ch, h, g0, D)

        def half_conv(dve, ch, b, h, j):
            dve.tensor_tensor(sc[h][:, 0:HALF, :], g1[h][:, 0:HALF, HV:W1],
                              slots(blk(own1, b, W1, W1 + HEADS), [P, HALF, HEADS]), ALU.add).then_inc(ch.semaphore, ch.one())
            dve.wait_ge(ch.semaphore, ch.count)
            dve.scalar_tensor_tensor(sc[h][:, 0:HALF, :], sc[h][:, 0:HALF, :], 0.2, sc[h][:, 0:HALF, :], ALU.mult, ALU.max).then_inc(ch.semaphore, ch.one())
            dve.wait_ge(ch.semaphore, ch.count)
            dve_maximum(dve, ch, h)
            dve_weigh(dve, ch, h, g1, 0)

        def half_l2(dve, ch, b, h, j):
            part = feat[:, h * HALF:(h + 1) * HALF]
            dve.tensor_tensor(kk[:], g2[h][:, 0:HALF, :], slots(blk(own2, b, 0, D), [P, HALF, D]), ALU.mult).then_inc(ch.semaphore, ch.one())
            dve.wait_ge(ch.semaphore, ch.count)
            dve.sem_inc(s(f"rows_free{h}"), 1)
            dve.tensor_reduce(sc[h][:, 0:HALF, :], kk[:].rearrange("p s (h d) -> p s h d", h=HEADS), AX.X, ALU.add).then_inc(ch.semaphore, ch.one())
            dve.wait_ge(ch.semaphore, ch.count)
            if h == 0:
                dve.wait_ge(s("feat_in"), 16 * j + 16)
                dve.wait_ge(s("msk_in"), 16)
                dve.sem_inc(s("msk_in"), -16)
            now = sc[h][:, 0:HALF, :]
            dve.tensor_tensor(now, now, part[:, :, 0:HEADS], ALU.add).then_inc(ch.semaphore, ch.one())
            dve.wait_ge(ch.semaphore, ch.count)
            dve.tensor_tensor(now, now, slots(cons[:, bass.ds(b, 1), :].rearrange("p o c -> p (o c)"), [P, HALF, HEADS]), ALU.mult).then_inc(ch.semaphore, ch.one())
            dve.wait_ge(ch.semaphore, ch.count)
            dve.tensor_tensor(now, now, part[:, :, HEADS:], ALU.add).then_inc(ch.semaphore, ch.one())
            dve.wait_ge(ch.semaphore, ch.count)
            dve.tensor_tensor(now, now, msk[:, h * HALF:(h + 1) * HALF].unsqueeze(2).broadcast_to([P, HALF, HEADS]), ALU.add).then_inc(ch.semaphore, ch.one())
            dve.wait_ge(ch.semaphore, ch.count)
            if h == 1:
                dve.sem_inc(s("msk_free"), 1)
                dve.sem_inc(s("feat_free"), 1)
            dve_maximum(dve, ch, h)
            dve.tensor_tensor(sw[:], ss[h][:], wt[:], ALU.mult).then_inc(ch.semaphore, ch.one())
            dve.wait_ge(ch.semaphore, ch.count)
            dve.tensor_reduce(ss[1 - h][:, HALF, :], sw[:].rearrange("p s h -> p h s"), AX.X, ALU.add).then_inc(ch.semaphore, ch.one())
            dve.wait_ge(ch.semaphore, ch.count)

        def half_l3(dve, ch, b, h, j):
            dve.tensor_reduce(g2[1 - h][:, HALF, :], g2[h][:].rearrange("p s c -> p c s"), AX.X, ALU.add).then_inc(ch.semaphore, ch.one())
            dve.wait_ge(ch.semaphore, ch.count)
            dve.sem_inc(s(f"rows_free{h}"), 1)

        def start_l0(dve, ch, b):
            dve.memset(sc[0][:, HALF, :], 0.0).then_inc(ch.semaphore, ch.one())
            dve.memset(g0[0][:, HALF, :], 0.0).then_inc(ch.semaphore, ch.one())
            dve.wait_ge(ch.semaphore, ch.count)

        def start_conv(dve, ch, b):
            m = sc[0][:, HALF, :]
            dve.tensor_copy(g1[0][:, HALF, 0:HV], blk(own1, b, 0, HV)).then_inc(ch.semaphore, ch.one())
            dve.tensor_tensor(m, blk(own1, b, HV, W1), blk(own1, b, W1, W1 + HEADS), ALU.add).then_inc(ch.semaphore, ch.one())
            dve.wait_ge(ch.semaphore, ch.count)
            dve.scalar_tensor_tensor(m, m, 0.2, m, ALU.mult, ALU.max).then_inc(ch.semaphore, ch.one())
            dve.wait_ge(ch.semaphore, ch.count)

        def start_l2(dve, ch, b):
            dve.memset(sc[0][:, HALF, :], START).then_inc(ch.semaphore, ch.one())
            dve.memset(ss[0][:, HALF, :], 0.0).then_inc(ch.semaphore, ch.one())
            dve.wait_ge(ch.semaphore, ch.count)

        def start_l3(dve, ch, b):
            dve.tensor_copy(g2[0][:, HALF, :], blk(own0, b, 0, D)).then_inc(ch.semaphore, ch.one())
            dve.wait_ge(ch.semaphore, ch.count)

        def scatter(pool, stage, target, rows=P):
            pool.wait_ge(s("table_ready"), 1)
            pool.sem_inc(s("table_ready"), -1)
            pool.indirect_dma_start(target, bass.IndirectOffsetOnAxis(ap=stage_i[0:rows].bitcast(U32), axis=0),
                                    stage[0:rows], None).then_inc(s("table_stored"), 16)

        with nc.Block() as block:
            @block.gpsimd
            def _(pool):
                with pool.Fori(0, NB) as b:
                    scatter(pool, stage0, table[0])
                pool.wait_ge(s("table_stored"), 16 * NB)

            @block.vector
            def _(dve):
                ch = Chain(s("dve_chain"))
                dve_to_l0(dve, ch, 0, lambda: None)
                dve.wait_ge(ch.semaphore, ch.count)
                dve.sem_inc(ch.semaphore, -ch.clear())
                with dve.Fori(1, NB) as b:
                    dve_to_l0(dve, ch, b, lambda: dve.wait_ge(s("table_stored"), 16 * b))
                    dve.wait_ge(ch.semaphore, ch.count)
                    dve.sem_inc(ch.semaphore, -ch.clear())

            @block.scalar
            def _(act):
                with act.Fori(0, NB) as b:
                    act_to_l0(act)

            @block.tensor
            def _(pe):
                with pe.Fori(0, NB) as b:
                    pe_to_l0(pe)

        def act_exps(act, b):
            start, end = block_range(act, b)
            with act.Fori(start, end) as j:
                for h in range(2):
                    act.wait_ge(s("shifted"), 1)
                    act.sem_inc(s("shifted"), -1)
                    act.activation(wt[:], sh[:], ACT.Exp).then_inc(s("exped"), 1)

        def edge_pass(number, rows, width, source, start, half, after, act_after, pe_after, stage, target,
                      types=False, mask=False, features=False, softmax=True):
            landed = [ctx.enter_context(nc.semaphore(f"rows_in{number}{h}")) for h in range(2)]
            before_this = NB * (number + 1)

            def gathers(pool, b):
                first_chunk, end = block_range(pool, b)
                with pool.Fori(first_chunk, end) as j:
                    for h in range(2):
                        pool.wait_ge(s(f"idx_in{h}"), 16)
                        pool.sem_inc(s(f"idx_in{h}"), -16)
                        if features and h == 0:
                            pool.wait_ge(s("first_in"), 16)
                            pool.sem_inc(s("first_in"), -16)
                            pool.wait_ge(s("feat_free"), 1)
                            pool.sem_inc(s("feat_free"), -1)
                            pool.indirect_dma_start(feat[:].rearrange("p s f -> p (s f)"), None, rec_ft,
                                                    bass.IndirectOffsetOnAxis(ap=first[:, 0:1].bitcast(U32), axis=0)).then_inc(s("feat_in"), 16)
                        pool.wait_ge(s(f"rows_free{h}"), 1)
                        pool.sem_inc(s(f"rows_free{h}"), -1)
                        for k in range(HALF):
                            pool.indirect_dma_start(rows[h][:, k, :], None, source,
                                                    bass.IndirectOffsetOnAxis(ap=idx[h][:, k:k + 1].bitcast(U32), axis=0)).then_inc(landed[h], 16)

            with nc.Block() as block:
                @block.sync
                def _(sp):
                    if mask:
                        sp.sem_inc(s("msk_free"), 1)
                    if types:
                        sp.sem_inc(s("typ_free"), 1)

                    def loads(j, gathered):
                        def one(t, c0, c1):
                            return t[bass.ds(j, 1), :, c0:c1].rearrange("j p s -> p (j s)")
                        for h in range(2):
                            gathered(landed[h], 16 * HALF)
                            sp.dma_start(idx[h][:], one(el_idx, h * HALF, (h + 1) * HALF)).then_inc(s(f"idx_in{h}"), 16)
                            if features and h == 0:
                                gathered(s("feat_in"), 16)
                                sp.dma_start(first[:], one(el_idx, SLOTS, SLOTS + 2)).then_inc(s("first_in"), 16)
                        if types:
                            sp.wait_ge(s("typ_free"), 1)
                            sp.sem_inc(s("typ_free"), -1)
                            sp.dma_start(typ[:], el_typ[bass.ds(j, 1)].rearrange("j p s -> (j p s)").partition_broadcast(TYPES)).then_inc(s("typ_in"), 16)
                        if mask:
                            sp.wait_ge(s("msk_free"), 1)
                            sp.sem_inc(s("msk_free"), -1)
                            sp.dma_start(msk[:], one(el_msk, 0, SLOTS)).then_inc(s("msk_in"), 16)

                    chunks = sp.value_load(bounds[0:1, NB:NB + 1], min_val=2, max_val=JMAX)
                    loads(0, lambda semaphore, each: None)
                    with sp.Fori(1, chunks) as j:
                        loads(j, lambda semaphore, each: sp.wait_ge(semaphore, j * each))
                    if mask:
                        sp.wait_ge(s("msk_free"), 1)
                        sp.sem_inc(s("msk_free"), -1)
                    if types:
                        sp.wait_ge(s("typ_free"), 1)
                        sp.sem_inc(s("typ_free"), -1)

                @block.gpsimd
                def _(pool):
                    gathers(pool, 0)
                    with pool.Fori(1, NB) as b:
                        gathers(pool, b)
                        scatter(pool, stage, target)
                    scatter(pool, stage, target, TAIL if target is out else P)
                    pool.wait_ge(s("table_stored"), 16 * (before_this + NB))

                @block.vector
                def _(dve):
                    ch = Chain(s("dve_chain"))
                    for h in range(2):
                        dve.sem_inc(s(f"rows_free{h}"), 1)
                    if features:
                        dve.sem_inc(s("feat_free"), 1)
                    with dve.Fori(0, NB) as b:
                        start(dve, ch, b)
                        dve.wait_ge(ch.semaphore, ch.count)
                        dve.sem_inc(ch.semaphore, -ch.clear())
                        first_chunk, end = block_range(dve, b)
                        with dve.Fori(first_chunk, end) as j:
                            for h in range(2):
                                dve.wait_ge(landed[h], 16 * HALF * (j + 1))
                                half(dve, ch, b, h, j)
                            dve.wait_ge(ch.semaphore, ch.count)
                            dve.sem_inc(ch.semaphore, -ch.clear())
                        after(dve, ch, b, lambda: dve.wait_ge(s("table_stored"), 16 * (before_this + b)))
                        dve.wait_ge(ch.semaphore, ch.count)
                        dve.sem_inc(ch.semaphore, -ch.clear())
                    for h in range(2):
                        dve.wait_ge(s(f"rows_free{h}"), 1)
                        dve.sem_inc(s(f"rows_free{h}"), -1)
                    if features:
                        dve.wait_ge(s("feat_free"), 1)
                        dve.sem_inc(s("feat_free"), -1)

                if softmax:
                    @block.scalar
                    def _(act):
                        if types:
                            act.sem_inc(s("onehot_free"), 1)
                        with act.Fori(0, NB) as b:
                            first_chunk, end = block_range(act, b)
                            with act.Fori(first_chunk, end) as j:
                                if types:
                                    act.wait_ge(s("typ_in"), 16)
                                    act.sem_inc(s("typ_in"), -16)
                                    act.activation(typ_d[:], typ[:], ACT.Square, bias=neg_p[0:TYPES]).then_inc(s("act_chain"), 1)
                                    act.wait_ge(s("act_chain"), 1)
                                    act.sem_inc(s("act_chain"), -1)
                                    act.sem_inc(s("typ_free"), 1)
                                    act.wait_ge(s("onehot_free"), 1)
                                    act.sem_inc(s("onehot_free"), -1)
                                    act.activation(onehot[:].rearrange("t p s -> t (p s)"), typ_d[:], ACT.Relu, bias=1.0, scale=-1.0).then_inc(s("onehot_in"), 1)
                                for h in range(2):
                                    act.wait_ge(s("shifted"), 1)
                                    act.sem_inc(s("shifted"), -1)
                                    act.activation(wt[:], sh[:], ACT.Exp).then_inc(s("exped"), 1)
                            act_after(act)
                        if types:
                            act.wait_ge(s("onehot_free"), 1)
                            act.sem_inc(s("onehot_free"), -1)

                if pe_after:
                    @block.tensor
                    def _(pe):
                        if types:
                            for h in range(2):
                                pe.sem_inc(s(f"rel_free{h}"), 1)
                        with pe.Fori(0, NB) as b:
                            if types:
                                first_chunk, end = block_range(pe, b)
                                with pe.Fori(first_chunk, end) as j:
                                    pe.wait_ge(s("onehot_in"), 1)
                                    pe.sem_inc(s("onehot_in"), -1)
                                    for h in range(2):
                                        pe.wait_ge(s(f"rel_free{h}"), 1)
                                        pe.sem_inc(s(f"rel_free{h}"), -1)
                                        for k in range(HALF):
                                            last = pe.matmul(ps_rel[h][:, k * D:(k + 1) * D], onehot[:, :, h * HALF + k], rel[:],
                                                             start=True, stop=True)
                                        last.then_inc(s(f"rel_ready{h}"), 1)
                            pe_after(pe)
                        if types:
                            for h in range(2):
                                pe.wait_ge(s(f"rel_free{h}"), 1)
                                pe.sem_inc(s(f"rel_free{h}"), -1)

        def act_l0(act):
            act_project(act)
            act_layernorm(act)
            act_project(act)

        def pe_l0(pe):
            pe_project(pe, wo0[:], D)
            pe_project(pe, w_g[0][:], D + REC)

        def act_l2(act):
            act_project(act)
            act_layernorm(act)
            act_layernorm(act)

        edge_pass(0, g0, W0, table[0], start_l0, half_l0, after_l0, act_l0, pe_l0, stage1, table[1], types=True, mask=True)
        edge_pass(1, g1, W1, table[1], start_conv, half_conv, after_conv(0), act_project,
                  lambda pe: pe_project(pe, w_g[1][:], D + REC), stage1, table[2])
        edge_pass(2, g1, W1, table[2], start_conv, half_conv, after_conv(1), act_project,
                  lambda pe: pe_project(pe, w_g[1][:], D + REC), stage1, table[3])
        edge_pass(3, g1, W1, table[3], start_conv, half_conv, after_conv(2), act_after_conv3,
                  lambda pe: pe_project(pe, w_l2[:], 3 * D), stage2, table[4])
        edge_pass(4, g2, D, table[4], start_l2, half_l2, after_l2, act_l2,
                  lambda pe: pe_project(pe, wo2[:], D), stage2, table[5], mask=True, features=True)
        edge_pass(5, g2, D, table[5], start_l3, half_l3, after_l3, None, None, stage2, out, softmax=False)


INPUTS = ["x", "src", "dst", "edge_attr_64", "edge_type_64", "edge_weight1", "node_vec1"]
INPUTS += ["L0_gnn_" + n for n in "query_embedding relation_embeddings Wq bq Wk bk Wv bv Wo bo".split()]
INPUTS += ["L1_gnn_" + n for n in "W1 a_src1 a_dst1 b1 W2 a_src2 a_dst2 b2".split()]
INPUTS += ["L2_gnn_" + n for n in "Wq bq Wk bk Wv bv We be Wc1 bc1 Wc2 bc2 Wd1 bd1 Wd2 bd2 Wo bo gamma beta".split()]


def kernel(**inputs):
    import numpy as np
    import concourse.bacc as bacc
    from concourse.bass_utils import run_bass_kernel_spmd

    nc = bacc.Bacc("TRN2", target_bir_lowering=False, num_devices=1)
    arrays, args = {}, {}
    for name in INPUTS:
        data = np.ascontiguousarray(inputs[name])
        arrays["in_" + name] = data
        args[name] = nc.dram_tensor("in_" + name, data.shape, mybir.dt.from_np(data.dtype), kind="ExternalInput").ap()
    out = nc.dram_tensor("out_0", args["x"].shape, F32, kind="ExternalOutput").ap()
    program(nc, args, out)
    result = run_bass_kernel_spmd(nc, [arrays], core_ids=[0])
    return result.results[0]["out_0"]
```

```python
from contextlib import ExitStack

import concourse.bass as bass
from concourse import mybir

ALU = mybir.AluOpType
ACT = mybir.ActivationFunctionType
AX = mybir.AxisListType
F32 = mybir.dt.float32
BF16 = mybir.dt.bfloat16
I32 = mybir.dt.int32
U32 = mybir.dt.uint32

P = 128
HEADS = 8
HALF = 4
SLOTS = 2 * HALF
RUN = 64
RC = RUN // SLOTS
EP = 125
BIG = 1e30
START = -1e29
EPS = 1e-5
RSQRT_SEED = 1597463007.0
KEYCAP = 4000
KEYSTEP = 4096


class Chain:

    def __init__(self, semaphore):
        self.semaphore, self.count = semaphore, 0

    def one(self):
        self.count += 1
        return 1

    def clear(self):
        count, self.count = self.count, 0
        return count


def heads(ap):
    return ap.rearrange("p (h d) -> p h d", h=HEADS)


def program(nc, a, out):
    N, D = a["x"].shape
    E = a["src"].shape[0]
    NB = -(-N // P)
    NPAD = NB * P
    TAIL = N - (NB - 1) * P
    EC = E // EP
    assert EP * EC == E and D == P
    HD = D // HEADS
    ED = a["edge_attr_64"].shape[1]
    CH, HB = 5, 3
    CB = 11
    FEARLY = EC // CB - 2 * NB
    assert EC % (CH * HB) == 0 and EC % CB == 0 and FEARLY % 2 == 1
    CW = a["L2_gnn_Wc1"].shape[1]
    CG = P // CW
    NG = -(-NB // CG)
    JMAX = E // SLOTS + NB + 2 * RC
    V = HD + 1
    HV = HEADS * V
    W0 = D + HV
    W1 = HV + HEADS
    REC = 2 * HEADS
    TYPES = a["L0_gnn_relation_embeddings"].shape[0]
    SCALE = 1.0 / HD ** 0.5

    with ExitStack() as ctx:
        def sb(name, shape, dt=F32):
            return ctx.enter_context(nc.sbuf_tensor(name, shape, dt))

        made = {}

        def s(name):
            if name not in made:
                made[name] = ctx.enter_context(nc.semaphore(name))
            return made[name]

        def dram(name, shape, dt=F32):
            return nc.dram_tensor(name, shape, dt, kind="Internal").ap()

        rec_id = dram("rec_id", [E + RUN, 2], I32)
        rec_ft = dram("rec_ft", [E + RUN, REC])
        el_idx = dram("el_idx", [JMAX, P, 12], I32)
        el_msk = dram("el_msk", [JMAX, P, SLOTS])
        el_typ = dram("el_typ", [JMAX, 2, P, HALF])
        dist_t = dram("dist_t", [EC, EP])
        keyrow = dram("keyrow", [NPAD])
        info_d = dram("info_d", [NPAD, 8])
        table = [dram(f"table{n}", [NPAD, w]) for n, w in enumerate([W0, W1, W1, W1, D, D])]

        ident = sb("ident", [P, P])
        ones = sb("ones", [P, P])
        zerob = sb("zerob", [P, P], BF16)
        zero_i = sb("zero_i", [RUN, REC], I32)
        before = sb("before", [P, P])
        iota_r = sb("iota_r", [P, P])
        iota_p = sb("iota_p", [P, 1])
        neg_p = sb("neg_p", [P, 1])
        run_at = sb("run_at", [P, RC])
        node_id = sb("node_id", [P, NB])
        head_of = sb("head_of", [P, HEADS])

        w_l0 = sb("w_l0", [P, 3 * D])
        b_l0 = sb("b_l0", [P, 3 * D])
        w_bot = sb("w_bot", [P, 2 * D])
        qe = sb("qe", [P, 1])
        rel = sb("rel", [2 * TYPES, D])
        wo0 = sb("wo0", [P, D])
        bo0 = sb("bo0", [P, D])
        w_g = [sb(f"w_g{n}", [P, D + REC]) for n in range(2)]
        a_col = sb("a_col", [P, 4])
        a_blk = sb("a_blk", [P, REC])
        b_g = [sb(f"b_g{n}", [P, D]) for n in range(2)]
        w_l2 = sb("w_l2", [P, 3 * D])
        b_l2 = sb("b_l2", [P, 3 * D])
        wo2 = sb("wo2", [P, D])
        bo2 = sb("bo2", [P, D])
        gam = sb("gam", [P, D])
        bet = sb("bet", [P, D])
        we2 = sb("we2", [P, REC])
        wd2 = sb("wd2", [P, 8 * HEADS])
        wd1 = sb("wd1", [P, 1])
        bd1 = sb("bd1", [P, 1])
        b_ft = sb("b_ft", [1, REC])
        wc1 = sb("wc1", [P, CW])
        bc1 = sb("bc1", [P, CW])
        wc2 = sb("wc2", [P, CG * HEADS])
        bc2 = sb("bc2", [P, HEADS])

        xs = sb("xs", [P, NB, D])
        own0 = sb("own0", [P, NB, D])
        own1 = sb("own1", [P, NB, HV + REC])
        own2 = sb("own2", [P, NB, 3 * D])
        cons = sb("cons", [P, NB, HEADS])
        dist = sb("dist", [EP, EC])
        info = sb("info", [P, NB, 8])
        perm = sb("perm", [P, NB], I32)
        permx = sb("permx", [P, NB], I32)
        dis = sb("dis", [P, NB])
        real = sb("real", [P, NB])
        padneg = sb("padneg", [P, NB])
        bounds = sb("bounds", [1, NB + 1], I32)
        rbounds = sb("rbounds", [1, NB + 1], I32)

        mvs = sb("mvs", [P, NB, 2])
        vars_ = sb("vars", [P, NB])
        st6s = sb("st6s", [P, NB, 6])
        c_hid = sb("c_hid", [P, NG * CG, CW])
        c_t = sb("c_t", [P, NG * P])
        c_z = sb("c_z", [P, NB, HEADS])
        c_pos = sb("c_pos", [P, NB, HEADS])
        c_e = sb("c_e", [P, NB, HEADS])
        rstds = sb("rstds", [P, NB])
        news = sb("news", [P, NB])
        st6 = sb("st6", [P, 6])
        mv = sb("mv", [P, 2])
        var = sb("var", [P, 1])
        rstd = sb("rstd", [P, 1])
        newt = sb("newt", [P, 1])
        hid = sb("hid", [P, D])
        hid_t = sb("hid_t", [P, D])
        den = sb("den", [P, HEADS])
        tmp = sb("tmp", [P, D])
        tmp2 = sb("tmp2", [P, D])
        col = sb("col", [P, 4])
        stage0 = sb("stage0", [P, W0])
        stage1 = sb("stage1", [P, W1])
        stage2 = sb("stage2", [P, D])
        stage_i = sb("stage_i", [P, 1], I32)

        ss = sb("ss", [P, SLOTS + 1, HEADS])

        bank = [ctx.enter_context(nc.psum_tensor(f"bank{n}", [P, 512], F32)) for n in range(8)]
        ps_t, ps_p, ps_rel = bank[0], bank[1], bank[2:4]

        with ExitStack() as early:
            def eb(name, shape, dt=F32):
                return early.enter_context(nc.sbuf_tensor(name, shape, dt))

            dst_i = eb("dst_i", [EP, EC], I32)
            rec_i = eb("rec_i", [EP, EC, 2], I32)
            src_i = eb("src_i", [EP, EC], I32)
            typ_i = eb("typ_i", [EP, EC], I32)
            int_t = eb("int_t", [EP, EC], I32)
            dst_f = eb("dst_f", [EP, EC])
            lo = [eb(f"lo{n}", [EP, EC]) for n in range(2)]
            hi = [eb(f"hi{n}", [EP, EC]) for n in range(2)]
            oh_lo = [eb(f"oh_lo{k}", [EP, 2, CH, P], BF16) for k in range(HB)]
            oh_hi = [eb(f"oh_hi{k}", [EP, 2, CH, NB], BF16) for k in range(HB)]
            deg = eb("deg", [P, NB])
            tot = eb("tot", [P, NB])
            cum = eb("cum", [P, NB])
            key = eb("key", [P, NB])
            pad_k = eb("pad_k", [P, NB])
            keyall = eb("keyall", [P, NPAD])
            greater = eb("greater", [P, NPAD], BF16)
            rank = eb("rank", [P, NB])
            rank_i = eb("rank_i", [P, NB], I32)
            inf = eb("inf", [P, NB, 8])
            w_t = eb("w_t", [P, D])
            blk_max = eb("blk_max", [NB, 2])
            blk_i = eb("blk_i", [NB, 2], I32)
            least = eb("least", [NB, 1])
            bnd_f = eb("bnd_f", [1, 2, NB + 1])
            before_nb = before[0:NB, 0:NB + 1]

            def bc(v, n=P):
                return v.partition_broadcast(n)

            with nc.Block() as block:
                @block.sync
                def _(sp):
                    sp.dma_start(dst_i[:], a["dst"].rearrange("(p c) -> p c", p=EP)).then_inc(s("dst_loaded"), 16)
                    sp.dma_start(src_i[:], a["src"].rearrange("(p c) -> p c", p=EP)).then_inc(s("src_loaded"), 16)
                    sp.dma_start(typ_i[:], a["edge_type_64"].rearrange("(p c) -> p c", p=EP)).then_inc(s("typ_loaded"), 16)
                    n = 0
                    wk, wq = a["L0_gnn_Wk"], a["L0_gnn_Wq"]
                    loads = [
                        (w_l0[:, 0:D], wk[0:D]), (w_l0[:, D:2 * D], a["L0_gnn_Wv"]), (w_l0[:, 2 * D:], wq[0:D]),
                        (w_bot[:, 0:D], wk[D:2 * D]), (w_bot[:, D:], wq[D:2 * D]),
                        (b_l0[:, 0:D], bc(a["L0_gnn_bk"])), (b_l0[:, D:2 * D], bc(a["L0_gnn_bv"])),
                        (b_l0[:, 2 * D:], bc(a["L0_gnn_bq"])),
                        (qe[:], a["L0_gnn_query_embedding"].rearrange("a (p b) -> p (a b)", b=1)),
                        (rel[0:TYPES], a["L0_gnn_relation_embeddings"]), (rel[TYPES:], a["L0_gnn_relation_embeddings"]),
                        (wo0[:], a["L0_gnn_Wo"]), (bo0[:], bc(a["L0_gnn_bo"])),
                        (w_g[0][:, 0:D], a["L1_gnn_W1"]), (w_g[1][:, 0:D], a["L1_gnn_W2"]),
                        (b_g[0][:], bc(a["L1_gnn_b1"])), (b_g[1][:], bc(a["L1_gnn_b2"])),
                        (w_l2[:, 0:D], a["L2_gnn_Wk"]), (w_l2[:, D:2 * D], a["L2_gnn_Wv"]), (w_l2[:, 2 * D:], a["L2_gnn_Wq"]),
                        (b_l2[:, 0:D], bc(a["L2_gnn_bk"])), (b_l2[:, D:2 * D], bc(a["L2_gnn_bv"])),
                        (b_l2[:, 2 * D:], bc(a["L2_gnn_bq"])),
                        (wo2[:], a["L2_gnn_Wo"]), (bo2[:], bc(a["L2_gnn_bo"])),
                        (gam[:], bc(a["L2_gnn_gamma"])), (bet[:], bc(a["L2_gnn_beta"])),
                        (b_ft[:, 0:HEADS], bc(a["L2_gnn_be"], 1)), (b_ft[:, HEADS:], bc(a["L2_gnn_bd2"], 1)),
                        (wc1[:], bc(a["L2_gnn_Wc1"].rearrange("a b -> (a b)"))), (bc1[:], bc(a["L2_gnn_bc1"])),
                        (bc2[:], bc(a["L2_gnn_bc2"])),
                    ]
                    loads += [(wd1[i * HD:(i + 1) * HD], a["L2_gnn_Wd1"].rearrange("a d -> d a")) for i in range(8)]
                    loads += [(dist[:], a["edge_weight1"].rearrange("(p c) o -> p (c o)", p=EP))]
                    loads += [(bd1[i * HD:(i + 1) * HD], a["L2_gnn_bd1"].rearrange("(d o) -> d o", o=1)) for i in range(8)]
                    loads += [(a_col[:, n:n + 1], a[f"L1_gnn_{w}"].rearrange("h (d o) -> (h d) o", o=1))
                              for n, w in enumerate(["a_src1", "a_dst1", "a_src2", "a_dst2"])]
                    for to, of in loads:
                        sp.dma_start(to, of).then_inc(s("weights"), 16)
                        n += 16
                    sp.wait_ge(s("cleared"), 1)
                    for i in range(2):
                        sp.dma_start(we2[i * ED:(i + 1) * ED, i * HEADS:(i + 1) * HEADS], a["L2_gnn_We"]).then_inc(s("weights"), 16)
                        n += 16
                    for i in range(8):
                        sp.dma_start(wd2[i * HD:(i + 1) * HD, i * HEADS:(i + 1) * HEADS], a["L2_gnn_Wd2"]).then_inc(s("weights"), 16)
                        n += 16
                    for i in range(CG):
                        sp.dma_start(wc2[i * CW:(i + 1) * CW, i * HEADS:(i + 1) * HEADS], a["L2_gnn_Wc2"]).then_inc(s("weights"), 16)
                        n += 16
                    nv = a["node_vec1"]
                    with nc.allow_non_contiguous_dma(reason="one word per node"):
                        sp.dma_start(inf[:, 0:NB - 1, 4], nv[0:(NB - 1) * P].rearrange("(b p) o -> p (b o)", p=P)).then_inc(s("weights"), 16)
                        sp.dma_start(inf[0:TAIL, NB - 1:NB, 4], nv[(NB - 1) * P:N]).then_inc(s("weights"), 16)
                    n += 32
                    sp.dma_start(rec_id[E:E + RUN], zero_i[:, 0:2]).then_inc(s("weights"), 16)
                    sp.dma_start(rec_ft[E:E + RUN], zero_i[:].bitcast(F32)).then_inc(s("weights"), 16)
                    n += 32
                    sp.wait_ge(s("rec_ready"), 1)
                    sp.sem_inc(s("rec_ready"), -1)
                    sp.dma_start(rec_id[0:E].rearrange("(p c) w -> p c w", p=EP), rec_i[:]).then_inc(s("weights"), 16)
                    n += 16
                    sp.wait_ge(s("key_ready"), 1)
                    sp.sem_inc(s("key_ready"), -1)
                    with nc.allow_non_contiguous_dma(reason="one word per node"):
                        sp.dma_start(keyrow.rearrange("(b p) -> p b", p=P), key[:]).then_inc(s("key_stored"), 16)
                    sp.wait_ge(s("key_stored"), 16)
                    sp.sem_inc(s("key_stored"), -16)
                    sp.dma_start(keyall[:], bc(keyrow)).then_inc(s("keys"), 16)
                    sp.wait_ge(s("weights"), n)
                    sp.sem_inc(s("weights"), -n)
                    sp.sem_inc(s("weights_in"), 2)
                    sp.wait_ge(s("info_stored"), 16 * NB)
                    sp.dma_start(info[:], info_d.rearrange("(b p) w -> p b w", p=P)).then_inc(s("info_in"), 16)

                @block.gpsimd
                def _(pool):
                    ch = Chain(s("pool_chain"))
                    pool.memset(zerob[:], 0.0).then_inc(ch.semaphore, ch.one())
                    pool.memset(zero_i[:], 0).then_inc(ch.semaphore, ch.one())
                    pool.memset(inf[:], 0.0).then_inc(ch.semaphore, ch.one())
                    pool.memset(we2[:], 0.0).then_inc(ch.semaphore, ch.one())
                    pool.memset(wd2[:], 0.0).then_inc(ch.semaphore, ch.one())
                    pool.memset(wc2[:], 0.0).then_inc(ch.semaphore, ch.one())
                    pool.memset(ones[:], 1.0).then_inc(ch.semaphore, ch.one())
                    pool.memset(before[:], 1.0).then_inc(ch.semaphore, ch.one())
                    pool.memset(head_of[:], 1.0).then_inc(ch.semaphore, ch.one())
                    pool.memset(stage0[:], 1.0).then_inc(ch.semaphore, ch.one())
                    pool.memset(own1[:], 1.0).then_inc(ch.semaphore, ch.one())
                    pool.iota(iota_r[:], [[1, P]], base=0, channel_multiplier=0, allow_small_or_imprecise_dtypes=True).then_inc(ch.semaphore, ch.one())
                    pool.iota(iota_p[:], [[0, 1]], base=0, channel_multiplier=1, allow_small_or_imprecise_dtypes=True).then_inc(ch.semaphore, ch.one())
                    pool.iota(run_at[:], [[SLOTS, RC]], base=0, channel_multiplier=0, allow_small_or_imprecise_dtypes=True).then_inc(ch.semaphore, ch.one())
                    pool.iota(node_id[:], [[P, NB]], base=0, channel_multiplier=1, allow_small_or_imprecise_dtypes=True).then_inc(ch.semaphore, ch.one())
                    pool.memset(ss[:], 1.0).then_inc(ch.semaphore, ch.one())
                    pool.wait_ge(ch.semaphore, ch.count)
                    pool.sem_inc(s("cleared"), 1)
                    pool.affine_select(out=ident[:], in_=ones[:], pattern=[[-1, P]], compare_op=ALU.is_equal,
                                       fill=0.0, base=0, channel_multiplier=1).then_inc(ch.semaphore, ch.one())
                    pool.affine_select(out=before[:], in_=before[:], pattern=[[1, P]], compare_op=ALU.is_gt,
                                       fill=0.0, base=0, channel_multiplier=-1).then_inc(ch.semaphore, ch.one())
                    pool.affine_select(out=head_of[:], in_=head_of[:], pattern=[[-HD, HEADS]], compare_op=ALU.is_ge,
                                       fill=0.0, base=0, channel_multiplier=1).then_inc(ch.semaphore, ch.one())
                    pool.wait_ge(ch.semaphore, ch.count)
                    pool.affine_select(out=head_of[:], in_=head_of[:], pattern=[[HD, HEADS]], compare_op=ALU.is_ge,
                                       fill=0.0, base=HD - 1, channel_multiplier=-1).then_inc(ch.semaphore, ch.one())
                    pool.wait_ge(ch.semaphore, ch.count)
                    pool.sem_inc(s("consts"), 2)
                    pool.wait_ge(ch.semaphore, ch.count)
                    pool.sem_inc(ch.semaphore, -ch.clear())
                    pool.wait_ge(s("rank_ready"), 1)
                    pool.sem_inc(s("rank_ready"), -1)
                    for b in range(NB):
                        pool.indirect_dma_start(info_d, bass.IndirectOffsetOnAxis(ap=rank_i[:, b:b + 1].bitcast(U32), axis=0),
                                                inf[:, b, :], None).then_inc(s("info_stored"), 16)

                @block.vector
                def _(dve):
                    ch = Chain(s("dve_chain"))
                    dve.wait_ge(s("dst_loaded"), 16)
                    dve.sem_inc(s("dst_loaded"), -16)
                    dve.wait_ge(s("consts"), 1)
                    dve.sem_inc(s("consts"), -1)
                    dve.tensor_copy(dst_f[:], dst_i[:]).then_inc(ch.semaphore, ch.one())
                    dve.tensor_scalar(neg_p[0:TYPES], iota_p[0:TYPES], -1.0, None, ALU.mult).then_inc(ch.semaphore, ch.one())
                    dve.tensor_scalar(neg_p[TYPES:], iota_p[TYPES:], -1.0, float(TYPES), ALU.mult, ALU.add).then_inc(ch.semaphore, ch.one())
                    for n, nodes in enumerate([dst_i, src_i]):
                        if n:
                            dve.wait_ge(s("src_loaded"), 16)
                            dve.sem_inc(s("src_loaded"), -16)
                        dve.tensor_scalar(int_t[:], nodes[:], P - 1, None, ALU.bitwise_and).then_inc(ch.semaphore, ch.one())
                        dve.wait_ge(ch.semaphore, ch.count)
                        dve.tensor_copy(lo[n][:], int_t[:]).then_inc(ch.semaphore, ch.one())
                        dve.wait_ge(ch.semaphore, ch.count)
                        dve.tensor_scalar(int_t[:], nodes[:], 7, None, ALU.logical_shift_right).then_inc(ch.semaphore, ch.one())
                        dve.wait_ge(ch.semaphore, ch.count)
                        dve.tensor_copy(hi[n][:], int_t[:]).then_inc(ch.semaphore, ch.one())
                        dve.wait_ge(ch.semaphore, ch.count)
                    dve.wait_ge(s("typ_loaded"), 16)
                    dve.sem_inc(s("typ_loaded"), -16)
                    dve.tensor_copy(rec_i[:, :, 0], src_i[:]).then_inc(ch.semaphore, ch.one())
                    dve.tensor_copy(rec_i[:, :, 1], typ_i[:]).then_inc(ch.semaphore, ch.one())
                    dve.wait_ge(ch.semaphore, ch.count)
                    dve.sem_inc(s("rec_ready"), 1)
                    dve.wait_ge(ch.semaphore, ch.count)
                    dve.sem_inc(ch.semaphore, -ch.clear())
                    with dve.Fori(0, EC // (CH * HB)) as i:
                        for k in range(HB):
                            c = i * (CH * HB) + k * CH
                            dve.wait_ge(s(f"onehot_free{k}"), 1)
                            dve.sem_inc(s(f"onehot_free{k}"), -1)
                            for n in range(2):
                                dve.tensor_tensor(oh_lo[k][:, n], iota_r[0:EP].unsqueeze(1).broadcast_to([EP, CH, P]),
                                                  lo[n][:, bass.ds(c, CH)].unsqueeze(2).broadcast_to([EP, CH, P]),
                                                  ALU.is_equal).then_inc(s(f"onehot_ready{k}"), 1)
                                dve.tensor_tensor(oh_hi[k][:, n], iota_r[0:EP, 0:NB].unsqueeze(1).broadcast_to([EP, CH, NB]),
                                                  hi[n][:, bass.ds(c, CH)].unsqueeze(2).broadcast_to([EP, CH, NB]),
                                                  ALU.is_equal).then_inc(s(f"onehot_ready{k}"), 1)
                    dve.wait_ge(s("counted"), 1)
                    dve.sem_inc(s("counted"), -1)
                    for k in range(HB):
                        dve.wait_ge(s(f"onehot_free{k}"), 1)
                        dve.sem_inc(s(f"onehot_free{k}"), -1)
                    dve.tensor_copy(deg[:], bank[4][:, 0:NB]).then_inc(ch.semaphore, ch.one())
                    dve.tensor_copy(inf[:, :, 2], bank[4][:, 0:NB]).then_inc(ch.semaphore, ch.one())
                    dve.tensor_copy(inf[:, :, 3], bank[5][:, 0:NB]).then_inc(ch.semaphore, ch.one())
                    dve.tensor_copy(inf[:, :, 0], node_id[:]).then_inc(ch.semaphore, ch.one())
                    dve.tensor_scalar(pad_k[:], node_id[:], float(N), -float(KEYSTEP), ALU.is_ge, ALU.mult).then_inc(ch.semaphore, ch.one())
                    dve.wait_ge(ch.semaphore, ch.count)
                    dve.sem_inc(s("deg_ready"), 1)
                    dve.tensor_scalar(key[:], deg[:], float(KEYCAP), float(KEYSTEP), ALU.min, ALU.mult).then_inc(ch.semaphore, ch.one())
                    dve.wait_ge(ch.semaphore, ch.count)
                    dve.tensor_tensor(key[:], key[:], pad_k[:], ALU.add).then_inc(ch.semaphore, ch.one())
                    dve.wait_ge(ch.semaphore, ch.count)
                    dve.tensor_tensor(key[:], key[:], node_id[:], ALU.subtract).then_inc(ch.semaphore, ch.one())
                    dve.wait_ge(ch.semaphore, ch.count)
                    dve.tensor_scalar(key[:], key[:], float(NPAD), None, ALU.add).then_inc(ch.semaphore, ch.one())
                    dve.wait_ge(ch.semaphore, ch.count)
                    dve.sem_inc(s("key_ready"), 1)
                    dve.wait_ge(s("sums_ready"), 1)
                    dve.sem_inc(s("sums_ready"), -1)
                    dve.tensor_copy(tot[:], bank[6][:, NB:2 * NB]).then_inc(ch.semaphore, ch.one())
                    dve.wait_ge(ch.semaphore, ch.count)
                    dve.tensor_tensor_scan(cum[:], ones[:, 0:NB], tot[:], 0.0, ALU.mult, ALU.add).then_inc(ch.semaphore, ch.one())
                    dve.wait_ge(ch.semaphore, ch.count)
                    dve.tensor_tensor(cum[:], cum[:], tot[:], ALU.subtract).then_inc(ch.semaphore, ch.one())
                    dve.wait_ge(ch.semaphore, ch.count)
                    dve.tensor_tensor(inf[:, :, 1], cum[:], bank[6][:, 0:NB], ALU.add).then_inc(ch.semaphore, ch.one())
                    dve.wait_ge(ch.semaphore, ch.count)
                    dve.wait_ge(s("keys"), 16)
                    dve.sem_inc(s("keys"), -16)
                    with dve.Fori(0, NB) as b:
                        dve.tensor_scalar(greater[:], keyall[:], key[:, bass.ds(b, 1)], 0.0, ALU.is_gt, ALU.add,
                                          accum_out=rank[:, bass.ds(b, 1)]).then_inc(s("ranked"), 1)
                        dve.wait_ge(s("ranked"), 1)
                        dve.sem_inc(s("ranked"), -1)
                    dve.tensor_copy(rank_i[:], rank[:]).then_inc(ch.semaphore, ch.one())
                    dve.wait_ge(ch.semaphore, ch.count)
                    dve.wait_ge(s("weights_in"), 2)
                    dve.sem_inc(s("rank_ready"), 1)
                    for n in range(2):
                        if n:
                            dve.wait_ge(s("a_used"), 1)
                            dve.sem_inc(s("a_used"), -1)
                        dve.tensor_scalar(a_blk[:, 0:HEADS], head_of[:], a_col[:, 2 * n:2 * n + 1], None, ALU.mult).then_inc(ch.semaphore, ch.one())
                        dve.tensor_scalar(a_blk[:, HEADS:], head_of[:], a_col[:, 2 * n + 1:2 * n + 2], None, ALU.mult).then_inc(ch.semaphore, ch.one())
                        dve.wait_ge(ch.semaphore, ch.count)
                        dve.sem_inc(s("a_ready"), 1)
                        dve.wait_ge(s("wt_psum"), 1)
                        dve.sem_inc(s("wt_psum"), -1)
                        dve.tensor_copy(w_t[:], bank[0][:, 0:D]).then_inc(s("wt_ready"), 1)
                        dve.wait_ge(s("wa_ready"), 1)
                        dve.sem_inc(s("wa_ready"), -1)
                        dve.tensor_copy(w_g[n][:, D:], bank[1][:, 0:REC]).then_inc(ch.semaphore, ch.one())
                        dve.wait_ge(ch.semaphore, ch.count)
                        dve.sem_inc(s("a_used"), 1)
                    dve.wait_ge(s("a_used"), 1)
                    dve.sem_inc(s("a_used"), -1)
                    dve.wait_ge(s("query_ready"), 1)
                    dve.sem_inc(s("query_ready"), -1)
                    dve.tensor_tensor(b_l0[:, 0:D], b_l0[:, 0:D], bank[7][:, 0:D], ALU.add).then_inc(ch.semaphore, ch.one())
                    dve.tensor_tensor(b_l0[:, 2 * D:], b_l0[:, 2 * D:], bank[7][:, D:2 * D], ALU.add).then_inc(ch.semaphore, ch.one())
                    dve.wait_ge(ch.semaphore, ch.count)
                    dve.wait_ge(s("info_in"), 16)
                    dve.sem_inc(s("info_in"), -16)
                    dve.tensor_copy(perm[:], info[:, :, 0]).then_inc(ch.semaphore, ch.one())
                    dve.tensor_scalar(permx[:], info[:, :, 0], float(N - 1), None, ALU.min).then_inc(ch.semaphore, ch.one())
                    dve.tensor_scalar(real[:], info[:, :, 0], float(N), None, ALU.is_lt).then_inc(ch.semaphore, ch.one())
                    dve.wait_ge(ch.semaphore, ch.count)
                    dve.tensor_scalar(padneg[:], real[:], -1.0, BIG, ALU.add, ALU.mult).then_inc(ch.semaphore, ch.one())
                    dve.tensor_scalar(dis[:], info[:, :, 3], 1.0, None, ALU.add).then_inc(ch.semaphore, ch.one())
                    dve.wait_ge(ch.semaphore, ch.count)
                    dve.tensor_copy(deg[:], info[:, :, 2]).then_inc(ch.semaphore, ch.one())
                    dve.wait_ge(ch.semaphore, ch.count)
                    dve.sem_inc(s("degp_ready"), 1)
                    dve.wait_ge(s("degt_ready"), 1)
                    dve.sem_inc(s("degt_ready"), -1)
                    dve.tensor_reduce(blk_max[:, 0:1], bank[0][0:NB, 0:P], AX.X, ALU.max).then_inc(ch.semaphore, ch.one())
                    dve.wait_ge(ch.semaphore, ch.count)
                    dve.tensor_scalar(blk_max[:, 1:2], blk_max[:, 0:1], float(RUN - 1), None, ALU.add).then_inc(ch.semaphore, ch.one())
                    dve.wait_ge(ch.semaphore, ch.count)
                    dve.tensor_scalar(blk_max[:, 0:1], blk_max[:, 0:1], float(SLOTS - 1), None, ALU.add).then_inc(ch.semaphore, ch.one())
                    dve.wait_ge(ch.semaphore, ch.count)
                    dve.tensor_copy(blk_i[:], blk_max[:]).then_inc(ch.semaphore, ch.one())
                    dve.wait_ge(ch.semaphore, ch.count)
                    dve.tensor_scalar(blk_i[:, 0:1], blk_i[:, 0:1], SLOTS.bit_length() - 1, None, ALU.logical_shift_right).then_inc(ch.semaphore, ch.one())
                    dve.tensor_scalar(blk_i[:, 1:2], blk_i[:, 1:2], RUN.bit_length() - 1, None, ALU.logical_shift_right).then_inc(ch.semaphore, ch.one())
                    dve.wait_ge(ch.semaphore, ch.count)
                    dve.tensor_copy(blk_max[:], blk_i[:]).then_inc(ch.semaphore, ch.one())
                    dve.wait_ge(ch.semaphore, ch.count)
                    dve.tensor_scalar(least[:], iota_p[0:NB], float(NB - 1), 1.0, ALU.is_ge, ALU.add).then_inc(ch.semaphore, ch.one())
                    dve.wait_ge(ch.semaphore, ch.count)
                    dve.tensor_tensor(blk_max[:, 0:1], blk_max[:, 0:1], least[:], ALU.max).then_inc(ch.semaphore, ch.one())
                    dve.tensor_scalar(blk_max[:, 1:2], blk_max[:, 1:2], 1.0, None, ALU.max).then_inc(ch.semaphore, ch.one())
                    dve.wait_ge(ch.semaphore, ch.count)
                    dve.sem_inc(s("blk_ready"), 1)
                    dve.wait_ge(s("bnd_ready"), 1)
                    dve.sem_inc(s("bnd_ready"), -1)
                    dve.tensor_copy(bounds[:], bank[6][0:1, 0:NB + 1]).then_inc(ch.semaphore, ch.one())
                    dve.tensor_copy(rbounds[:], bank[6][0:1, 32:32 + NB + 1]).then_inc(ch.semaphore, ch.one())
                    dve.wait_ge(ch.semaphore, ch.count)
                    dve.sem_inc(s("dis_arg"), 1)
                    dve.wait_ge(s("dis_exp"), 1)
                    dve.sem_inc(s("dis_exp"), -1)
                    dve.tensor_tensor(cum[:], tot[:], tot[:], ALU.mult).then_inc(ch.semaphore, ch.one())
                    dve.wait_ge(ch.semaphore, ch.count)
                    dve.tensor_tensor(cum[:], cum[:], dis[:], ALU.mult).then_inc(ch.semaphore, ch.one())
                    dve.wait_ge(ch.semaphore, ch.count)
                    dve.tensor_scalar(cum[:], cum[:], -0.5, 1.5, ALU.mult, ALU.add).then_inc(ch.semaphore, ch.one())
                    dve.wait_ge(ch.semaphore, ch.count)
                    dve.tensor_tensor(dis[:], tot[:], cum[:], ALU.mult).then_inc(ch.semaphore, ch.one())
                    dve.wait_ge(ch.semaphore, ch.count)
                    dve.tensor_tensor(dis[:], dis[:], real[:], ALU.mult).then_inc(ch.semaphore, ch.one())
                    dve.wait_ge(ch.semaphore, ch.count)
                    dve.sem_inc(ch.semaphore, -ch.clear())

                @block.scalar
                def _(act):
                    act.wait_ge(s("dis_arg"), 1)
                    act.sem_inc(s("dis_arg"), -1)
                    act.activation(cum[:], dis[:], ACT.Ln).then_inc(s("act_chain"), 1)
                    act.wait_ge(s("act_chain"), 1)
                    act.sem_inc(s("act_chain"), -1)
                    act.activation(tot[:], cum[:], ACT.Exp, scale=-0.5).then_inc(s("dis_exp"), 1)

                @block.tensor
                def _(pe):
                    for k in range(HB):
                        pe.sem_inc(s(f"onehot_free{k}"), 1)
                    pe.wait_ge(s("consts"), 1)
                    pe.sem_inc(s("consts"), -1)
                    for n in range(2):
                        pe.matmul(bank[4 + n][:, 0:NB], zerob[:], zerob[:, 0:NB], start=True, stop=False, skip_group_check=True)
                    with pe.Fori(0, EC // (CH * HB)) as i:
                        for k in range(HB):
                            pe.wait_ge(s(f"onehot_ready{k}"), 4)
                            pe.sem_inc(s(f"onehot_ready{k}"), -4)
                            for c in range(CH):
                                for n in range(2):
                                    last = pe.matmul(bank[4 + n][:, 0:NB], oh_lo[k][:, n, c], oh_hi[k][:, n, c],
                                                     start=False, stop=False, skip_group_check=True)
                            last.then_inc(s(f"onehot_free{k}"), 1)
                    for n in range(2):
                        last = pe.matmul(bank[4 + n][:, 0:NB], zerob[:], zerob[:, 0:NB], start=False, stop=True, skip_group_check=True)
                    last.then_inc(s("counted"), 1)
                    pe.wait_ge(s("deg_ready"), 1)
                    pe.sem_inc(s("deg_ready"), -1)
                    pe.matmul(bank[6][:, 0:NB], before[:], deg[:], start=True, stop=True)
                    pe.matmul(bank[6][:, NB:2 * NB], ones[:], deg[:], start=True, stop=True).then_inc(s("sums_ready"), 1)
                    pe.wait_ge(s("weights_in"), 2)
                    for n in range(2):
                        pe.wait_ge(s("a_ready"), 1)
                        pe.sem_inc(s("a_ready"), -1)
                        pe.transpose(bank[0][:, 0:D], w_g[n][:, 0:D], ident[:]).then_inc(s("wt_psum"), 1)
                        pe.wait_ge(s("wt_ready"), 1)
                        pe.sem_inc(s("wt_ready"), -1)
                        pe.matmul(bank[1][:, 0:REC], w_t[:], a_blk[:], start=True, stop=True).then_inc(s("wa_ready"), 1)
                    pe.matmul(bank[7][:, 0:2 * D], qe[:].broadcast_to([P, P]), w_bot[:], start=True, stop=True).then_inc(s("query_ready"), 1)
                    pe.wait_ge(s("degp_ready"), 1)
                    pe.sem_inc(s("degp_ready"), -1)
                    pe.transpose(bank[0][0:NB, 0:P], deg[:], ident[:]).then_inc(s("degt_ready"), 1)
                    pe.wait_ge(s("blk_ready"), 1)
                    pe.sem_inc(s("blk_ready"), -1)
                    pe.matmul(bank[6][0:1, 0:NB + 1], blk_max[:, 0:1], before_nb, start=True, stop=True)
                    pe.matmul(bank[6][0:1, 32:32 + NB + 1], blk_max[:, 1:2], before_nb, start=True, stop=True).then_inc(s("bnd_ready"), 1)

        def block_range(engine, b, table=bounds, most=JMAX):
            return (engine.value_load(table[0:1, bass.ds(b, 1)], min_val=0, max_val=most),
                    engine.value_load(table[0:1, bass.ds(b + 1, 1)], min_val=1, max_val=most))

        attr = [sb(f"attr{k}", [EP, CB * ED]) for k in range(2)]
        near = [sb(f"near{k}", [P, 2, EP]) for k in range(2)]
        turn = sb("turn", [P, EP])
        a_t = [sb(f"a_t{k}", [P, 6, EP]) for k in range(2)]
        h_t = [sb(f"h_t{k}", [P, 2, EP]) for k in range(2)]
        fts = [sb(f"fts{k}", [EP, CB, REC]) for k in range(2)]
        ps_a = [bank[2:4], bank[6:8]]
        ps_f = [bank[4 + k][0:EP, 0:CB * REC] for k in range(2)]
        pairs = CB // 2
        groups = [(g, min(8, CB - g)) for g in range(0, CB, 8)]
        assert pairs == 5 and CB % 2 == 1 and len(groups) == 2
        attr_d = a["edge_attr_64"].rearrange("(p c) f -> p (c f)", p=EP)
        fts_d = rec_ft[0:E].rearrange("(p c) f -> p c f", p=EP)

        def act_attr_load(act, k, t):
            act.dma_start(attr[k][:], attr_d[:, bass.ds(t * (CB * ED), CB * ED)]).then_inc(s(f"attr_in{k}"), 16)
            for n, (c, m) in enumerate(groups):
                act.dma_start(near[k][0:m * HD, n], dist_t[bass.ds(t * CB + c, m)].unsqueeze(1).broadcast_to([m, HD, EP])).then_inc(s(f"near_in{k}"), 16)

        def pe_turn_edges(pe, k):
            pe.wait_ge(s(f"attr_in{k}"), 16)
            pe.sem_inc(s(f"attr_in{k}"), -16)
            for n in range(pairs):
                pe.transpose(ps_a[k][n // 4][:, (n % 4) * EP:(n % 4 + 1) * EP], attr[k][:, n * 2 * ED:(n + 1) * 2 * ED], ident[0:EP, 0:EP])
            pe.transpose(ps_a[k][1][0:ED, EP:2 * EP], attr[k][:, pairs * 2 * ED:], ident[0:EP, 0:EP]).then_inc(s(f"attr_t{k}"), 1)

        def act_copy_turned(act, k):
            act.wait_ge(s(f"near_in{k}"), 32)
            act.sem_inc(s(f"near_in{k}"), -32)
            act.activation(h_t[k][:, 0], near[k][:, 0], ACT.Relu, bias=bd1[:], scale=wd1[:])
            m = groups[1][1] * HD
            act.activation(h_t[k][0:m, 1], near[k][0:m, 1], ACT.Relu, bias=bd1[0:m], scale=wd1[0:m])
            act.wait_ge(s(f"attr_t{k}"), 1)
            act.sem_inc(s(f"attr_t{k}"), -1)
            act.activation(a_t[k][:, 0:4].rearrange("p n e -> p (n e)"), ps_a[k][0][:, 0:4 * EP], ACT.Copy)
            act.activation(a_t[k][:, 4], ps_a[k][1][:, 0:EP], ACT.Copy)
            act.activation(a_t[k][0:ED, 5], ps_a[k][1][0:ED, EP:2 * EP], ACT.Copy).then_inc(s("act_chain"), 1)
            act.wait_ge(s("act_chain"), 1)
            act.sem_inc(s("act_chain"), -1)
            act.sem_inc(s(f"t_copied{k}"), 1)

        def pe_features(pe, k):
            pe.wait_ge(s(f"t_copied{k}"), 1)
            pe.sem_inc(s(f"t_copied{k}"), -1)
            o = ps_f[k].rearrange("p (c f) -> p c f", f=REC)
            pe.matmul(o, ones[0:1, 0:EP], b_ft[:].unsqueeze(1).broadcast_to([1, CB, REC]), start=True, stop=False, skip_group_check=True)
            for n in range(pairs):
                pe.matmul(o[:, 2 * n:2 * n + 2, 0:HEADS], a_t[k][:, n], we2[:].rearrange("p (c h) -> p c h", c=2),
                          start=False, stop=True, skip_group_check=True)
            pe.matmul(o[:, 2 * pairs:, 0:HEADS], a_t[k][0:ED, pairs], we2[0:ED, 0:HEADS].unsqueeze(1),
                      start=False, stop=True, skip_group_check=True)
            for n, (c, m) in enumerate(groups):
                last = pe.matmul(o[:, c:c + m, HEADS:], h_t[k][0:m * HD, n],
                                 wd2[0:m * HD, 0:m * HEADS].rearrange("p (c h) -> p c h", c=m),
                                 start=False, stop=True, skip_group_check=True)
            last.then_inc(s(f"ft_ready{k}"), 1)

        def act_store_features(act, k, t):
            act.wait_ge(s(f"ft_ready{k}"), 1)
            act.sem_inc(s(f"ft_ready{k}"), -1)
            act.wait_ge(s(f"fts_free{k}"), 16)
            act.sem_inc(s(f"fts_free{k}"), -16)
            act.activation(fts[k][:].rearrange("p c f -> p (c f)"), ps_f[k], ACT.Copy).then_inc(s("act_chain"), 1)
            act.wait_ge(s("act_chain"), 1)
            act.sem_inc(s("act_chain"), -1)
            act.dma_start(fts_d[:, bass.ds(t * CB, CB)], fts[k][:]).then_inc(s(f"fts_free{k}"), 16)

        with ExitStack() as mid:
            def eb(name, shape, dt=F32):
                return mid.enter_context(nc.sbuf_tensor(name, shape, dt))

            left = eb("left", [P, 1])
            at_f = eb("at_f", [P, 1])
            at_c = eb("at_c", [P, 1])
            at_i = eb("at_i", [P, 1], I32)
            rec = eb("rec", [P, RUN, 2], I32)
            src_f = eb("src_f", [P, RUN])
            has = eb("has", [P, RUN])
            iota64 = iota_r[:, 0:RUN]
            el_i = eb("el_i", [P, RC, 12], I32)
            el_m = eb("el_m", [P, RC, SLOTS])
            el_t = eb("el_t", [P, RC, 2, HALF])

            with nc.Block() as block:
                @block.gpsimd
                def _(pool):
                    with pool.Fori(0, NB) as b:
                        start, end = block_range(pool, b, rbounds)
                        with pool.Fori(start, end) as r:
                            pool.wait_ge(s("run_ready"), 1)
                            pool.sem_inc(s("run_ready"), -1)
                            pool.indirect_dma_start(rec[:].rearrange("p s w -> p (s w)"), None, rec_id,
                                                    bass.IndirectOffsetOnAxis(ap=at_i[:].bitcast(U32), axis=0)).then_inc(s("run_in"), 16)
                    for b in range(NB):
                        pool.indirect_dma_start(xs[:, b, :], None, a["x"],
                                                bass.IndirectOffsetOnAxis(ap=permx[:, b:b + 1].bitcast(U32), axis=0)).then_inc(s("x_in"), 16)
                    pool.wait_ge(s("x_in"), 16 * NB)

                @block.vector
                def _(dve):
                    ch = Chain(s("dve_chain"))
                    dve.memset(el_i[:], 0).then_inc(s("dve_chain"), 1)
                    dve.wait_ge(s("dve_chain"), 1)
                    dve.sem_inc(s("dve_chain"), -1)
                    with dve.Fori(0, NB) as b:
                        start, end = block_range(dve, b, rbounds)
                        dve.tensor_copy(left[:], info[:, bass.ds(b, 1), 2]).then_inc(ch.semaphore, ch.one())
                        dve.tensor_copy(at_f[:], info[:, bass.ds(b, 1), 1]).then_inc(ch.semaphore, ch.one())
                        dve.wait_ge(ch.semaphore, ch.count)
                        dve.sem_inc(ch.semaphore, -ch.clear())
                        with dve.Fori(start, end) as r:
                            dve.tensor_scalar(at_c[:], at_f[:], float(E), None, ALU.min).then_inc(ch.semaphore, ch.one())
                            dve.wait_ge(ch.semaphore, ch.count)
                            dve.tensor_copy(at_i[:], at_c[:]).then_inc(ch.semaphore, ch.one())
                            dve.tensor_scalar(has[:], iota64, left[:], None, ALU.is_lt).then_inc(ch.semaphore, ch.one())
                            dve.wait_ge(ch.semaphore, ch.count)
                            dve.sem_inc(s("run_ready"), 1)
                            dve.wait_ge(s("el_free"), 1)
                            dve.sem_inc(s("el_free"), -1)
                            dve.tensor_scalar(el_i[:, :, SLOTS], run_at[:], at_c[:], float(E), ALU.add, ALU.min).then_inc(ch.semaphore, ch.one())
                            dve.tensor_scalar(el_m[:].rearrange("p c s -> p (c s)"), has[:], -1.0, BIG, ALU.add, ALU.mult).then_inc(ch.semaphore, ch.one())
                            dve.wait_ge(s("run_in"), 16 * r + 16)
                            dve.tensor_copy(el_t[:].rearrange("p c h s -> p (c h s)"), rec[:, :, 1]).then_inc(ch.semaphore, ch.one())
                            dve.tensor_copy(src_f[:], rec[:, :, 0]).then_inc(ch.semaphore, ch.one())
                            dve.wait_ge(ch.semaphore, ch.count)
                            dve.scalar_tensor_tensor(src_f[:], src_f[:], -float(NPAD - 1), has[:], ALU.add, ALU.mult).then_inc(ch.semaphore, ch.one())
                            dve.wait_ge(ch.semaphore, ch.count)
                            dve.tensor_scalar(el_i[:, :, 0:SLOTS], src_f[:].rearrange("p (c s) -> p c s", s=SLOTS),
                                              float(NPAD - 1), None, ALU.add).then_inc(ch.semaphore, ch.one())
                            dve.tensor_scalar(left[:], left[:], -float(RUN), None, ALU.add).then_inc(ch.semaphore, ch.one())
                            dve.tensor_scalar(at_f[:], at_f[:], float(RUN), None, ALU.add).then_inc(ch.semaphore, ch.one())
                            dve.wait_ge(ch.semaphore, ch.count)
                            dve.sem_inc(s("el_ready"), 1)
                            dve.wait_ge(ch.semaphore, ch.count)
                            dve.sem_inc(ch.semaphore, -ch.clear())
                    dve.wait_ge(s("el_free"), 1)
                    dve.sem_inc(s("el_free"), -1)

                @block.scalar
                def _(act):
                    for n in range(0, EC, P):
                        m = min(P, EC - n)
                        act.wait_ge(s("dist_turned"), 1)
                        act.sem_inc(s("dist_turned"), -1)
                        act.activation(turn[0:m], bank[4][0:m, 0:EP], ACT.Copy).then_inc(s("act_chain"), 1)
                        act.wait_ge(s("act_chain"), 1)
                        act.sem_inc(s("act_chain"), -1)
                        act.sem_inc(s("turn_copied"), 1)
                        act.dma_start(dist_t[n:n + m], turn[0:m]).then_inc(s("turn_stored"), 16)
                        act.wait_ge(s("turn_stored"), 16)
                        act.sem_inc(s("turn_stored"), -16)

                    def step(k, t, ahead=True, load=True):
                        if ahead:
                            act_copy_turned(act, 1 - k)
                        act_store_features(act, k, t)
                        if load:
                            act_attr_load(act, k, t + 2)

                    for k in range(2):
                        act.sem_inc(s(f"fts_free{k}"), 16)
                        act_attr_load(act, k, k)
                    act_copy_turned(act, 0)
                    with act.Fori(0, (FEARLY - 3) // 2) as i:
                        for k in range(2):
                            step(k, 2 * i + k)
                    step(0, FEARLY - 3)
                    step(1, FEARLY - 2, load=False)
                    step(0, FEARLY - 1, ahead=False, load=False)
                    for k in range(2):
                        act.wait_ge(s(f"fts_free{k}"), 16)
                        act.sem_inc(s(f"fts_free{k}"), -16)

                @block.tensor
                def _(pe):
                    for n in range(0, EC, P):
                        m = min(P, EC - n)
                        if n:
                            pe.wait_ge(s("turn_copied"), 1)
                            pe.sem_inc(s("turn_copied"), -1)
                        pe.transpose(bank[4][0:m, 0:EP], dist[:, n:n + m], ident[0:EP, 0:EP]).then_inc(s("dist_turned"), 1)
                    pe.wait_ge(s("turn_copied"), 1)
                    pe.sem_inc(s("turn_copied"), -1)

                    def step(k, ahead=True):
                        if ahead:
                            pe_turn_edges(pe, 1 - k)
                        pe_features(pe, k)

                    pe_turn_edges(pe, 0)
                    with pe.Fori(0, (FEARLY - 1) // 2) as i:
                        for k in range(2):
                            step(k)
                    step(0, ahead=False)

                @block.sync
                def _(sp):
                    sp.sem_inc(s("el_free"), 1)
                    with sp.Fori(0, NB) as b:
                        start, end = block_range(sp, b, bounds, JMAX - RC)
                        with sp.Fori(start, end, RC) as j:
                            sp.wait_ge(s("el_ready"), 1)
                            sp.sem_inc(s("el_ready"), -1)
                            sp.dma_start(el_idx[bass.ds(j, RC)].rearrange("j p s -> p j s"), el_i[:]).then_inc(s("el_stored"), 16)
                            sp.dma_start(el_msk[bass.ds(j, RC)].rearrange("j p s -> p j s"), el_m[:]).then_inc(s("el_stored"), 16)
                            for h in range(2):
                                sp.dma_start(el_typ[bass.ds(j, RC), h].rearrange("j p s -> p j s"), el_t[:, :, h]).then_inc(s("el_stored"), 16)
                            sp.wait_ge(s("el_stored"), 64)
                            sp.sem_inc(s("el_stored"), -64)
                            sp.sem_inc(s("el_free"), 1)

        idx = [sb(f"idx{h}", [P, HALF], I32) for h in range(2)]
        first = sb("first", [P, 2], I32)
        msk = sb("msk", [P, SLOTS])
        typ = sb("typ", [2 * TYPES, P * HALF])
        typ_d = sb("typ_d", [2 * TYPES, P * HALF])
        onehot = sb("onehot", [2 * TYPES, P, HALF])
        feat = sb("feat", [P, SLOTS, REC])
        ft = sb("ft", [P, SLOTS, REC])
        sc = sb("sc", [P, SLOTS + 1, HEADS])
        top = sb("top", [P, HEADS])
        sh = sb("sh", [P, SLOTS + 1, HEADS])
        wt = sb("wt", [P, SLOTS + 1, HEADS])
        sw = sb("sw", [P, SLOTS + 1, HEADS])
        kk = [sb(f"kk{h}", [P, HALF, D]) for h in range(2)]
        work = sb("work", [P, SLOTS + 1, W1])
        prod = sb("prod", [P, SLOTS + 1, HV])
        land0 = [sb(f"land0{h}", [P, HALF, W0]) for h in range(2)]
        land1 = [sb(f"land1{h}", [P, HALF, W1]) for h in range(2)]
        land2 = [sb(f"land2{h}", [P, HALF + 1, D]) for h in range(2)]

        def dve_rsqrt(dve, ch, v, to, t, one_column=True):
            dve.tensor_scalar(to.bitcast(I32), v.bitcast(I32), -0.5, RSQRT_SEED, ALU.mult, ALU.add).then_inc(ch.semaphore, ch.one())
            dve.tensor_scalar(v, v, -0.5, None, ALU.mult).then_inc(ch.semaphore, ch.one())
            dve.wait_ge(ch.semaphore, ch.count)
            for _ in range(4):
                if one_column:
                    dve.tensor_scalar(t, to, to, v, ALU.mult, ALU.mult).then_inc(ch.semaphore, ch.one())
                    dve.wait_ge(ch.semaphore, ch.count)
                else:
                    dve.tensor_tensor(t, to, to, ALU.mult).then_inc(ch.semaphore, ch.one())
                    dve.wait_ge(ch.semaphore, ch.count)
                    dve.tensor_tensor(t, t, v, ALU.mult).then_inc(ch.semaphore, ch.one())
                    dve.wait_ge(ch.semaphore, ch.count)
                dve.scalar_tensor_tensor(to, t, 1.5, to, ALU.add, ALU.mult).then_inc(ch.semaphore, ch.one())
                dve.wait_ge(ch.semaphore, ch.count)

        def dve_layernorm(dve, ch, x, to, relu=True):
            dve.bn_stats(st6[:], x).then_inc(ch.semaphore, ch.one())
            dve.wait_ge(ch.semaphore, ch.count)
            dve.bn_aggr(mv[:], st6[:]).then_inc(ch.semaphore, ch.one())
            dve.wait_ge(ch.semaphore, ch.count)
            dve.tensor_scalar(var[:], mv[:, 1:2], EPS, None, ALU.add).then_inc(ch.semaphore, ch.one())
            dve.wait_ge(ch.semaphore, ch.count)
            dve_rsqrt(dve, ch, var[:], rstd[:], newt[:])
            dve.tensor_scalar(to, x, mv[:, 0:1], rstd[:], ALU.subtract, ALU.mult).then_inc(ch.semaphore, ch.one())
            dve.wait_ge(ch.semaphore, ch.count)
            if relu:
                dve.tensor_scalar(to, to, 0.0, None, ALU.max).then_inc(ch.semaphore, ch.one())
                dve.wait_ge(ch.semaphore, ch.count)

        def pe_project(pe, w, n):
            pe.wait_ge(s("hid_ready"), 1)
            pe.sem_inc(s("hid_ready"), -1)
            pe.transpose(ps_t[:, 0:P], hid[:], ident[:]).then_inc(s("hid_turned"), 1)
            pe.wait_ge(s("hid_t_ready"), 1)
            pe.sem_inc(s("hid_t_ready"), -1)
            pe.matmul(ps_p[:, 0:n], hid_t[:], w, start=True, stop=True).then_inc(s("projected"), 1)

        def dve_project(dve, ch):
            dve.wait_ge(ch.semaphore, ch.count)
            dve.sem_inc(s("hid_ready"), 1)
            dve.wait_ge(s("hid_turned"), 1)
            dve.sem_inc(s("hid_turned"), -1)
            dve.tensor_copy(hid_t[:], ps_t[:, 0:P]).then_inc(ch.semaphore, ch.one())
            dve.wait_ge(ch.semaphore, ch.count)
            dve.sem_inc(s("hid_t_ready"), 1)
            dve.wait_ge(s("projected"), 1)
            dve.sem_inc(s("projected"), -1)

        def dve_table(dve, ch, b, number):
            dve.tensor_copy(stage_i[:], perm[:, bass.ds(b, 1)]).then_inc(ch.semaphore, ch.one())
            dve.wait_ge(ch.semaphore, ch.count)
            dve.sem_inc(s("table_ready"), 1)

        def blk(t, b, c0, c1):
            return t[:, bass.ds(b, 1), c0:c1].rearrange("p o c -> p (o c)")

        def wait_table_stored(dve, stores_before, b):
            dve.wait_ge(s("table_stored"), 16 * (stores_before + b))

        scattered = [0]

        def dve_to_l0(dve, ch, b, wait):
            dve.tensor_scalar(hid[:], blk(xs, b, 0, D), mvs[:, bass.ds(b, 1), 0], rstds[:, bass.ds(b, 1)], ALU.subtract, ALU.mult).then_inc(ch.semaphore, ch.one())
            dve.wait_ge(ch.semaphore, ch.count)
            dve.tensor_scalar(hid[:], hid[:], 0.0, None, ALU.max).then_inc(ch.semaphore, ch.one())
            dve.wait_ge(ch.semaphore, ch.count)
            dve_project(dve, ch)
            wait()
            dve.tensor_tensor(stage0[:, 0:D], ps_p[:, 0:D], b_l0[:, 0:D], ALU.add).then_inc(ch.semaphore, ch.one())
            dve.tensor_tensor(stage0[:, D:].rearrange("p (h v) -> p h v", h=HEADS)[:, :, 0:HD],
                              heads(ps_p[:, D:2 * D]), heads(b_l0[:, D:2 * D]), ALU.add).then_inc(ch.semaphore, ch.one())
            dve.tensor_copy(stage_i[:], perm[:, bass.ds(b, 1)]).then_inc(ch.semaphore, ch.one())
            dve.wait_ge(ch.semaphore, ch.count)
            dve.sem_inc(s("table_ready"), 1)
            dve.tensor_tensor(blk(own0, b, 0, D), ps_p[:, 2 * D:3 * D], b_l0[:, 2 * D:], ALU.add).then_inc(ch.semaphore, ch.one())
            dve.wait_ge(ch.semaphore, ch.count)
            dve.tensor_scalar(blk(own0, b, 0, D), blk(own0, b, 0, D), SCALE, None, ALU.mult).then_inc(ch.semaphore, ch.one())
            dve.wait_ge(ch.semaphore, ch.count)

        def dve_to_conv(dve, ch, b, wait, number):
            dve_project(dve, ch)
            dve.tensor_copy(blk(own1, b, 0, HV).rearrange("p (h v) -> p h v", h=HEADS)[:, :, 0:HD], heads(ps_p[:, 0:D])).then_inc(ch.semaphore, ch.one())
            dve.tensor_copy(blk(own1, b, HV, HV + REC), ps_p[:, D:D + REC]).then_inc(ch.semaphore, ch.one())
            dve.wait_ge(ch.semaphore, ch.count)
            wait()
            dve.tensor_scalar(stage1[:, HV:W1], blk(own1, b, HV, W1), padneg[:, bass.ds(b, 1)], None, ALU.add).then_inc(ch.semaphore, ch.one())
            dve.tensor_copy(stage1[:, 0:HV], blk(own1, b, 0, HV)).then_inc(ch.semaphore, ch.one())
            dve_table(dve, ch, b, number)

        def dve_softmax_mean(dve, ch, state, eps):
            by_head = state.rearrange("p (h v) -> p h v", h=HEADS)
            dve.tensor_scalar(den[:], by_head[:, :, HD], eps, None, ALU.add).then_inc(ch.semaphore, ch.one())
            dve.wait_ge(ch.semaphore, ch.count)
            dve.reciprocal(den[:], den[:]).then_inc(ch.semaphore, ch.one())
            dve.wait_ge(ch.semaphore, ch.count)
            dve.tensor_tensor(heads(tmp[:]), by_head[:, :, 0:HD], den[:].unsqueeze(2).broadcast_to([P, HEADS, HD]), ALU.mult).then_inc(ch.semaphore, ch.one())
            dve.wait_ge(ch.semaphore, ch.count)

        def after_l0(dve, ch, b, wait):
            dve_softmax_mean(dve, ch, work[:, SLOTS, 0:HV], 1e-8)
            dve.tensor_copy(hid[:], tmp[:]).then_inc(ch.semaphore, ch.one())
            dve.wait_ge(ch.semaphore, ch.count)
            dve_project(dve, ch)
            dve.tensor_tensor(tmp[:], ps_p[:, 0:D], bo0[:], ALU.add).then_inc(ch.semaphore, ch.one())
            dve.wait_ge(ch.semaphore, ch.count)
            dve.tensor_tensor(blk(xs, b, 0, D), blk(xs, b, 0, D), tmp[:], ALU.add).then_inc(ch.semaphore, ch.one())
            dve.wait_ge(ch.semaphore, ch.count)
            dve_layernorm(dve, ch, blk(xs, b, 0, D), hid[:])
            dve_to_conv(dve, ch, b, wait, 1)

        def after_conv(n):
            def run(dve, ch, b, wait):
                dve_softmax_mean(dve, ch, work[:, SLOTS, 0:HV], 1e-16)
                if n < 2:
                    dve.tensor_tensor(hid[:], tmp[:], b_g[min(n, 1)][:], ALU.add).then_inc(ch.semaphore, ch.one())
                    dve.wait_ge(ch.semaphore, ch.count)
                    dve_to_conv(dve, ch, b, wait, n + 2)
                    return
                dve.tensor_tensor(tmp[:], tmp[:], b_g[1][:], ALU.add).then_inc(ch.semaphore, ch.one())
                dve.wait_ge(ch.semaphore, ch.count)
                dve.tensor_reduce(col[:, 0:1], tmp[:], AX.X, ALU.max).then_inc(ch.semaphore, ch.one())
                dve.wait_ge(ch.semaphore, ch.count)
                dve.tensor_scalar(tmp[:], tmp[:], col[:, 0:1], None, ALU.subtract).then_inc(ch.semaphore, ch.one())
                dve.wait_ge(ch.semaphore, ch.count)
                dve.sem_inc(s("logits_ready"), 1)
                dve.wait_ge(s("log_sum"), 1)
                dve.sem_inc(s("log_sum"), -1)
                dve.tensor_scalar(tmp[:], tmp[:], col[:, 2:3], None, ALU.subtract).then_inc(ch.semaphore, ch.one())
                dve.wait_ge(ch.semaphore, ch.count)
                dve.tensor_tensor(blk(xs, b, 0, D), blk(xs, b, 0, D), tmp[:], ALU.add).then_inc(ch.semaphore, ch.one())
                dve.wait_ge(ch.semaphore, ch.count)
                dve_layernorm(dve, ch, blk(xs, b, 0, D), hid[:])
                dve.tensor_copy(blk(own2, b, 2 * D, 3 * D), hid[:]).then_inc(ch.semaphore, ch.one())
                dve.wait_ge(ch.semaphore, ch.count)
                dve_project(dve, ch)
                wait()
                dve.tensor_tensor(blk(own2, b, 0, 2 * D), ps_p[:, 0:2 * D], b_l2[:, 0:2 * D], ALU.add).then_inc(ch.semaphore, ch.one())
                dve.tensor_tensor(stage2[:], ps_p[:, 2 * D:3 * D], b_l2[:, 2 * D:], ALU.add).then_inc(ch.semaphore, ch.one())
                dve.wait_ge(ch.semaphore, ch.count)
                dve.tensor_scalar(blk(own2, b, 0, D), blk(own2, b, 0, D), SCALE, None, ALU.mult).then_inc(ch.semaphore, ch.one())
                dve_table(dve, ch, b, 4)
            return run

        def act_after_conv3(act):
            act.wait_ge(s("logits_ready"), 1)
            act.sem_inc(s("logits_ready"), -1)
            act.activation(tmp2[:], tmp[:], ACT.Exp, accum_out=col[:, 1:2]).then_inc(s("act_chain"), 1)
            act.wait_ge(s("act_chain"), 1)
            act.sem_inc(s("act_chain"), -1)
            act.activation(col[:, 2:3], col[:, 1:2], ACT.Ln).then_inc(s("log_sum"), 1)

        def after_l2(dve, ch, b, wait):
            dve.tensor_scalar(den[:], ss[:, SLOTS, :], 1e-30, None, ALU.max).then_inc(ch.semaphore, ch.one())
            dve.wait_ge(ch.semaphore, ch.count)
            dve.reciprocal(den[:], den[:]).then_inc(ch.semaphore, ch.one())
            dve.wait_ge(ch.semaphore, ch.count)
            dve.tensor_tensor(den[:], den[:], ss[:, SLOTS, :], ALU.mult).then_inc(ch.semaphore, ch.one())
            dve.wait_ge(ch.semaphore, ch.count)
            dve.tensor_tensor(heads(hid[:]), heads(blk(own2, b, D, 2 * D)), den[:].unsqueeze(2).broadcast_to([P, HEADS, HD]), ALU.mult).then_inc(ch.semaphore, ch.one())
            dve.wait_ge(ch.semaphore, ch.count)
            dve_project(dve, ch)
            dve.tensor_tensor(tmp[:], ps_p[:, 0:D], bo2[:], ALU.add).then_inc(ch.semaphore, ch.one())
            dve.wait_ge(ch.semaphore, ch.count)
            dve.tensor_tensor(tmp[:], tmp[:], blk(own2, b, 2 * D, 3 * D), ALU.add).then_inc(ch.semaphore, ch.one())
            dve.wait_ge(ch.semaphore, ch.count)
            dve_layernorm(dve, ch, tmp[:], hid[:], relu=False)
            dve.tensor_tensor(tmp[:], hid[:], gam[:], ALU.mult).then_inc(ch.semaphore, ch.one())
            dve.wait_ge(ch.semaphore, ch.count)
            dve.tensor_tensor(tmp[:], tmp[:], bet[:], ALU.add).then_inc(ch.semaphore, ch.one())
            dve.wait_ge(ch.semaphore, ch.count)
            dve.tensor_tensor(blk(xs, b, 0, D), blk(xs, b, 0, D), tmp[:], ALU.add).then_inc(ch.semaphore, ch.one())
            dve.wait_ge(ch.semaphore, ch.count)
            dve_layernorm(dve, ch, blk(xs, b, 0, D), hid[:])
            wait()
            dve.tensor_scalar(stage2[:], hid[:], dis[:, bass.ds(b, 1)], None, ALU.mult).then_inc(ch.semaphore, ch.one())
            dve.wait_ge(ch.semaphore, ch.count)
            dve.tensor_copy(blk(own0, b, 0, D), stage2[:]).then_inc(ch.semaphore, ch.one())
            dve_table(dve, ch, b, 5)

        def after_l3(dve, ch, b, wait):
            dve.tensor_scalar(tmp[:], land2[0][:, HALF, :], dis[:, bass.ds(b, 1)], None, ALU.mult).then_inc(ch.semaphore, ch.one())
            dve.wait_ge(ch.semaphore, ch.count)
            wait()
            dve.tensor_tensor(stage2[:], blk(xs, b, 0, D), tmp[:], ALU.add).then_inc(ch.semaphore, ch.one())
            dve_table(dve, ch, b, 6)

        def slots(ap, n):
            return ap.unsqueeze(1).broadcast_to([P, n, ap.shape[1]])

        S1 = SLOTS + 1
        now = sc[:, 0:SLOTS, :]

        def dve_weights(dve, ch):
            dve.tensor_reduce(top[:], sc[:].rearrange("p s h -> p h s"), AX.X, ALU.max).then_inc(ch.semaphore, ch.one())
            dve.wait_ge(ch.semaphore, ch.count)
            dve.tensor_tensor(sh[:], sc[:], slots(top[:], S1), ALU.subtract).then_inc(ch.semaphore, ch.one())
            dve.wait_ge(ch.semaphore, ch.count)
            dve.sem_inc(s("shifted"), 1)
            dve.wait_ge(s("exped"), 1)
            dve.sem_inc(s("exped"), -1)

        def act_weights(act):
            act.wait_ge(s("shifted"), 1)
            act.sem_inc(s("shifted"), -1)
            act.activation(sc[:, SLOTS, :], top[:], ACT.Copy)
            act.activation(wt[:], sh[:], ACT.Exp).then_inc(s("exped"), 1)

        def dve_weigh(dve, ch):
            dve.tensor_tensor(prod[:].rearrange("p s (h v) -> p s h v", h=HEADS),
                              work[:, :, 0:HV].rearrange("p s (h v) -> p s h v", h=HEADS),
                              wt[:].unsqueeze(3).broadcast_to([P, S1, HEADS, V]), ALU.mult).then_inc(ch.semaphore, ch.one())
            dve.wait_ge(ch.semaphore, ch.count)
            dve.sem_inc(s("work_free"), 1)
            dve.tensor_reduce(work[:, SLOTS, 0:HV], prod[:].rearrange("p s c -> p c s"), AX.X, ALU.add).then_inc(ch.semaphore, ch.one())
            dve.wait_ge(ch.semaphore, ch.count)

        def dve_scores(dve, ch, h, keys, queries):
            dve.tensor_tensor(kk[h][:], keys, slots(queries, HALF), ALU.mult).then_inc(ch.semaphore, ch.one())
            dve.wait_ge(ch.semaphore, ch.count)

        def dve_scores_sum(dve, ch, h):
            dve.tensor_reduce(sc[:, h * HALF:(h + 1) * HALF, :], kk[h][:].rearrange("p s (h d) -> p s h d", h=HEADS), AX.X, ALU.add).then_inc(ch.semaphore, ch.one())
            dve.wait_ge(ch.semaphore, ch.count)

        def dve_mask(dve, ch):
            dve.tensor_tensor(now, now, msk[:].unsqueeze(2).broadcast_to([P, SLOTS, HEADS]), ALU.add).then_inc(ch.semaphore, ch.one())
            dve.wait_ge(ch.semaphore, ch.count)
            dve.sem_inc(s("msk_free"), 1)

        def chunk_l0(dve, ch, b, j, landed):
            for h in range(2):
                dve.wait_ge(s(f"rel_ready{h}"), 1)
                dve.sem_inc(s(f"rel_ready{h}"), -1)
                dve_scores(dve, ch, h, ps_rel[h][:].rearrange("p (s d) -> p s d", d=D), blk(own0, b, 0, D))
                dve.sem_inc(s(f"rel_free{h}"), 1)
                dve_scores_sum(dve, ch, h)
            dve.wait_ge(s("msk_in"), 16)
            dve.sem_inc(s("msk_in"), -16)
            dve_mask(dve, ch)
            dve_weights(dve, ch)
            dve_weigh(dve, ch)

        def chunk_conv(dve, ch, b, j, landed):
            dve.wait_ge(s("copied"), 2)
            dve.sem_inc(s("copied"), -2)
            dve.tensor_tensor(now, work[:, 0:SLOTS, HV:W1], slots(blk(own1, b, W1, W1 + HEADS), SLOTS), ALU.add).then_inc(ch.semaphore, ch.one())
            dve.wait_ge(ch.semaphore, ch.count)
            dve.scalar_tensor_tensor(now, now, 0.2, now, ALU.mult, ALU.max).then_inc(ch.semaphore, ch.one())
            dve.wait_ge(ch.semaphore, ch.count)
            dve_weights(dve, ch)
            dve_weigh(dve, ch)

        def chunk_l2(dve, ch, b, j, landed):
            for h in range(2):
                dve.wait_ge(s("copied"), 1)
                dve.sem_inc(s("copied"), -1)
                dve_scores(dve, ch, h, work[:, h * HALF:(h + 1) * HALF, 0:D], blk(own2, b, 0, D))
                dve_scores_sum(dve, ch, h)
            dve.wait_ge(s("feat_copied"), 1)
            dve.sem_inc(s("feat_copied"), -1)
            dve.wait_ge(s("msk_in"), 16)
            dve.sem_inc(s("msk_in"), -16)
            dve.tensor_tensor(now, now, ft[:, :, 0:HEADS], ALU.add).then_inc(ch.semaphore, ch.one())
            dve.wait_ge(ch.semaphore, ch.count)
            dve.tensor_tensor(now, now, slots(cons[:, bass.ds(b, 1), :].rearrange("p o c -> p (o c)"), SLOTS), ALU.mult).then_inc(ch.semaphore, ch.one())
            dve.wait_ge(ch.semaphore, ch.count)
            dve.tensor_tensor(now, now, ft[:, :, HEADS:], ALU.add).then_inc(ch.semaphore, ch.one())
            dve.wait_ge(ch.semaphore, ch.count)
            dve.sem_inc(s("work_free"), 1)
            dve_mask(dve, ch)
            dve_weights(dve, ch)
            dve.tensor_tensor(sw[:], ss[:], wt[:], ALU.mult).then_inc(ch.semaphore, ch.one())
            dve.wait_ge(ch.semaphore, ch.count)
            dve.tensor_reduce(ss[:, SLOTS, :], sw[:].rearrange("p s h -> p h s"), AX.X, ALU.add).then_inc(ch.semaphore, ch.one())
            dve.wait_ge(ch.semaphore, ch.count)

        def chunk_l3(dve, ch, b, j, landed):
            for h in range(2):
                dve.wait_ge(landed[h], 16 * HALF * (j + 1))
                dve.tensor_reduce(land2[1 - h][:, HALF, :], land2[h][:].rearrange("p s c -> p c s"), AX.X, ALU.add).then_inc(ch.semaphore, ch.one())
                dve.wait_ge(ch.semaphore, ch.count)
                dve.sem_inc(s(f"rows_free{h}"), 1)

        def act_onehot(act):
            act.wait_ge(s("typ_in"), 32)
            act.sem_inc(s("typ_in"), -32)
            act.activation(typ_d[:], typ[:], ACT.Square, bias=neg_p[:]).then_inc(s("act_chain"), 1)
            act.wait_ge(s("act_chain"), 1)
            act.sem_inc(s("act_chain"), -1)
            act.sem_inc(s("typ_free"), 1)
            act.wait_ge(s("onehot_free"), 1)
            act.sem_inc(s("onehot_free"), -1)
            act.activation(onehot[:].rearrange("t p s -> t (p s)"), typ_d[:], ACT.Relu, bias=1.0, scale=-1.0).then_inc(s("act_chain"), 1)
            act.wait_ge(s("act_chain"), 1)
            act.sem_inc(s("act_chain"), -1)
            act.sem_inc(s("onehot_in"), 1)

        def act_copy_l0(act, n, landed):
            act.wait_ge(s("work_free"), 1)
            act.sem_inc(s("work_free"), -1)
            for h in range(2):
                act.wait_ge(landed[h], 16 * HALF * (n + 1))
                act.activation(work[:, h * HALF:(h + 1) * HALF, 0:HV], land0[h][:, :, D:W0], ACT.Copy).then_inc(s(f"rows_free{h}"), 1)

        def act_copy_conv(act, n, landed):
            act.wait_ge(s("work_free"), 1)
            act.sem_inc(s("work_free"), -1)
            for h in range(2):
                act.wait_ge(landed[h], 16 * HALF * (n + 1))
                act.activation(work[:, h * HALF:(h + 1) * HALF, :], land1[h][:], ACT.Copy).then_inc(s("act_chain"), 1)
                act.wait_ge(s("act_chain"), 1)
                act.sem_inc(s("act_chain"), -1)
                act.sem_inc(s(f"rows_free{h}"), 1)
                act.sem_inc(s("copied"), 1)

        def act_copy_l2(act, n, landed):
            act.wait_ge(s("work_free"), 1)
            act.sem_inc(s("work_free"), -1)
            for h in range(2):
                act.wait_ge(landed[h], 16 * HALF * (n + 1))
                act.activation(work[:, h * HALF:(h + 1) * HALF, 0:D], land2[h][:, 0:HALF, :], ACT.Copy).then_inc(s("act_chain"), 1)
                act.wait_ge(s("act_chain"), 1)
                act.sem_inc(s("act_chain"), -1)
                act.sem_inc(s(f"rows_free{h}"), 1)
                act.sem_inc(s("copied"), 1)
            act.wait_ge(s("feat_in"), 16 * n + 16)
            act.activation(ft[:], feat[:], ACT.Copy).then_inc(s("act_chain"), 1)
            act.wait_ge(s("act_chain"), 1)
            act.sem_inc(s("act_chain"), -1)
            act.sem_inc(s("feat_free"), 1)
            act.sem_inc(s("feat_copied"), 1)

        def start_l0(dve, ch, b):
            dve.memset(sc[:, SLOTS, :], 0.0).then_inc(ch.semaphore, ch.one())
            dve.memset(work[:, SLOTS, :], 0.0).then_inc(ch.semaphore, ch.one())
            dve.wait_ge(ch.semaphore, ch.count)

        def start_conv(dve, ch, b):
            m = sc[:, SLOTS, :]
            dve.tensor_copy(work[:, SLOTS, 0:HV], blk(own1, b, 0, HV)).then_inc(ch.semaphore, ch.one())
            dve.tensor_tensor(m, blk(own1, b, HV, W1), blk(own1, b, W1, W1 + HEADS), ALU.add).then_inc(ch.semaphore, ch.one())
            dve.wait_ge(ch.semaphore, ch.count)
            dve.scalar_tensor_tensor(m, m, 0.2, m, ALU.mult, ALU.max).then_inc(ch.semaphore, ch.one())
            dve.wait_ge(ch.semaphore, ch.count)

        def start_l2(dve, ch, b):
            dve.memset(sc[:, SLOTS, :], START).then_inc(ch.semaphore, ch.one())
            dve.memset(ss[:, SLOTS, :], 0.0).then_inc(ch.semaphore, ch.one())
            dve.wait_ge(ch.semaphore, ch.count)

        def start_l3(dve, ch, b):
            dve.tensor_copy(land2[0][:, HALF, :], blk(own0, b, 0, D)).then_inc(ch.semaphore, ch.one())
            dve.wait_ge(ch.semaphore, ch.count)

        def scatter(pool, stage, target, rows=P):
            pool.wait_ge(s("table_ready"), 1)
            pool.sem_inc(s("table_ready"), -1)
            pool.indirect_dma_start(target, bass.IndirectOffsetOnAxis(ap=stage_i[0:rows].bitcast(U32), axis=0),
                                    stage[0:rows], None).then_inc(s("table_stored"), 16)

        with nc.Block() as block:
            @block.gpsimd
            def _(pool):
                with pool.Fori(0, NB) as b:
                    scatter(pool, stage0, table[0])
                pool.wait_ge(s("table_stored"), 16 * NB)

            @block.vector
            def _(dve):
                ch = Chain(s("dve_chain"))
                dve.memset(c_hid[:], 0.0).then_inc(ch.semaphore, ch.one())
                dve.wait_ge(ch.semaphore, ch.count)
                nodes = c_hid[:, 0:NB, :]
                dve.tensor_tensor(nodes, wc1[:].unsqueeze(1).broadcast_to([P, NB, CW]),
                                  info[:, :, 4:5].broadcast_to([P, NB, CW]), ALU.mult).then_inc(ch.semaphore, ch.one())
                dve.wait_ge(ch.semaphore, ch.count)
                dve.tensor_tensor(nodes, nodes, bc1[:].unsqueeze(1).broadcast_to([P, NB, CW]), ALU.add).then_inc(ch.semaphore, ch.one())
                dve.wait_ge(ch.semaphore, ch.count)
                dve.tensor_scalar(nodes, nodes, 0.0, None, ALU.max).then_inc(ch.semaphore, ch.one())
                dve.wait_ge(ch.semaphore, ch.count)
                dve.sem_inc(s("c_hid_ready"), 1)
                for b in range(NB):
                    dve.bn_stats(st6s[:, b, :], xs[:, b, :]).then_inc(ch.semaphore, ch.one())
                dve.wait_ge(ch.semaphore, ch.count)
                for b in range(NB):
                    dve.bn_aggr(mvs[:, b, :], st6s[:, b, :]).then_inc(ch.semaphore, ch.one())
                dve.wait_ge(ch.semaphore, ch.count)
                dve.tensor_scalar(vars_[:], mvs[:, :, 1], EPS, None, ALU.add).then_inc(ch.semaphore, ch.one())
                dve.wait_ge(ch.semaphore, ch.count)
                dve_rsqrt(dve, ch, vars_[:], rstds[:], news[:], one_column=False)
                dve.wait_ge(ch.semaphore, ch.count)
                dve.sem_inc(ch.semaphore, -ch.clear())
                dve.wait_ge(s("c_z_ready"), 1)
                dve.sem_inc(s("c_z_ready"), -1)
                dve.tensor_tensor(c_z[:], bank[4][:, 0:NB * HEADS].rearrange("p (b h) -> p b h", h=HEADS),
                                  bc2[:].unsqueeze(1).broadcast_to([P, NB, HEADS]), ALU.add).then_inc(ch.semaphore, ch.one())
                dve.wait_ge(ch.semaphore, ch.count)
                dve.tensor_scalar(c_pos[:], c_z[:], 0.0, None, ALU.is_ge).then_inc(ch.semaphore, ch.one())
                dve.scalar_tensor_tensor(c_z[:], c_z[:], -1.0, c_z[:], ALU.mult, ALU.max).then_inc(ch.semaphore, ch.one())
                dve.wait_ge(ch.semaphore, ch.count)
                dve.sem_inc(s("c_arg"), 1)
                dve.wait_ge(s("c_exp"), 1)
                dve.sem_inc(s("c_exp"), -1)
                dve.tensor_tensor(c_pos[:], c_pos[:], c_e[:], ALU.max).then_inc(ch.semaphore, ch.one())
                dve.tensor_scalar(c_e[:], c_e[:], 1.0, None, ALU.add).then_inc(ch.semaphore, ch.one())
                dve.wait_ge(ch.semaphore, ch.count)
                dve.reciprocal(c_e[:], c_e[:]).then_inc(ch.semaphore, ch.one())
                dve.wait_ge(ch.semaphore, ch.count)
                dve.tensor_tensor(cons[:], c_e[:], c_pos[:], ALU.mult).then_inc(ch.semaphore, ch.one())
                dve.wait_ge(ch.semaphore, ch.count)
                dve_to_l0(dve, ch, 0, lambda: None)
                dve.wait_ge(ch.semaphore, ch.count)
                dve.sem_inc(ch.semaphore, -ch.clear())
                with dve.Fori(1, NB) as b:
                    dve_to_l0(dve, ch, b, lambda: dve.wait_ge(s("table_stored"), 16 * b))
                    dve.wait_ge(ch.semaphore, ch.count)
                    dve.sem_inc(ch.semaphore, -ch.clear())

            @block.scalar
            def _(act):
                act.wait_ge(s("c_hid_turned"), 1)
                act.sem_inc(s("c_hid_turned"), -1)
                act.activation(c_t[:, 0:4 * P], bank[2][:, 0:4 * P], ACT.Copy)
                act.activation(c_t[:, 4 * P:], bank[3][:, 0:(NG - 4) * P], ACT.Copy).then_inc(s("c_copied"), 1)
                act.wait_ge(s("c_arg"), 1)
                act.sem_inc(s("c_arg"), -1)
                act.activation(c_e[:], c_z[:], ACT.Exp, scale=-1.0).then_inc(s("c_exp"), 1)

            @block.tensor
            def _(pe):
                pe.wait_ge(s("c_hid_ready"), 1)
                pe.sem_inc(s("c_hid_ready"), -1)
                for g in range(NG):
                    last = pe.transpose(bank[2 + g // 4][:, (g % 4) * P:(g % 4 + 1) * P],
                                        c_hid[:, g * CG:(g + 1) * CG, :].rearrange("p b w -> p (b w)"), ident[:])
                last.then_inc(s("c_hid_turned"), 1)
                pe.wait_ge(s("c_copied"), 1)
                pe.sem_inc(s("c_copied"), -1)
                for g in range(NG):
                    last = pe.matmul(bank[4][:, g * CG * HEADS:(g + 1) * CG * HEADS], c_t[:, g * P:(g + 1) * P], wc2[:], start=True, stop=True)
                last.then_inc(s("c_z_ready"), 1)
                with pe.Fori(0, NB) as b:
                    pe_project(pe, w_l0[:], 3 * D)

        def edge_pass(number, rows, source, start, chunk, after, act_copy, act_after, pe_after, stage, target,
                      types=False, mask=False, features=False, copies=False, frees=1,
                      makes_features=None):
            landed = [ctx.enter_context(nc.semaphore(f"rows_in{number}{h}")) for h in range(2)]
            before_this = NB * (number + 1)

            def gathers(pool, b):
                first_chunk, end = block_range(pool, b)
                with pool.Fori(first_chunk, end) as j:
                    for h in range(2):
                        pool.wait_ge(s(f"idx_in{h}"), 16)
                        pool.sem_inc(s(f"idx_in{h}"), -16)
                        pool.wait_ge(s(f"rows_free{h}"), frees)
                        pool.sem_inc(s(f"rows_free{h}"), -frees)
                        for k in range(HALF):
                            pool.indirect_dma_start(rows[h][:, k, :], None, source,
                                                    bass.IndirectOffsetOnAxis(ap=idx[h][:, k:k + 1].bitcast(U32), axis=0)).then_inc(landed[h], 16)
                    if features:
                        pool.wait_ge(s("first_in"), 16)
                        pool.sem_inc(s("first_in"), -16)
                        pool.wait_ge(s("feat_free"), 1)
                        pool.sem_inc(s("feat_free"), -1)
                        pool.indirect_dma_start(feat[:].rearrange("p s f -> p (s f)"), None, rec_ft,
                                                bass.IndirectOffsetOnAxis(ap=first[:, 0:1].bitcast(U32), axis=0)).then_inc(s("feat_in"), 16)

            with nc.Block() as block:
                @block.sync
                def _(sp):
                    if mask:
                        sp.sem_inc(s("msk_free"), 1)
                    if types:
                        sp.sem_inc(s("typ_free"), 1)

                    def loads(j, gathered):
                        def one(t, c0, c1):
                            return t[bass.ds(j, 1), :, c0:c1].rearrange("j p s -> p (j s)")
                        for h in range(2):
                            gathered(landed[h], 16 * HALF)
                            sp.dma_start(idx[h][:], one(el_idx, h * HALF, (h + 1) * HALF)).then_inc(s(f"idx_in{h}"), 16)
                            if features and h == 0:
                                gathered(s("feat_in"), 16)
                                sp.dma_start(first[:], one(el_idx, SLOTS, SLOTS + 2)).then_inc(s("first_in"), 16)
                        if types:
                            sp.wait_ge(s("typ_free"), 1)
                            sp.sem_inc(s("typ_free"), -1)
                            for h in range(2):
                                sp.dma_start(typ[h * TYPES:(h + 1) * TYPES],
                                             el_typ[bass.ds(j, 1), h].rearrange("j p s -> (j p s)").partition_broadcast(TYPES)).then_inc(s("typ_in"), 16)
                        if mask:
                            sp.wait_ge(s("msk_free"), 1)
                            sp.sem_inc(s("msk_free"), -1)
                            sp.dma_start(msk[:], one(el_msk, 0, SLOTS)).then_inc(s("msk_in"), 16)

                    chunks = sp.value_load(bounds[0:1, NB:NB + 1], min_val=2, max_val=JMAX)
                    loads(0, lambda semaphore, each: None)
                    with sp.Fori(1, chunks) as j:
                        loads(j, lambda semaphore, each: sp.wait_ge(semaphore, j * each))
                    if mask:
                        sp.wait_ge(s("msk_free"), 1)
                        sp.sem_inc(s("msk_free"), -1)
                    if types:
                        sp.wait_ge(s("typ_free"), 1)
                        sp.sem_inc(s("typ_free"), -1)

                @block.gpsimd
                def _(pool):
                    gathers(pool, 0)
                    with pool.Fori(1, NB) as b:
                        gathers(pool, b)
                        scatter(pool, stage, target)
                    scatter(pool, stage, target, TAIL if target is out else P)
                    pool.wait_ge(s("table_stored"), 16 * (before_this + NB))

                @block.vector
                def _(dve):
                    ch = Chain(s("dve_chain"))
                    for h in range(2):
                        dve.sem_inc(s(f"rows_free{h}"), frees)
                    if features:
                        dve.sem_inc(s("feat_free"), 1)
                    if copies:
                        dve.sem_inc(s("work_free"), 1)
                    with dve.Fori(0, NB) as b:
                        start(dve, ch, b)
                        dve.wait_ge(ch.semaphore, ch.count)
                        dve.sem_inc(ch.semaphore, -ch.clear())
                        first_chunk, end = block_range(dve, b)
                        with dve.Fori(first_chunk, end) as j:
                            chunk(dve, ch, b, j, landed)
                            dve.wait_ge(ch.semaphore, ch.count)
                            dve.sem_inc(ch.semaphore, -ch.clear())
                        after(dve, ch, b, lambda: dve.wait_ge(s("table_stored"), 16 * (before_this + b)))
                        dve.wait_ge(ch.semaphore, ch.count)
                        dve.sem_inc(ch.semaphore, -ch.clear())
                    for h in range(2):
                        dve.wait_ge(s(f"rows_free{h}"), frees)
                        dve.sem_inc(s(f"rows_free{h}"), -frees)
                    if features:
                        dve.wait_ge(s("feat_free"), 1)
                        dve.sem_inc(s("feat_free"), -1)
                    if copies:
                        dve.wait_ge(s("work_free"), 1)
                        dve.sem_inc(s("work_free"), -1)

                if act_copy:
                    @block.scalar
                    def _(act):
                        def step(j):
                            if types:
                                act_onehot(act)
                            act_weights(act)
                            act_copy(act, j + 1, landed)

                        def features(b, before=True):
                            if before:
                                act_store_features(act, 0, makes_features + b - 1)
                            act_copy_turned(act, 0)

                        if types:
                            act_onehot(act)
                        act_copy(act, 0, landed)
                        if makes_features:
                            act.sem_inc(s("fts_free0"), 16)
                            act_attr_load(act, 0, makes_features)
                            first_chunk, end = block_range(act, 0)
                            with act.Fori(first_chunk, end) as j:
                                step(j)
                            features(0, before=False)
                        with act.Fori(1 if makes_features else 0, NB - 1) as b:
                            if makes_features:
                                act_attr_load(act, 0, makes_features + b)
                            first_chunk, end = block_range(act, b)
                            with act.Fori(first_chunk, end) as j:
                                step(j)
                            if act_after:
                                act_after(act)
                            if makes_features:
                                features(b)
                        if makes_features:
                            act_attr_load(act, 0, makes_features + NB - 1)
                        first_chunk, end = block_range(act, NB - 1)
                        with act.Fori(first_chunk, end - 1) as j:
                            step(j)
                        act_weights(act)
                        if act_after:
                            act_after(act)
                        if makes_features:
                            features(NB - 1)
                            act_store_features(act, 0, makes_features + NB - 1)
                            act.wait_ge(s("fts_free0"), 16)
                            act.sem_inc(s("fts_free0"), -16)

                if pe_after:
                    @block.tensor
                    def _(pe):
                        def make_k(n):
                            pe.wait_ge(s("onehot_in"), 1)
                            pe.sem_inc(s("onehot_in"), -1)
                            for h in range(2):
                                mine = slice(h * TYPES, (h + 1) * TYPES)
                                pe.wait_ge(s(f"rel_free{h}"), 1)
                                pe.sem_inc(s(f"rel_free{h}"), -1)
                                for k in range(HALF):
                                    last = pe.matmul(ps_rel[h][:, k * D:(k + 1) * D], onehot[mine, :, k], rel[mine],
                                                     start=k == 0, stop=False, skip_group_check=True)
                                if h:
                                    last.then_inc(s("onehot_free"), 1)
                                pe.wait_ge(landed[h], 16 * HALF * (n + 1))
                                pe.matmul(ps_rel[h][:].rearrange("p (s d) -> p s d", d=D), ident[:], rows[h][:, :, 0:D],
                                          start=False, stop=True, skip_group_check=True).then_inc(s("pe_chain"), 1)
                                pe.wait_ge(s("pe_chain"), 1)
                                pe.sem_inc(s("pe_chain"), -1)
                                pe.sem_inc(s(f"rel_ready{h}"), 1)
                                pe.sem_inc(s(f"rows_free{h}"), 1)

                        if types:
                            pe.sem_inc(s("onehot_free"), 1)
                            for h in range(2):
                                pe.sem_inc(s(f"rel_free{h}"), 1)
                            make_k(0)
                        with pe.Fori(0, NB - 1) as b:
                            if types:
                                first_chunk, end = block_range(pe, b)
                                with pe.Fori(first_chunk, end) as j:
                                    make_k(j + 1)
                            if makes_features:
                                pe_turn_edges(pe, 0)
                            pe_after(pe)
                            if makes_features:
                                pe_features(pe, 0)
                        if types:
                            first_chunk, end = block_range(pe, NB - 1)
                            with pe.Fori(first_chunk, end - 1) as j:
                                make_k(j + 1)
                        if makes_features:
                            pe_turn_edges(pe, 0)
                        pe_after(pe)
                        if makes_features:
                            pe_features(pe, 0)
                        if types:
                            pe.wait_ge(s("onehot_free"), 1)
                            pe.sem_inc(s("onehot_free"), -1)
                            for h in range(2):
                                pe.wait_ge(s(f"rel_free{h}"), 1)
                                pe.sem_inc(s(f"rel_free{h}"), -1)

        def pe_l0(pe):
            pe_project(pe, wo0[:], D)
            pe_project(pe, w_g[0][:], D + REC)

        def pe_conv(pe):
            pe_project(pe, w_g[1][:], D + REC)

        edge_pass(0, land0, table[0], start_l0, chunk_l0, after_l0, act_copy_l0, None, pe_l0, stage1, table[1],
                  types=True, mask=True, copies=True, frees=2)
        edge_pass(1, land1, table[1], start_conv, chunk_conv, after_conv(0), act_copy_conv, None, pe_conv,
                  stage1, table[2], copies=True, makes_features=FEARLY)
        edge_pass(2, land1, table[2], start_conv, chunk_conv, after_conv(1), act_copy_conv, None, pe_conv,
                  stage1, table[3], copies=True, makes_features=FEARLY + NB)
        edge_pass(3, land1, table[3], start_conv, chunk_conv, after_conv(2), act_copy_conv, act_after_conv3,
                  lambda pe: pe_project(pe, w_l2[:], 3 * D), stage2, table[4], copies=True)
        edge_pass(4, land2, table[4], start_l2, chunk_l2, after_l2, act_copy_l2, None,
                  lambda pe: pe_project(pe, wo2[:], D), stage2, table[5], mask=True, features=True, copies=True)
        edge_pass(5, land2, table[5], start_l3, chunk_l3, after_l3, None, None, None, stage2, out)


INPUTS = ["x", "src", "dst", "edge_attr_64", "edge_type_64", "edge_weight1", "node_vec1"]
INPUTS += ["L0_gnn_" + n for n in "query_embedding relation_embeddings Wq bq Wk bk Wv bv Wo bo".split()]
INPUTS += ["L1_gnn_" + n for n in "W1 a_src1 a_dst1 b1 W2 a_src2 a_dst2 b2".split()]
INPUTS += ["L2_gnn_" + n for n in "Wq bq Wk bk Wv bv We be Wc1 bc1 Wc2 bc2 Wd1 bd1 Wd2 bd2 Wo bo gamma beta".split()]


def kernel(**inputs):
    import numpy as np
    import concourse.bacc as bacc
    from concourse.bass_utils import run_bass_kernel_spmd

    nc = bacc.Bacc("TRN2", target_bir_lowering=False, num_devices=1)
    arrays, args = {}, {}
    for name in INPUTS:
        data = np.ascontiguousarray(inputs[name])
        arrays["in_" + name] = data
        args[name] = nc.dram_tensor("in_" + name, data.shape, mybir.dt.from_np(data.dtype), kind="ExternalInput").ap()
    out = nc.dram_tensor("out_0", args["x"].shape, F32, kind="ExternalOutput").ap()
    program(nc, args, out)
    result = run_bass_kernel_spmd(nc, [arrays], core_ids=[0])
    return result.results[0]["out_0"]
```

```python
from contextlib import ExitStack

import concourse.bass as bass
from concourse import mybir

ALU = mybir.AluOpType
ACT = mybir.ActivationFunctionType
AX = mybir.AxisListType
F32 = mybir.dt.float32
BF16 = mybir.dt.bfloat16
I32 = mybir.dt.int32
U32 = mybir.dt.uint32

P = 128
HEADS = 8
HALF = 4
SLOTS = 2 * HALF
RUN = 64
RC = RUN // SLOTS
EP = 125
BIG = 1e30
START = -1e29
EPS = 1e-5
RSQRT_SEED = 1597463007.0
KEYCAP = 4000
KEYSTEP = 4096


class Chain:

    def __init__(self, semaphore):
        self.semaphore, self.count = semaphore, 0

    def one(self):
        self.count += 1
        return 1

    def clear(self):
        count, self.count = self.count, 0
        return count


def heads(ap):
    return ap.rearrange("p (h d) -> p h d", h=HEADS)


def program(nc, a, out):
    N, D = a["x"].shape
    E = a["src"].shape[0]
    NB = -(-N // P)
    NPAD = NB * P
    TAIL = N - (NB - 1) * P
    EC = E // EP
    assert EP * EC == E and D == P
    HD = D // HEADS
    ED = a["edge_attr_64"].shape[1]
    CH, HB = 5, 3
    DVE_RANKS = 3 * NB // 5
    CB = 11
    FEARLY = EC // CB - 2 * NB
    assert EC % (CH * HB) == 0 and EC % CB == 0 and FEARLY % 2 == 1
    CW = a["L2_gnn_Wc1"].shape[1]
    CG = P // CW
    NG = -(-NB // CG)
    JMAX = E // SLOTS + 2 * NB + 2 * RC
    V = HD + 1
    HV = HEADS * V
    W0 = D + HV
    W1 = HV + HEADS
    REC = 2 * HEADS
    TYPES = a["L0_gnn_relation_embeddings"].shape[0]
    SCALE = 1.0 / HD ** 0.5

    with ExitStack() as ctx:
        def sb(name, shape, dt=F32):
            return ctx.enter_context(nc.sbuf_tensor(name, shape, dt))

        made = {}

        def s(name):
            if name not in made:
                made[name] = ctx.enter_context(nc.semaphore(name))
            return made[name]

        def dram(name, shape, dt=F32):
            return nc.dram_tensor(name, shape, dt, kind="Internal").ap()

        rec_id = dram("rec_id", [E + RUN, 2], I32)
        rec_ft = dram("rec_ft", [E + RUN, REC])
        el_idx = dram("el_idx", [JMAX, P, 12], I32)
        el_msk = dram("el_msk", [JMAX, P, SLOTS])
        el_typ = dram("el_typ", [JMAX, 2, P, HALF])
        dist_t = dram("dist_t", [EC, EP])
        next_at = dram("next_at", [NPAD + P, 1], I32)
        placed = dram("placed", [E, 1], I32)
        ft_placed = dram("ft_placed", [E, REC])
        keyrow = dram("keyrow", [NPAD])
        info_d = dram("info_d", [NPAD, 8])
        table = [dram(f"table{n}", [NPAD, w]) for n, w in enumerate([W0, W1, W1, W1, D, D])]

        ident = sb("ident", [P, P])
        ones = sb("ones", [P, P])
        zerob = sb("zerob", [P, P], BF16)
        zero_i = sb("zero_i", [RUN, REC], I32)
        before = sb("before", [P, P])
        iota_r = sb("iota_r", [P, P])
        iota_p = sb("iota_p", [P, 1])
        neg_p = sb("neg_p", [P, 1])
        run_at = sb("run_at", [P, RC])
        node_id = sb("node_id", [P, NB])
        head_of = sb("head_of", [P, HEADS])

        w_l0 = sb("w_l0", [P, 3 * D])
        b_l0 = sb("b_l0", [P, 3 * D])
        w_bot = sb("w_bot", [P, 2 * D])
        qe = sb("qe", [P, 1])
        rel = sb("rel", [2 * TYPES, D])
        wo0 = sb("wo0", [P, D])
        bo0 = sb("bo0", [P, D])
        w_g = [sb(f"w_g{n}", [P, D + REC]) for n in range(2)]
        a_col = sb("a_col", [P, 4])
        a_blk = sb("a_blk", [P, REC])
        b_g = [sb(f"b_g{n}", [P, D]) for n in range(2)]
        w_l2 = sb("w_l2", [P, 3 * D])
        b_l2 = sb("b_l2", [P, 3 * D])
        wo2 = sb("wo2", [P, D])
        bo2 = sb("bo2", [P, D])
        gam = sb("gam", [P, D])
        bet = sb("bet", [P, D])
        we2 = sb("we2", [P, REC])
        wd2 = sb("wd2", [P, 8 * HEADS])
        wd1 = sb("wd1", [P, 1])
        bd1 = sb("bd1", [P, 1])
        b_ft = sb("b_ft", [1, REC])
        wc1 = sb("wc1", [P, CW])
        bc1 = sb("bc1", [P, CW])
        wc2 = sb("wc2", [P, CG * HEADS])
        bc2 = sb("bc2", [P, HEADS])

        xs = sb("xs", [P, NB, D])
        own0 = sb("own0", [P, NB, D])
        own1 = sb("own1", [P, NB, HV + REC])
        own2 = sb("own2", [P, NB, 3 * D])
        cons = sb("cons", [P, NB, HEADS])
        dist = sb("dist", [EP, EC])
        info = sb("info", [P, NB, 8])
        perm = sb("perm", [P, NB], I32)
        permx = sb("permx", [P, NB], I32)
        dis = sb("dis", [P, NB])
        real = sb("real", [P, NB])
        padneg = sb("padneg", [P, NB])
        bounds = sb("bounds", [1, NB + 1], I32)
        counts = sb("counts", [1, NB], I32)
        rbounds = sb("rbounds", [1, NB + 1], I32)

        unsorted = sb("unsorted", [1, 1], I32)

        mvs = sb("mvs", [P, NB, 2])
        vars_ = sb("vars", [P, NB])
        st6s = sb("st6s", [P, NB, 6])
        c_hid = sb("c_hid", [P, NG * CG, CW])
        c_t = sb("c_t", [P, NG * P])
        c_z = sb("c_z", [P, NB, HEADS])
        c_pos = sb("c_pos", [P, NB, HEADS])
        c_e = sb("c_e", [P, NB, HEADS])
        rstds = sb("rstds", [P, NB])
        news = sb("news", [P, NB])
        st6 = sb("st6", [P, 6])
        mv = sb("mv", [P, 2])
        var = sb("var", [P, 1])
        rstd = sb("rstd", [P, 1])
        newt = sb("newt", [P, 1])
        hid = sb("hid", [P, D])
        hid_t = sb("hid_t", [P, D])
        den = sb("den", [P, HEADS])
        tmp = sb("tmp", [P, D])
        tmp2 = sb("tmp2", [P, D])
        col = sb("col", [P, 4])
        stage0 = sb("stage0", [P, W0])
        stage1 = sb("stage1", [P, W1])
        stage2 = sb("stage2", [P, D])
        stage_i = sb("stage_i", [P, 1], I32)

        ss = sb("ss", [P, SLOTS + 1, HEADS])

        bank = [ctx.enter_context(nc.psum_tensor(f"bank{n}", [P, 512], F32)) for n in range(8)]
        ps_t, ps_p, ps_rel = bank[0], bank[1], bank[2:4]

        with ExitStack() as early:
            def eb(name, shape, dt=F32):
                return early.enter_context(nc.sbuf_tensor(name, shape, dt))

            dst_i = eb("dst_i", [EP, EC], I32)
            rec_i = eb("rec_i", [EP, EC, 2], I32)
            src_i = eb("src_i", [EP, EC], I32)
            typ_i = eb("typ_i", [EP, EC], I32)
            int_t = eb("int_t", [EP, EC], I32)
            dst_f = eb("dst_f", [EP, EC])
            lo = [eb(f"lo{n}", [EP, EC]) for n in range(2)]
            hi = [eb(f"hi{n}", [EP, EC]) for n in range(2)]
            LO = P // 2
            oh_lo = [eb(f"oh_lo{k}", [EP, 2, CH, LO], BF16) for k in range(HB)]
            oh_hi = [eb(f"oh_hi{k}", [EP, 2, CH, 2 * NB], BF16) for k in range(HB)]
            deg = eb("deg", [P, NB])
            tot = eb("tot", [P, NB])
            cum = eb("cum", [P, NB])
            key = eb("key", [P, NB])
            pad_k = eb("pad_k", [P, NB])
            keyall = eb("keyall", [P, NPAD])
            greater = eb("greater", [P, NPAD], BF16)
            signs = eb("signs", [P, NPAD], BF16)
            neg_key = eb("neg_key", [P, NB])
            rank = eb("rank", [P, NB])
            rank_i = eb("rank_i", [P, NB], I32)
            inf = eb("inf", [P, NB, 8])
            w_t = eb("w_t", [P, D])
            blk_max = eb("blk_max", [NB, 2])
            blk_i = eb("blk_i", [NB, 2], I32)
            least = eb("least", [NB, 1])
            bnd_f = eb("bnd_f", [1, 2, NB + 1])
            before_nb = before[0:NB, 0:NB + 1]

            def bc(v, n=P):
                return v.partition_broadcast(n)

            with nc.Block() as block:
                @block.sync
                def _(sp):
                    sp.dma_start(dst_i[:], a["dst"].rearrange("(p c) -> p c", p=EP)).then_inc(s("dst_loaded"), 16)
                    sp.dma_start(src_i[:], a["src"].rearrange("(p c) -> p c", p=EP)).then_inc(s("src_loaded"), 16)
                    sp.dma_start(typ_i[:], a["edge_type_64"].rearrange("(p c) -> p c", p=EP)).then_inc(s("typ_loaded"), 16)
                    n = 0
                    wk, wq = a["L0_gnn_Wk"], a["L0_gnn_Wq"]
                    loads = [
                        (w_l0[:, 0:D], wk[0:D]), (w_l0[:, D:2 * D], a["L0_gnn_Wv"]), (w_l0[:, 2 * D:], wq[0:D]),
                        (w_bot[:, 0:D], wk[D:2 * D]), (w_bot[:, D:], wq[D:2 * D]),
                        (b_l0[:, 0:D], bc(a["L0_gnn_bk"])), (b_l0[:, D:2 * D], bc(a["L0_gnn_bv"])),
                        (b_l0[:, 2 * D:], bc(a["L0_gnn_bq"])),
                        (qe[:], a["L0_gnn_query_embedding"].rearrange("a (p b) -> p (a b)", b=1)),
                        (rel[0:TYPES], a["L0_gnn_relation_embeddings"]), (rel[TYPES:], a["L0_gnn_relation_embeddings"]),
                        (wo0[:], a["L0_gnn_Wo"]), (bo0[:], bc(a["L0_gnn_bo"])),
                        (w_g[0][:, 0:D], a["L1_gnn_W1"]), (w_g[1][:, 0:D], a["L1_gnn_W2"]),
                        (b_g[0][:], bc(a["L1_gnn_b1"])), (b_g[1][:], bc(a["L1_gnn_b2"])),
                        (w_l2[:, 0:D], a["L2_gnn_Wk"]), (w_l2[:, D:2 * D], a["L2_gnn_Wv"]), (w_l2[:, 2 * D:], a["L2_gnn_Wq"]),
                        (b_l2[:, 0:D], bc(a["L2_gnn_bk"])), (b_l2[:, D:2 * D], bc(a["L2_gnn_bv"])),
                        (b_l2[:, 2 * D:], bc(a["L2_gnn_bq"])),
                        (wo2[:], a["L2_gnn_Wo"]), (bo2[:], bc(a["L2_gnn_bo"])),
                        (gam[:], bc(a["L2_gnn_gamma"])), (bet[:], bc(a["L2_gnn_beta"])),
                        (b_ft[:, 0:HEADS], bc(a["L2_gnn_be"], 1)), (b_ft[:, HEADS:], bc(a["L2_gnn_bd2"], 1)),
                        (wc1[:], bc(a["L2_gnn_Wc1"].rearrange("a b -> (a b)"))), (bc1[:], bc(a["L2_gnn_bc1"])),
                        (bc2[:], bc(a["L2_gnn_bc2"])),
                    ]
                    loads += [(wd1[i * HD:(i + 1) * HD], a["L2_gnn_Wd1"].rearrange("a d -> d a")) for i in range(8)]
                    loads += [(dist[:], a["edge_weight1"].rearrange("(p c) o -> p (c o)", p=EP))]
                    loads += [(bd1[i * HD:(i + 1) * HD], a["L2_gnn_bd1"].rearrange("(d o) -> d o", o=1)) for i in range(8)]
                    loads += [(a_col[:, n:n + 1], a[f"L1_gnn_{w}"].rearrange("h (d o) -> (h d) o", o=1))
                              for n, w in enumerate(["a_src1", "a_dst1", "a_src2", "a_dst2"])]
                    for to, of in loads:
                        sp.dma_start(to, of).then_inc(s("weights"), 16)
                        n += 16
                    sp.wait_ge(s("cleared"), 1)
                    for i in range(2):
                        sp.dma_start(we2[i * ED:(i + 1) * ED, i * HEADS:(i + 1) * HEADS], a["L2_gnn_We"]).then_inc(s("weights"), 16)
                        n += 16
                    for i in range(8):
                        sp.dma_start(wd2[i * HD:(i + 1) * HD, i * HEADS:(i + 1) * HEADS], a["L2_gnn_Wd2"]).then_inc(s("weights"), 16)
                        n += 16
                    for i in range(CG):
                        sp.dma_start(wc2[i * CW:(i + 1) * CW, i * HEADS:(i + 1) * HEADS], a["L2_gnn_Wc2"]).then_inc(s("weights"), 16)
                        n += 16
                    nv = a["node_vec1"]
                    with nc.allow_non_contiguous_dma(reason="one word per node"):
                        sp.dma_start(inf[:, 0:NB - 1, 4], nv[0:(NB - 1) * P].rearrange("(b p) o -> p (b o)", p=P)).then_inc(s("weights"), 16)
                        sp.dma_start(inf[0:TAIL, NB - 1:NB, 4], nv[(NB - 1) * P:N]).then_inc(s("weights"), 16)
                    n += 32
                    sp.dma_start(rec_id[E:E + RUN], zero_i[:, 0:2]).then_inc(s("weights"), 16)
                    sp.dma_start(rec_ft[E:E + RUN], zero_i[:].bitcast(F32)).then_inc(s("weights"), 16)
                    n += 32
                    sp.wait_ge(s("rec_ready"), 1)
                    sp.sem_inc(s("rec_ready"), -1)
                    sp.dma_start(rec_id[0:E].rearrange("(p c) w -> p c w", p=EP), rec_i[:]).then_inc(s("weights"), 16)
                    n += 16
                    sp.wait_ge(s("key_ready"), 1)
                    sp.sem_inc(s("key_ready"), -1)
                    with nc.allow_non_contiguous_dma(reason="one word per node"):
                        sp.dma_start(keyrow.rearrange("(b p) -> p b", p=P), key[:]).then_inc(s("key_stored"), 16)
                    sp.wait_ge(s("key_stored"), 16)
                    sp.sem_inc(s("key_stored"), -16)
                    sp.dma_start(keyall[:], bc(keyrow)).then_inc(s("keys"), 16)
                    sp.wait_ge(s("weights"), n)
                    sp.sem_inc(s("weights"), -n)
                    sp.sem_inc(s("weights_in"), 2)
                    sp.wait_ge(s("info_stored"), 16 * NB)
                    sp.dma_start(info[:], info_d.rearrange("(b p) w -> p b w", p=P)).then_inc(s("info_in"), 16)

                @block.gpsimd
                def _(pool):
                    ch = Chain(s("pool_chain"))
                    pool.memset(zerob[:], 0.0).then_inc(ch.semaphore, ch.one())
                    pool.memset(zero_i[:], 0).then_inc(ch.semaphore, ch.one())
                    pool.memset(inf[:], 0.0).then_inc(ch.semaphore, ch.one())
                    pool.memset(we2[:], 0.0).then_inc(ch.semaphore, ch.one())
                    pool.memset(wd2[:], 0.0).then_inc(ch.semaphore, ch.one())
                    pool.memset(wc2[:], 0.0).then_inc(ch.semaphore, ch.one())
                    pool.memset(ones[:], 1.0).then_inc(ch.semaphore, ch.one())
                    pool.memset(before[:], 1.0).then_inc(ch.semaphore, ch.one())
                    pool.memset(head_of[:], 1.0).then_inc(ch.semaphore, ch.one())
                    pool.memset(stage0[:], 1.0).then_inc(ch.semaphore, ch.one())
                    pool.memset(own1[:], 1.0).then_inc(ch.semaphore, ch.one())
                    pool.iota(iota_r[:], [[1, P]], base=0, channel_multiplier=0, allow_small_or_imprecise_dtypes=True).then_inc(ch.semaphore, ch.one())
                    pool.iota(iota_p[:], [[0, 1]], base=0, channel_multiplier=1, allow_small_or_imprecise_dtypes=True).then_inc(ch.semaphore, ch.one())
                    pool.iota(run_at[:], [[SLOTS, RC]], base=0, channel_multiplier=0, allow_small_or_imprecise_dtypes=True).then_inc(ch.semaphore, ch.one())
                    pool.iota(node_id[:], [[P, NB]], base=0, channel_multiplier=1, allow_small_or_imprecise_dtypes=True).then_inc(ch.semaphore, ch.one())
                    pool.memset(ss[:], 1.0).then_inc(ch.semaphore, ch.one())
                    pool.wait_ge(ch.semaphore, ch.count)
                    pool.sem_inc(s("cleared"), 1)
                    pool.affine_select(out=ident[:], in_=ones[:], pattern=[[-1, P]], compare_op=ALU.is_equal,
                                       fill=0.0, base=0, channel_multiplier=1).then_inc(ch.semaphore, ch.one())
                    pool.affine_select(out=before[:], in_=before[:], pattern=[[1, P]], compare_op=ALU.is_gt,
                                       fill=0.0, base=0, channel_multiplier=-1).then_inc(ch.semaphore, ch.one())
                    pool.affine_select(out=head_of[:], in_=head_of[:], pattern=[[-HD, HEADS]], compare_op=ALU.is_ge,
                                       fill=0.0, base=0, channel_multiplier=1).then_inc(ch.semaphore, ch.one())
                    pool.wait_ge(ch.semaphore, ch.count)
                    pool.affine_select(out=head_of[:], in_=head_of[:], pattern=[[HD, HEADS]], compare_op=ALU.is_ge,
                                       fill=0.0, base=HD - 1, channel_multiplier=-1).then_inc(ch.semaphore, ch.one())
                    pool.wait_ge(ch.semaphore, ch.count)
                    pool.sem_inc(s("consts"), 2)
                    pool.wait_ge(ch.semaphore, ch.count)
                    pool.sem_inc(ch.semaphore, -ch.clear())
                    pool.wait_ge(s("rank_ready"), 1)
                    pool.sem_inc(s("rank_ready"), -1)
                    for b in range(NB):
                        pool.indirect_dma_start(info_d, bass.IndirectOffsetOnAxis(ap=rank_i[:, b:b + 1].bitcast(U32), axis=0),
                                                inf[:, b, :], None).then_inc(s("info_stored"), 16)

                @block.vector
                def _(dve):
                    ch = Chain(s("dve_chain"))
                    dve.wait_ge(s("dst_loaded"), 16)
                    dve.sem_inc(s("dst_loaded"), -16)
                    dve.wait_ge(s("consts"), 1)
                    dve.sem_inc(s("consts"), -1)
                    dve.tensor_copy(dst_f[:], dst_i[:]).then_inc(ch.semaphore, ch.one())
                    dve.tensor_scalar(neg_p[0:TYPES], iota_p[0:TYPES], -1.0, None, ALU.mult).then_inc(ch.semaphore, ch.one())
                    dve.tensor_scalar(neg_p[TYPES:], iota_p[TYPES:], -1.0, float(TYPES), ALU.mult, ALU.add).then_inc(ch.semaphore, ch.one())
                    for n, nodes in enumerate([dst_i, src_i]):
                        if n:
                            dve.wait_ge(s("src_loaded"), 16)
                            dve.sem_inc(s("src_loaded"), -16)
                        dve.tensor_scalar(int_t[:], nodes[:], LO - 1, None, ALU.bitwise_and).then_inc(ch.semaphore, ch.one())
                        dve.wait_ge(ch.semaphore, ch.count)
                        dve.tensor_copy(lo[n][:], int_t[:]).then_inc(ch.semaphore, ch.one())
                        dve.wait_ge(ch.semaphore, ch.count)
                        dve.tensor_scalar(int_t[:], nodes[:], LO.bit_length() - 1, None, ALU.logical_shift_right).then_inc(ch.semaphore, ch.one())
                        dve.wait_ge(ch.semaphore, ch.count)
                        dve.tensor_copy(hi[n][:], int_t[:]).then_inc(ch.semaphore, ch.one())
                        dve.wait_ge(ch.semaphore, ch.count)
                    dve.wait_ge(s("typ_loaded"), 16)
                    dve.sem_inc(s("typ_loaded"), -16)
                    dve.tensor_copy(rec_i[:, :, 0], src_i[:]).then_inc(ch.semaphore, ch.one())
                    dve.tensor_copy(rec_i[:, :, 1], typ_i[:]).then_inc(ch.semaphore, ch.one())
                    dve.wait_ge(ch.semaphore, ch.count)
                    dve.sem_inc(s("rec_ready"), 1)
                    dve.wait_ge(ch.semaphore, ch.count)
                    dve.sem_inc(ch.semaphore, -ch.clear())
                    with dve.Fori(0, EC // (CH * HB)) as i:
                        for k in range(HB):
                            c = i * (CH * HB) + k * CH
                            dve.wait_ge(s(f"onehot_free{k}"), 1)
                            dve.sem_inc(s(f"onehot_free{k}"), -1)
                            for n in range(2):
                                dve.tensor_tensor(oh_lo[k][:, n], iota_r[0:EP, 0:LO].unsqueeze(1).broadcast_to([EP, CH, LO]),
                                                  lo[n][:, bass.ds(c, CH)].unsqueeze(2).broadcast_to([EP, CH, LO]),
                                                  ALU.is_equal).then_inc(s(f"onehot_ready{k}"), 1)
                                dve.tensor_tensor(oh_hi[k][:, n], iota_r[0:EP, 0:2 * NB].unsqueeze(1).broadcast_to([EP, CH, 2 * NB]),
                                                  hi[n][:, bass.ds(c, CH)].unsqueeze(2).broadcast_to([EP, CH, 2 * NB]),
                                                  ALU.is_equal).then_inc(s(f"onehot_ready{k}"), 1)
                    dve.wait_ge(s("counted"), 1)
                    dve.sem_inc(s("counted"), -1)
                    for k in range(HB):
                        dve.wait_ge(s(f"onehot_free{k}"), 1)
                        dve.sem_inc(s(f"onehot_free{k}"), -1)
                    dve.tensor_copy(deg[:], bank[4][:, 0:NB]).then_inc(ch.semaphore, ch.one())
                    dve.tensor_copy(inf[:, :, 2], bank[4][:, 0:NB]).then_inc(ch.semaphore, ch.one())
                    dve.tensor_copy(inf[:, :, 3], bank[5][:, 0:NB]).then_inc(ch.semaphore, ch.one())
                    dve.tensor_copy(inf[:, :, 0], node_id[:]).then_inc(ch.semaphore, ch.one())
                    dve.tensor_scalar(pad_k[:], node_id[:], float(N), -float(KEYSTEP), ALU.is_ge, ALU.mult).then_inc(ch.semaphore, ch.one())
                    dve.wait_ge(ch.semaphore, ch.count)
                    dve.sem_inc(s("deg_ready"), 1)
                    dve.tensor_scalar(key[:], deg[:], float(KEYCAP), float(KEYSTEP), ALU.min, ALU.mult).then_inc(ch.semaphore, ch.one())
                    dve.wait_ge(ch.semaphore, ch.count)
                    dve.tensor_tensor(key[:], key[:], pad_k[:], ALU.add).then_inc(ch.semaphore, ch.one())
                    dve.wait_ge(ch.semaphore, ch.count)
                    dve.tensor_tensor(key[:], key[:], node_id[:], ALU.subtract).then_inc(ch.semaphore, ch.one())
                    dve.wait_ge(ch.semaphore, ch.count)
                    dve.tensor_scalar(key[:], key[:], float(NPAD), None, ALU.add).then_inc(ch.semaphore, ch.one())
                    dve.wait_ge(ch.semaphore, ch.count)
                    dve.sem_inc(s("key_ready"), 1)
                    dve.wait_ge(s("sums_ready"), 1)
                    dve.sem_inc(s("sums_ready"), -1)
                    dve.tensor_copy(tot[:], bank[6][:, NB:2 * NB]).then_inc(ch.semaphore, ch.one())
                    dve.wait_ge(ch.semaphore, ch.count)
                    dve.tensor_tensor_scan(cum[:], ones[:, 0:NB], tot[:], 0.0, ALU.mult, ALU.add).then_inc(ch.semaphore, ch.one())
                    dve.wait_ge(ch.semaphore, ch.count)
                    dve.tensor_tensor(cum[:], cum[:], tot[:], ALU.subtract).then_inc(ch.semaphore, ch.one())
                    dve.wait_ge(ch.semaphore, ch.count)
                    dve.tensor_tensor(inf[:, :, 1], cum[:], bank[6][:, 0:NB], ALU.add).then_inc(ch.semaphore, ch.one())
                    dve.wait_ge(ch.semaphore, ch.count)
                    dve.wait_ge(s("keys"), 16)
                    dve.sem_inc(s("keys"), -16)
                    dve.sem_inc(s("keys_in"), 1)
                    dve.wait_ge(ch.semaphore, ch.count)
                    with dve.Fori(0, DVE_RANKS) as b:
                        dve.tensor_scalar(greater[:], keyall[:], key[:, bass.ds(b, 1)], 0.0, ALU.is_gt, ALU.add,
                                          accum_out=rank[:, bass.ds(b, 1)]).then_inc(s("ranked"), 1)
                        dve.wait_ge(s("ranked"), 1)
                        dve.sem_inc(s("ranked"), -1)
                    dve.wait_ge(s("signs_summed"), 1)
                    dve.sem_inc(s("signs_summed"), -1)
                    dve.tensor_scalar(rank[:, DVE_RANKS:], rank[:, DVE_RANKS:], float(NPAD - 1), 0.5, ALU.add, ALU.mult).then_inc(ch.semaphore, ch.one())
                    dve.wait_ge(ch.semaphore, ch.count)
                    dve.tensor_copy(rank_i[:], rank[:]).then_inc(ch.semaphore, ch.one())
                    dve.wait_ge(ch.semaphore, ch.count)
                    dve.wait_ge(s("weights_in"), 2)
                    dve.sem_inc(s("rank_ready"), 1)
                    for n in range(2):
                        if n:
                            dve.wait_ge(s("a_used"), 1)
                            dve.sem_inc(s("a_used"), -1)
                        dve.tensor_scalar(a_blk[:, 0:HEADS], head_of[:], a_col[:, 2 * n:2 * n + 1], None, ALU.mult).then_inc(ch.semaphore, ch.one())
                        dve.tensor_scalar(a_blk[:, HEADS:], head_of[:], a_col[:, 2 * n + 1:2 * n + 2], None, ALU.mult).then_inc(ch.semaphore, ch.one())
                        dve.wait_ge(ch.semaphore, ch.count)
                        dve.sem_inc(s("a_ready"), 1)
                        dve.wait_ge(s("wt_psum"), 1)
                        dve.sem_inc(s("wt_psum"), -1)
                        dve.tensor_copy(w_t[:], bank[0][:, 0:D]).then_inc(s("wt_ready"), 1)
                        dve.wait_ge(s("wa_ready"), 1)
                        dve.sem_inc(s("wa_ready"), -1)
                        dve.tensor_copy(w_g[n][:, D:], bank[1][:, 0:REC]).then_inc(ch.semaphore, ch.one())
                        dve.wait_ge(ch.semaphore, ch.count)
                        dve.sem_inc(s("a_used"), 1)
                    dve.wait_ge(s("a_used"), 1)
                    dve.sem_inc(s("a_used"), -1)
                    dve.wait_ge(s("query_ready"), 1)
                    dve.sem_inc(s("query_ready"), -1)
                    dve.tensor_tensor(b_l0[:, 0:D], b_l0[:, 0:D], bank[7][:, 0:D], ALU.add).then_inc(ch.semaphore, ch.one())
                    dve.tensor_tensor(b_l0[:, 2 * D:], b_l0[:, 2 * D:], bank[7][:, D:2 * D], ALU.add).then_inc(ch.semaphore, ch.one())
                    dve.wait_ge(ch.semaphore, ch.count)
                    dve.wait_ge(s("info_in"), 16)
                    dve.sem_inc(s("info_in"), -16)
                    dve.tensor_copy(perm[:], info[:, :, 0]).then_inc(ch.semaphore, ch.one())
                    dve.tensor_scalar(permx[:], info[:, :, 0], float(N - 1), None, ALU.min).then_inc(ch.semaphore, ch.one())
                    dve.tensor_scalar(real[:], info[:, :, 0], float(N), None, ALU.is_lt).then_inc(ch.semaphore, ch.one())
                    dve.wait_ge(ch.semaphore, ch.count)
                    dve.tensor_scalar(padneg[:], real[:], -1.0, BIG, ALU.add, ALU.mult).then_inc(ch.semaphore, ch.one())
                    dve.tensor_scalar(dis[:], info[:, :, 3], 1.0, None, ALU.add).then_inc(ch.semaphore, ch.one())
                    dve.wait_ge(ch.semaphore, ch.count)
                    dve.tensor_copy(deg[:], info[:, :, 2]).then_inc(ch.semaphore, ch.one())
                    dve.wait_ge(ch.semaphore, ch.count)
                    dve.sem_inc(s("degp_ready"), 1)
                    dve.wait_ge(s("degt_ready"), 1)
                    dve.sem_inc(s("degt_ready"), -1)
                    dve.tensor_reduce(blk_max[:, 0:1], bank[0][0:NB, 0:P], AX.X, ALU.max).then_inc(ch.semaphore, ch.one())
                    dve.wait_ge(ch.semaphore, ch.count)
                    dve.tensor_scalar(blk_max[:, 1:2], blk_max[:, 0:1], float(RUN - 1), None, ALU.add).then_inc(ch.semaphore, ch.one())
                    dve.wait_ge(ch.semaphore, ch.count)
                    dve.tensor_scalar(blk_max[:, 0:1], blk_max[:, 0:1], float(SLOTS - 1), None, ALU.add).then_inc(ch.semaphore, ch.one())
                    dve.wait_ge(ch.semaphore, ch.count)
                    dve.tensor_copy(blk_i[:], blk_max[:]).then_inc(ch.semaphore, ch.one())
                    dve.wait_ge(ch.semaphore, ch.count)
                    dve.tensor_scalar(blk_i[:, 0:1], blk_i[:, 0:1], SLOTS.bit_length() - 1, None, ALU.logical_shift_right).then_inc(ch.semaphore, ch.one())
                    dve.tensor_scalar(blk_i[:, 1:2], blk_i[:, 1:2], RUN.bit_length() - 1, None, ALU.logical_shift_right).then_inc(ch.semaphore, ch.one())
                    dve.wait_ge(ch.semaphore, ch.count)
                    dve.tensor_copy(blk_max[:], blk_i[:]).then_inc(ch.semaphore, ch.one())
                    dve.wait_ge(ch.semaphore, ch.count)
                    dve.tensor_scalar(least[:], iota_p[0:NB], float(NB - 1), 2.0, ALU.is_ge, ALU.add).then_inc(ch.semaphore, ch.one())
                    dve.wait_ge(ch.semaphore, ch.count)
                    dve.tensor_tensor(blk_max[:, 0:1], blk_max[:, 0:1], least[:], ALU.max).then_inc(ch.semaphore, ch.one())
                    dve.tensor_scalar(blk_max[:, 1:2], blk_max[:, 1:2], 1.0, None, ALU.max).then_inc(ch.semaphore, ch.one())
                    dve.wait_ge(ch.semaphore, ch.count)
                    dve.sem_inc(s("blk_ready"), 1)
                    dve.wait_ge(s("bnd_ready"), 1)
                    dve.sem_inc(s("bnd_ready"), -1)
                    dve.tensor_copy(bounds[:], bank[6][0:1, 0:NB + 1]).then_inc(ch.semaphore, ch.one())
                    dve.tensor_copy(bnd_f[:, 0], bank[6][0:1, 0:NB + 1]).then_inc(ch.semaphore, ch.one())
                    dve.tensor_copy(rbounds[:], bank[6][0:1, 32:32 + NB + 1]).then_inc(ch.semaphore, ch.one())
                    dve.wait_ge(ch.semaphore, ch.count)
                    dve.tensor_tensor(counts[:], bnd_f[:, 0, 1:NB + 1], bnd_f[:, 0, 0:NB], ALU.subtract).then_inc(ch.semaphore, ch.one())
                    dve.wait_ge(ch.semaphore, ch.count)
                    dve.sem_inc(s("dis_arg"), 1)
                    dve.wait_ge(s("dis_exp"), 1)
                    dve.sem_inc(s("dis_exp"), -1)
                    dve.tensor_tensor(cum[:], tot[:], tot[:], ALU.mult).then_inc(ch.semaphore, ch.one())
                    dve.wait_ge(ch.semaphore, ch.count)
                    dve.tensor_tensor(cum[:], cum[:], dis[:], ALU.mult).then_inc(ch.semaphore, ch.one())
                    dve.wait_ge(ch.semaphore, ch.count)
                    dve.tensor_scalar(cum[:], cum[:], -0.5, 1.5, ALU.mult, ALU.add).then_inc(ch.semaphore, ch.one())
                    dve.wait_ge(ch.semaphore, ch.count)
                    dve.tensor_tensor(dis[:], tot[:], cum[:], ALU.mult).then_inc(ch.semaphore, ch.one())
                    dve.wait_ge(ch.semaphore, ch.count)
                    dve.tensor_tensor(dis[:], dis[:], real[:], ALU.mult).then_inc(ch.semaphore, ch.one())
                    dve.wait_ge(ch.semaphore, ch.count)
                    dve.sem_inc(ch.semaphore, -ch.clear())

                @block.scalar
                def _(act):
                    act.wait_ge(s("keys_in"), 1)
                    act.sem_inc(s("keys_in"), -1)
                    act.activation(neg_key[:], key[:], ACT.Copy, scale=-1.0).then_inc(s("act_chain"), 1)
                    act.wait_ge(s("act_chain"), 1)
                    act.sem_inc(s("act_chain"), -1)
                    with act.Fori(DVE_RANKS, NB) as b:
                        act.activation(signs[:], keyall[:], ACT.Sign, bias=neg_key[:, bass.ds(b, 1)],
                                       accum_out=rank[:, bass.ds(b, 1)]).then_inc(s("act_chain"), 1)
                        act.wait_ge(s("act_chain"), 1)
                        act.sem_inc(s("act_chain"), -1)
                    act.sem_inc(s("signs_summed"), 1)
                    act.wait_ge(s("dis_arg"), 1)
                    act.sem_inc(s("dis_arg"), -1)
                    act.activation(cum[:], dis[:], ACT.Ln).then_inc(s("act_chain"), 1)
                    act.wait_ge(s("act_chain"), 1)
                    act.sem_inc(s("act_chain"), -1)
                    act.activation(tot[:], cum[:], ACT.Exp, scale=-0.5).then_inc(s("dis_exp"), 1)

                @block.tensor
                def _(pe):
                    for k in range(HB):
                        pe.sem_inc(s(f"onehot_free{k}"), 1)
                    pe.wait_ge(s("consts"), 1)
                    pe.sem_inc(s("consts"), -1)
                    for n in range(2):
                        pe.matmul(bank[4 + n][:, 0:NB], zerob[:], zerob[:, 0:NB], start=True, stop=False, skip_group_check=True)
                    with pe.Fori(0, EC // (CH * HB)) as i:
                        for k in range(HB):
                            pe.wait_ge(s(f"onehot_ready{k}"), 4)
                            pe.sem_inc(s(f"onehot_ready{k}"), -4)
                            for c in range(CH):
                                for n in range(2):
                                    for half in range(2):
                                        last = pe.matmul(bank[4 + n][half * LO:(half + 1) * LO, 0:NB], oh_lo[k][:, n, c],
                                                         oh_hi[k][:, n, c, half::2], start=False, stop=False, skip_group_check=True)
                            last.then_inc(s(f"onehot_free{k}"), 1)
                    for n in range(2):
                        last = pe.matmul(bank[4 + n][:, 0:NB], zerob[:], zerob[:, 0:NB], start=False, stop=True, skip_group_check=True)
                    last.then_inc(s("counted"), 1)
                    pe.wait_ge(s("deg_ready"), 1)
                    pe.sem_inc(s("deg_ready"), -1)
                    pe.matmul(bank[6][:, 0:NB], before[:], deg[:], start=True, stop=True)
                    pe.matmul(bank[6][:, NB:2 * NB], ones[:], deg[:], start=True, stop=True).then_inc(s("sums_ready"), 1)
                    pe.wait_ge(s("weights_in"), 2)
                    for n in range(2):
                        pe.wait_ge(s("a_ready"), 1)
                        pe.sem_inc(s("a_ready"), -1)
                        pe.transpose(bank[0][:, 0:D], w_g[n][:, 0:D], ident[:]).then_inc(s("wt_psum"), 1)
                        pe.wait_ge(s("wt_ready"), 1)
                        pe.sem_inc(s("wt_ready"), -1)
                        pe.matmul(bank[1][:, 0:REC], w_t[:], a_blk[:], start=True, stop=True).then_inc(s("wa_ready"), 1)
                    pe.matmul(bank[7][:, 0:2 * D], qe[:].broadcast_to([P, P]), w_bot[:], start=True, stop=True).then_inc(s("query_ready"), 1)
                    pe.wait_ge(s("degp_ready"), 1)
                    pe.sem_inc(s("degp_ready"), -1)
                    pe.transpose(bank[0][0:NB, 0:P], deg[:], ident[:]).then_inc(s("degt_ready"), 1)
                    pe.wait_ge(s("blk_ready"), 1)
                    pe.sem_inc(s("blk_ready"), -1)
                    pe.matmul(bank[6][0:1, 0:NB + 1], blk_max[:, 0:1], before_nb, start=True, stop=True)
                    pe.matmul(bank[6][0:1, 32:32 + NB + 1], blk_max[:, 1:2], before_nb, start=True, stop=True).then_inc(s("bnd_ready"), 1)

            falls = eb("falls", [EP, EC - 1])
            fall_n = eb("fall_n", [EP, 2])
            ends = eb("ends", [1, 2, EP])
            here = eb("here", [EP, 1])
            here_i = eb("here_i", [EP, 1], I32)
            same = eb("same", [EP, EP])
            same_later = eb("same_later", [EP, EP])
            n_same = eb("n_same", [EP, 2])
            next_place = eb("next_place", [EP, 1], I32)
            place = eb("place", [EP, 1])
            place_i = eb("place_i", [EP, 1], I32)
            places = eb("places", [EP, EC], I32)
            next_i = eb("next_i", [EP, 1], I32)
            to_f = eb("to_f", [EP, 2])
            to_i = eb("to_i", [EP, 1], I32)
            spare = eb("spare", [EP, 1])
            rec_c = eb("rec_c", [EP, 2], I32)
            start_i = eb("start_i", [P, NB], I32)

            def is_unsorted(engine):
                return engine.value_load(unsorted[:], min_val=0, max_val=1) > 0

            with nc.Block() as block:
                @block.vector
                def _(dve):
                    ch = Chain(s("dve_chain"))
                    dve.wait_ge(s("ends_ready"), 1)
                    dve.sem_inc(s("ends_ready"), -1)
                    dve.tensor_copy(ends[:].rearrange("o t e -> o (t e)"), bank[0][0:1, 0:2 * EP]).then_inc(ch.semaphore, ch.one())
                    dve.wait_ge(ch.semaphore, ch.count)
                    dve.tensor_tensor(falls[:], dst_f[:, 0:EC - 1], dst_f[:, 1:EC], ALU.is_gt).then_inc(ch.semaphore, ch.one())
                    dve.wait_ge(ch.semaphore, ch.count)
                    dve.tensor_tensor(ends[:, 1, 0:EP - 1], ends[:, 1, 0:EP - 1], ends[:, 0, 1:EP], ALU.is_gt).then_inc(ch.semaphore, ch.one())
                    dve.wait_ge(ch.semaphore, ch.count)
                    dve.tensor_reduce(fall_n[:, 0:1], falls[:], AX.X, ALU.add).then_inc(ch.semaphore, ch.one())
                    dve.wait_ge(ch.semaphore, ch.count)
                    dve.tensor_reduce(fall_n[0:1, 1:2], ends[:, 1, 0:EP - 1], AX.X, ALU.add).then_inc(ch.semaphore, ch.one())
                    dve.wait_ge(ch.semaphore, ch.count)
                    dve.tensor_tensor(fall_n[0:1, 0:1], fall_n[0:1, 0:1], fall_n[0:1, 1:2], ALU.add).then_inc(ch.semaphore, ch.one())
                    dve.wait_ge(ch.semaphore, ch.count)
                    dve.sem_inc(s("falls_ready"), 1)
                    dve.wait_ge(s("falls_summed"), 1)
                    dve.sem_inc(s("falls_summed"), -1)
                    dve.tensor_scalar(unsorted[:], bank[1][0:1, 0:1], 1.0, None, ALU.min).then_inc(ch.semaphore, ch.one())
                    dve.wait_ge(ch.semaphore, ch.count)
                    dve.sem_inc(ch.semaphore, -ch.clear())
                    for reader in ["pe", "pool", "sp"]:
                        dve.sem_inc(s(f"order_known_{reader}"), 1)
                    with dve.If(is_unsorted(dve)):
                        dve.tensor_scalar(spare[:], iota_p[0:EP], float(NPAD), None, ALU.add).then_inc(ch.semaphore, ch.one())
                        dve.tensor_copy(start_i[:], inf[:, :, 1]).then_inc(ch.semaphore, ch.one())
                        dve.wait_ge(ch.semaphore, ch.count)
                        dve.sem_inc(ch.semaphore, -ch.clear())
                        dve.sem_inc(s("starts_ready"), 1)
                        with dve.Fori(0, EC) as c:
                            dve.tensor_copy(here[:], dst_f[:, bass.ds(c, 1)]).then_inc(ch.semaphore, ch.one())
                            dve.tensor_copy(here_i[:], dst_f[:, bass.ds(c, 1)]).then_inc(ch.semaphore, ch.one())
                            dve.tensor_copy(rec_c[:], rec_i[:, bass.ds(c, 1), :].rearrange("p o w -> p (o w)")).then_inc(ch.semaphore, ch.one())
                            dve.wait_ge(ch.semaphore, ch.count)
                            dve.sem_inc(s("column_ready"), 1)
                            dve.sem_inc(s("here_ready"), 1)
                            dve.wait_ge(s("here_spread"), 1)
                            dve.sem_inc(s("here_spread"), -1)
                            dve.tensor_scalar(same[:], bank[0][0:EP, 0:EP], here[:], None, ALU.is_equal).then_inc(ch.semaphore, ch.one())
                            dve.wait_ge(ch.semaphore, ch.count)
                            dve.tensor_tensor(same_later[:], same[:], before[0:EP, 0:EP], ALU.mult).then_inc(ch.semaphore, ch.one())
                            dve.wait_ge(ch.semaphore, ch.count)
                            dve.tensor_reduce(n_same[:, 0:1], same[:], AX.X, ALU.add).then_inc(ch.semaphore, ch.one())
                            dve.tensor_reduce(n_same[:, 1:2], same_later[:], AX.X, ALU.add).then_inc(ch.semaphore, ch.one())
                            dve.wait_ge(ch.semaphore, ch.count)
                            dve.wait_ge(s("at_in"), 16 * c + 16)
                            dve.tensor_copy(place[:], next_place[:]).then_inc(ch.semaphore, ch.one())
                            dve.wait_ge(ch.semaphore, ch.count)
                            dve.tensor_tensor(place[:], place[:], n_same[:, 0:1], ALU.add).then_inc(ch.semaphore, ch.one())
                            dve.wait_ge(ch.semaphore, ch.count)
                            dve.tensor_tensor(place[:], place[:], n_same[:, 1:2], ALU.subtract).then_inc(ch.semaphore, ch.one())
                            dve.wait_ge(ch.semaphore, ch.count)
                            dve.tensor_copy(next_i[:], place[:]).then_inc(ch.semaphore, ch.one())
                            dve.tensor_scalar(place_i[:], place[:], -1.0, None, ALU.add).then_inc(ch.semaphore, ch.one())
                            dve.tensor_scalar(places[:, bass.ds(c, 1)], place[:], -1.0, None, ALU.add).then_inc(ch.semaphore, ch.one())
                            dve.tensor_scalar(to_f[:, 0:1], n_same[:, 1:2], 0.0, None, ALU.is_gt).then_inc(ch.semaphore, ch.one())
                            dve.scalar_tensor_tensor(to_f[:, 1:2], here[:], -1.0, spare[:], ALU.mult, ALU.add).then_inc(ch.semaphore, ch.one())
                            dve.wait_ge(ch.semaphore, ch.count)
                            dve.tensor_tensor(to_f[:, 0:1], to_f[:, 0:1], to_f[:, 1:2], ALU.mult).then_inc(ch.semaphore, ch.one())
                            dve.wait_ge(ch.semaphore, ch.count)
                            dve.tensor_tensor(to_i[:], to_f[:, 0:1], here[:], ALU.add).then_inc(ch.semaphore, ch.one())
                            dve.wait_ge(ch.semaphore, ch.count)
                            dve.sem_inc(ch.semaphore, -ch.clear())
                            dve.sem_inc(s("place_ready"), 1)
                            dve.wait_ge(s("column_stored"), 1)
                            dve.sem_inc(s("column_stored"), -1)
                        dve.sem_inc(s("places_ready"), 1)

                @block.tensor
                def _(pe):
                    pe.matmul(bank[0][0:1, 0:EP], dst_f[:, 0:1], ident[0:EP, 0:EP], start=True, stop=True)
                    pe.matmul(bank[0][0:1, EP:2 * EP], dst_f[:, EC - 1:EC], ident[0:EP, 0:EP], start=True, stop=True).then_inc(s("ends_ready"), 1)
                    pe.wait_ge(s("falls_ready"), 1)
                    pe.sem_inc(s("falls_ready"), -1)
                    pe.matmul(bank[1][0:1, 0:1], ones[0:EP, 0:1], fall_n[:, 0:1], start=True, stop=True).then_inc(s("falls_summed"), 1)
                    pe.wait_ge(s("order_known_pe"), 1)
                    pe.sem_inc(s("order_known_pe"), -1)
                    with pe.If(is_unsorted(pe)):
                        with pe.Fori(0, EC):
                            pe.wait_ge(s("here_ready"), 1)
                            pe.sem_inc(s("here_ready"), -1)
                            pe.matmul(bank[0][0:EP, 0:EP], here[:].broadcast_to([EP, EP]), ident[0:EP, 0:EP], start=True, stop=True).then_inc(s("here_spread"), 1)

                @block.gpsimd
                def _(pool):
                    pool.wait_ge(s("order_known_pool"), 1)
                    pool.sem_inc(s("order_known_pool"), -1)
                    with pool.If(is_unsorted(pool)):
                        pool.wait_ge(s("starts_stored"), 16)
                        pool.sem_inc(s("starts_stored"), -16)
                        with pool.Fori(0, EC) as c:
                            pool.wait_ge(s("column_ready"), 1)
                            pool.sem_inc(s("column_ready"), -1)
                            pool.indirect_dma_start(next_place[:], None, next_at,
                                                    bass.IndirectOffsetOnAxis(ap=here_i[:].bitcast(U32), axis=0)).then_inc(s("at_in"), 16)
                            pool.wait_ge(s("place_ready"), 1)
                            pool.sem_inc(s("place_ready"), -1)
                            pool.indirect_dma_start(rec_id, bass.IndirectOffsetOnAxis(ap=place_i[:].bitcast(U32), axis=0),
                                                    rec_c[:], None).then_inc(s("placed_in"), 16)
                            pool.indirect_dma_start(next_at, bass.IndirectOffsetOnAxis(ap=to_i[:].bitcast(U32), axis=0),
                                                    next_i[:], None).then_inc(s("placed_in"), 16)
                            pool.wait_ge(s("placed_in"), 32 * c + 32)
                            pool.sem_inc(s("column_stored"), 1)

                @block.sync
                def _(sp):
                    sp.wait_ge(s("order_known_sp"), 1)
                    sp.sem_inc(s("order_known_sp"), -1)
                    with sp.If(is_unsorted(sp)):
                        sp.wait_ge(s("starts_ready"), 1)
                        sp.sem_inc(s("starts_ready"), -1)
                        with nc.allow_non_contiguous_dma(reason="one word per node"):
                            sp.dma_start(next_at[0:NPAD].rearrange("(b p) o -> p (b o)", p=P), start_i[:]).then_inc(s("starts_stored"), 16)
                        sp.wait_ge(s("places_ready"), 1)
                        sp.sem_inc(s("places_ready"), -1)
                        sp.dma_start(placed.rearrange("(p c) o -> p (c o)", p=EP), places[:]).then_inc(s("places_stored"), 16)
                        sp.wait_ge(s("places_stored"), 16)
                        sp.sem_inc(s("places_stored"), -16)

        def block_range(engine, b, table=bounds, most=JMAX):
            return (engine.value_load(table[0:1, bass.ds(b, 1)], min_val=0, max_val=most),
                    engine.value_load(table[0:1, bass.ds(b + 1, 1)], min_val=1, max_val=most))

        attr = [sb(f"attr{k}", [EP, CB * ED]) for k in range(2)]
        near = [sb(f"near{k}", [P, 2, EP]) for k in range(2)]
        turn = sb("turn", [P, EP])
        a_t = [sb(f"a_t{k}", [P, 6, EP]) for k in range(2)]
        h_t = [sb(f"h_t{k}", [P, 2, EP]) for k in range(2)]
        fts = [sb(f"fts{k}", [EP, CB, REC]) for k in range(2)]
        ps_a = [bank[2:4], bank[6:8]]
        ps_f = [bank[4 + k][0:EP, 0:CB * REC] for k in range(2)]
        pairs = CB // 2
        groups = [(g, min(8, CB - g)) for g in range(0, CB, 8)]
        assert pairs == 5 and CB % 2 == 1 and len(groups) == 2
        attr_d = a["edge_attr_64"].rearrange("(p c) f -> p (c f)", p=EP)
        fts_d = rec_ft[0:E].rearrange("(p c) f -> p c f", p=EP)

        def act_attr_load(act, k, t):
            act.dma_start(attr[k][:], attr_d[:, bass.ds(t * (CB * ED), CB * ED)]).then_inc(s(f"attr_in{k}"), 16)
            for n, (c, m) in enumerate(groups):
                act.dma_start(near[k][0:m * HD, n], dist_t[bass.ds(t * CB + c, m)].unsqueeze(1).broadcast_to([m, HD, EP])).then_inc(s(f"near_in{k}"), 16)

        def pe_turn_edges(pe, k):
            pe.wait_ge(s(f"attr_in{k}"), 16)
            pe.sem_inc(s(f"attr_in{k}"), -16)
            for n in range(pairs):
                pe.transpose(ps_a[k][n // 4][:, (n % 4) * EP:(n % 4 + 1) * EP], attr[k][:, n * 2 * ED:(n + 1) * 2 * ED], ident[0:EP, 0:EP])
            pe.transpose(ps_a[k][1][0:ED, EP:2 * EP], attr[k][:, pairs * 2 * ED:], ident[0:EP, 0:EP]).then_inc(s(f"attr_t{k}"), 1)

        def act_copy_turned(act, k):
            act.wait_ge(s(f"near_in{k}"), 32)
            act.sem_inc(s(f"near_in{k}"), -32)
            act.activation(h_t[k][:, 0], near[k][:, 0], ACT.Relu, bias=bd1[:], scale=wd1[:])
            m = groups[1][1] * HD
            act.activation(h_t[k][0:m, 1], near[k][0:m, 1], ACT.Relu, bias=bd1[0:m], scale=wd1[0:m])
            act.wait_ge(s(f"attr_t{k}"), 1)
            act.sem_inc(s(f"attr_t{k}"), -1)
            act.activation(a_t[k][:, 0:4].rearrange("p n e -> p (n e)"), ps_a[k][0][:, 0:4 * EP], ACT.Copy)
            act.activation(a_t[k][:, 4], ps_a[k][1][:, 0:EP], ACT.Copy)
            act.activation(a_t[k][0:ED, 5], ps_a[k][1][0:ED, EP:2 * EP], ACT.Copy).then_inc(s("act_chain"), 1)
            act.wait_ge(s("act_chain"), 1)
            act.sem_inc(s("act_chain"), -1)
            act.sem_inc(s(f"t_copied{k}"), 1)

        def pe_features(pe, k):
            pe.wait_ge(s(f"t_copied{k}"), 1)
            pe.sem_inc(s(f"t_copied{k}"), -1)
            o = ps_f[k].rearrange("p (c f) -> p c f", f=REC)
            pe.matmul(o, ones[0:1, 0:EP], b_ft[:].unsqueeze(1).broadcast_to([1, CB, REC]), start=True, stop=False, skip_group_check=True)
            for n in range(pairs):
                pe.matmul(o[:, 2 * n:2 * n + 2, 0:HEADS], a_t[k][:, n], we2[:].rearrange("p (c h) -> p c h", c=2),
                          start=False, stop=True, skip_group_check=True)
            pe.matmul(o[:, 2 * pairs:, 0:HEADS], a_t[k][0:ED, pairs], we2[0:ED, 0:HEADS].unsqueeze(1),
                      start=False, stop=True, skip_group_check=True)
            for n, (c, m) in enumerate(groups):
                last = pe.matmul(o[:, c:c + m, HEADS:], h_t[k][0:m * HD, n],
                                 wd2[0:m * HD, 0:m * HEADS].rearrange("p (c h) -> p c h", c=m),
                                 start=False, stop=True, skip_group_check=True)
            last.then_inc(s(f"ft_ready{k}"), 1)

        def act_store_features(act, k, t):
            act.wait_ge(s(f"ft_ready{k}"), 1)
            act.sem_inc(s(f"ft_ready{k}"), -1)
            act.wait_ge(s(f"fts_free{k}"), 16)
            act.sem_inc(s(f"fts_free{k}"), -16)
            act.activation(fts[k][:].rearrange("p c f -> p (c f)"), ps_f[k], ACT.Copy).then_inc(s("act_chain"), 1)
            act.wait_ge(s("act_chain"), 1)
            act.sem_inc(s("act_chain"), -1)
            act.dma_start(fts_d[:, bass.ds(t * CB, CB)], fts[k][:]).then_inc(s(f"fts_free{k}"), 16)

        with ExitStack() as mid:
            def eb(name, shape, dt=F32):
                return mid.enter_context(nc.sbuf_tensor(name, shape, dt))

            left = eb("left", [P, 1])
            at_f = eb("at_f", [P, 1])
            at_c = eb("at_c", [P, 1])
            at_i = eb("at_i", [P, 1], I32)
            rec = eb("rec", [P, RUN, 2], I32)
            src_f = eb("src_f", [P, RUN])
            typ_f = eb("typ_f", [P, RUN])
            has = eb("has", [P, RUN])
            iota64 = iota_r[:, 0:RUN]
            el_i = eb("el_i", [P, RC, 12], I32)
            el_m = eb("el_m", [P, RC, SLOTS])
            el_t = eb("el_t", [P, RC, 2, HALF])

            with nc.Block() as block:
                @block.gpsimd
                def _(pool):
                    with pool.Fori(0, NB) as b:
                        start, end = block_range(pool, b, rbounds)
                        with pool.Fori(start, end) as r:
                            pool.wait_ge(s("run_ready"), 1)
                            pool.sem_inc(s("run_ready"), -1)
                            pool.indirect_dma_start(rec[:].rearrange("p s w -> p (s w)"), None, rec_id,
                                                    bass.IndirectOffsetOnAxis(ap=at_i[:].bitcast(U32), axis=0)).then_inc(s("run_in"), 16)
                    for b in range(NB):
                        pool.indirect_dma_start(xs[:, b, :], None, a["x"],
                                                bass.IndirectOffsetOnAxis(ap=permx[:, b:b + 1].bitcast(U32), axis=0)).then_inc(s("x_in"), 16)
                    pool.wait_ge(s("x_in"), 16 * NB)

                @block.vector
                def _(dve):
                    ch = Chain(s("dve_chain"))
                    dve.memset(el_i[:], 0).then_inc(s("dve_chain"), 1)
                    dve.wait_ge(s("dve_chain"), 1)
                    dve.sem_inc(s("dve_chain"), -1)
                    with dve.Fori(0, NB) as b:
                        start, end = block_range(dve, b, rbounds)
                        dve.tensor_copy(left[:], info[:, bass.ds(b, 1), 2]).then_inc(ch.semaphore, ch.one())
                        dve.tensor_copy(at_f[:], info[:, bass.ds(b, 1), 1]).then_inc(ch.semaphore, ch.one())
                        dve.wait_ge(ch.semaphore, ch.count)
                        dve.sem_inc(ch.semaphore, -ch.clear())
                        with dve.Fori(start, end) as r:
                            dve.tensor_scalar(at_c[:], at_f[:], float(E), None, ALU.min).then_inc(ch.semaphore, ch.one())
                            dve.wait_ge(ch.semaphore, ch.count)
                            dve.tensor_copy(at_i[:], at_c[:]).then_inc(ch.semaphore, ch.one())
                            dve.tensor_scalar(has[:], iota64, left[:], None, ALU.is_lt).then_inc(ch.semaphore, ch.one())
                            dve.wait_ge(ch.semaphore, ch.count)
                            dve.sem_inc(s("run_ready"), 1)
                            dve.wait_ge(s("el_free"), 1)
                            dve.sem_inc(s("el_free"), -1)
                            dve.tensor_scalar(el_i[:, :, SLOTS], run_at[:], at_c[:], float(E), ALU.add, ALU.min).then_inc(ch.semaphore, ch.one())
                            dve.tensor_scalar(el_m[:].rearrange("p c s -> p (c s)"), has[:], -1.0, BIG, ALU.add, ALU.mult).then_inc(ch.semaphore, ch.one())
                            dve.wait_ge(s("run_in"), 16 * r + 16)
                            dve.tensor_scalar(typ_f[:], rec[:, :, 1], 1.0, None, ALU.add).then_inc(ch.semaphore, ch.one())
                            dve.tensor_copy(src_f[:], rec[:, :, 0]).then_inc(ch.semaphore, ch.one())
                            dve.wait_ge(ch.semaphore, ch.count)
                            dve.tensor_tensor(typ_f[:], typ_f[:], has[:], ALU.mult).then_inc(ch.semaphore, ch.one())
                            dve.scalar_tensor_tensor(src_f[:], src_f[:], -float(NPAD - 1), has[:], ALU.add, ALU.mult).then_inc(ch.semaphore, ch.one())
                            dve.wait_ge(ch.semaphore, ch.count)
                            dve.tensor_scalar(el_i[:, :, 0:SLOTS], src_f[:].rearrange("p (c s) -> p c s", s=SLOTS),
                                              float(NPAD - 1), None, ALU.add).then_inc(ch.semaphore, ch.one())
                            dve.tensor_scalar(el_t[:].rearrange("p c h s -> p (c h s)"), typ_f[:], -1.0, None, ALU.add).then_inc(ch.semaphore, ch.one())
                            dve.tensor_scalar(left[:], left[:], -float(RUN), None, ALU.add).then_inc(ch.semaphore, ch.one())
                            dve.tensor_scalar(at_f[:], at_f[:], float(RUN), None, ALU.add).then_inc(ch.semaphore, ch.one())
                            dve.wait_ge(ch.semaphore, ch.count)
                            dve.sem_inc(s("el_ready"), 1)
                            dve.wait_ge(ch.semaphore, ch.count)
                            dve.sem_inc(ch.semaphore, -ch.clear())
                    dve.wait_ge(s("el_free"), 1)
                    dve.sem_inc(s("el_free"), -1)

                @block.scalar
                def _(act):
                    for n in range(0, EC, P):
                        m = min(P, EC - n)
                        act.wait_ge(s("dist_turned"), 1)
                        act.sem_inc(s("dist_turned"), -1)
                        act.activation(turn[0:m], bank[4][0:m, 0:EP], ACT.Copy).then_inc(s("act_chain"), 1)
                        act.wait_ge(s("act_chain"), 1)
                        act.sem_inc(s("act_chain"), -1)
                        act.sem_inc(s("turn_copied"), 1)
                        act.dma_start(dist_t[n:n + m], turn[0:m]).then_inc(s("turn_stored"), 16)
                        act.wait_ge(s("turn_stored"), 16)
                        act.sem_inc(s("turn_stored"), -16)

                    def step(k, t, ahead=True, load=True):
                        if ahead:
                            act_copy_turned(act, 1 - k)
                        if load:
                            act_attr_load(act, 1 - k, t + 3)
                        act_store_features(act, k, t)

                    for k in range(2):
                        act.sem_inc(s(f"fts_free{k}"), 16)
                        act_attr_load(act, k, k)
                    act_copy_turned(act, 0)
                    act_attr_load(act, 0, 2)
                    with act.Fori(0, (FEARLY - 3) // 2) as i:
                        for k in range(2):
                            step(k, 2 * i + k)
                    step(0, FEARLY - 3, load=False)
                    step(1, FEARLY - 2, load=False)
                    step(0, FEARLY - 1, ahead=False, load=False)
                    for k in range(2):
                        act.wait_ge(s(f"fts_free{k}"), 16)
                        act.sem_inc(s(f"fts_free{k}"), -16)

                @block.tensor
                def _(pe):
                    for n in range(0, EC, P):
                        m = min(P, EC - n)
                        if n:
                            pe.wait_ge(s("turn_copied"), 1)
                            pe.sem_inc(s("turn_copied"), -1)
                        pe.transpose(bank[4][0:m, 0:EP], dist[:, n:n + m], ident[0:EP, 0:EP]).then_inc(s("dist_turned"), 1)
                    pe.wait_ge(s("turn_copied"), 1)
                    pe.sem_inc(s("turn_copied"), -1)

                    def step(k, ahead=True):
                        if ahead:
                            pe_turn_edges(pe, 1 - k)
                        pe_features(pe, k)

                    pe_turn_edges(pe, 0)
                    with pe.Fori(0, (FEARLY - 1) // 2) as i:
                        for k in range(2):
                            step(k)
                    step(0, ahead=False)

                @block.sync
                def _(sp):
                    sp.sem_inc(s("el_free"), 1)
                    with sp.Fori(0, NB) as b:
                        start, end = block_range(sp, b, bounds, JMAX - RC)
                        with sp.Fori(start, end, RC) as j:
                            sp.wait_ge(s("el_ready"), 1)
                            sp.sem_inc(s("el_ready"), -1)
                            sp.dma_start(el_idx[bass.ds(j, RC)].rearrange("j p s -> p j s"), el_i[:]).then_inc(s("el_stored"), 16)
                            sp.dma_start(el_msk[bass.ds(j, RC)].rearrange("j p s -> p j s"), el_m[:]).then_inc(s("el_stored"), 16)
                            for h in range(2):
                                sp.dma_start(el_typ[bass.ds(j, RC), h].rearrange("j p s -> p j s"), el_t[:, :, h]).then_inc(s("el_stored"), 16)
                            sp.wait_ge(s("el_stored"), 64)
                            sp.sem_inc(s("el_stored"), -64)
                            sp.sem_inc(s("el_free"), 1)

        idx = [sb(f"idx{h}", [P, HALF], I32) for h in range(2)]
        first = sb("first", [P, 2], I32)
        msk = sb("msk", [P, SLOTS])
        typ = sb("typ", [2 * TYPES, P * HALF])
        typ_d = sb("typ_d", [2 * TYPES, P * HALF])
        onehot = sb("onehot", [2 * TYPES, P, HALF])
        feat = sb("feat", [P, SLOTS, REC])
        ft = sb("ft", [P, SLOTS, REC])
        sc = sb("sc", [P, SLOTS + 1, HEADS])
        top = sb("top", [P, HEADS])
        sh = sb("sh", [P, SLOTS + 1, HEADS])
        wt = sb("wt", [P, SLOTS + 1, HEADS])
        sw = sb("sw", [P, SLOTS + 1, HEADS])
        kk = [sb(f"kk{h}", [P, HALF, D]) for h in range(2)]
        work = sb("work", [P, SLOTS + 1, W1])
        prod = sb("prod", [P, SLOTS + 1, HV])
        land0 = [sb(f"land0{h}", [P, HALF, W0]) for h in range(2)]
        land1 = [sb(f"land1{h}", [P, HALF, W1]) for h in range(2)]
        land2 = [sb(f"land2{h}", [P, HALF + 1, D]) for h in range(2)]

        def dve_rsqrt(dve, ch, v, to, t, one_column=True):
            dve.tensor_scalar(to.bitcast(I32), v.bitcast(I32), -0.5, RSQRT_SEED, ALU.mult, ALU.add).then_inc(ch.semaphore, ch.one())
            dve.tensor_scalar(v, v, -0.5, None, ALU.mult).then_inc(ch.semaphore, ch.one())
            dve.wait_ge(ch.semaphore, ch.count)
            for _ in range(3):
                if one_column:
                    dve.tensor_scalar(t, to, to, v, ALU.mult, ALU.mult).then_inc(ch.semaphore, ch.one())
                    dve.wait_ge(ch.semaphore, ch.count)
                else:
                    dve.tensor_tensor(t, to, to, ALU.mult).then_inc(ch.semaphore, ch.one())
                    dve.wait_ge(ch.semaphore, ch.count)
                    dve.tensor_tensor(t, t, v, ALU.mult).then_inc(ch.semaphore, ch.one())
                    dve.wait_ge(ch.semaphore, ch.count)
                dve.scalar_tensor_tensor(to, t, 1.5, to, ALU.add, ALU.mult).then_inc(ch.semaphore, ch.one())
                dve.wait_ge(ch.semaphore, ch.count)

        def dve_centre(dve, ch, x):
            dve.bn_stats(st6[:], x).then_inc(ch.semaphore, ch.one())
            dve.wait_ge(ch.semaphore, ch.count)
            dve.bn_aggr(mv[:], st6[:]).then_inc(ch.semaphore, ch.one())
            dve.wait_ge(ch.semaphore, ch.count)
            dve.tensor_scalar(var[:], mv[:, 1:2], EPS, None, ALU.add).then_inc(ch.semaphore, ch.one())
            dve.tensor_scalar(hid[:], x, mv[:, 0:1], 0.0, ALU.subtract, ALU.max).then_inc(ch.semaphore, ch.one())
            dve.wait_ge(ch.semaphore, ch.count)

        def dve_seed(dve, ch):
            dve.tensor_scalar(rstd[:].bitcast(I32), var[:].bitcast(I32), -0.5, RSQRT_SEED, ALU.mult, ALU.add).then_inc(ch.semaphore, ch.one())
            dve.tensor_scalar(var[:], var[:], -0.5, None, ALU.mult).then_inc(ch.semaphore, ch.one())
            dve.wait_ge(ch.semaphore, ch.count)
            dve_newton(dve, ch, 1)

        def dve_newton(dve, ch, steps):
            for _ in range(steps):
                dve.tensor_scalar(newt[:], rstd[:], rstd[:], var[:], ALU.mult, ALU.mult).then_inc(ch.semaphore, ch.one())
                dve.wait_ge(ch.semaphore, ch.count)
                dve.scalar_tensor_tensor(rstd[:], newt[:], 1.5, rstd[:], ALU.add, ALU.mult).then_inc(ch.semaphore, ch.one())
                dve.wait_ge(ch.semaphore, ch.count)

        def pe_project(pe, w, n):
            pe.wait_ge(s("hid_ready"), 1)
            pe.sem_inc(s("hid_ready"), -1)
            pe.transpose(ps_t[:, 0:P], hid[:], ident[:]).then_inc(s("hid_turned"), 1)
            pe.wait_ge(s("hid_t_ready"), 1)
            pe.sem_inc(s("hid_t_ready"), -1)
            pe.matmul(ps_p[:, 0:n], hid_t[:], w, start=True, stop=True).then_inc(s("projected"), 1)

        def dve_project(dve, ch, meanwhile=None, normalise=False):
            dve.wait_ge(ch.semaphore, ch.count)
            dve.sem_inc(s("hid_ready"), 1)
            if normalise:
                dve_seed(dve, ch)
            dve.wait_ge(s("hid_turned"), 1)
            dve.sem_inc(s("hid_turned"), -1)
            dve.tensor_copy(hid_t[:], ps_t[:, 0:P]).then_inc(ch.semaphore, ch.one())
            dve.wait_ge(ch.semaphore, ch.count)
            dve.sem_inc(s("hid_t_ready"), 1)
            if normalise:
                dve_newton(dve, ch, 2)
            if meanwhile:
                meanwhile()
            dve.wait_ge(s("projected"), 1)
            dve.sem_inc(s("projected"), -1)

        def dve_table(dve, ch, b, number):
            dve.tensor_copy(stage_i[:], perm[:, bass.ds(b, 1)]).then_inc(ch.semaphore, ch.one())
            dve.wait_ge(ch.semaphore, ch.count)
            dve.sem_inc(s("table_ready"), 1)

        def blk(t, b, c0, c1):
            return t[:, bass.ds(b, 1), c0:c1].rearrange("p o c -> p (o c)")

        def dve_to_l0(dve, ch, b, wait, padding=False):
            dve.tensor_scalar(hid[:], blk(xs, b, 0, D), mvs[:, bass.ds(b, 1), 0], rstds[:, bass.ds(b, 1)], ALU.subtract, ALU.mult).then_inc(ch.semaphore, ch.one())
            dve.wait_ge(ch.semaphore, ch.count)
            dve.tensor_scalar(hid[:], hid[:], 0.0, None, ALU.max).then_inc(ch.semaphore, ch.one())
            dve.wait_ge(ch.semaphore, ch.count)
            dve_project(dve, ch)
            wait()
            dve.tensor_tensor(stage0[:, 0:D], ps_p[:, 0:D], b_l0[:, 0:D], ALU.add).then_inc(ch.semaphore, ch.one())
            dve.tensor_tensor(stage0[:, D:].rearrange("p (h v) -> p h v", h=HEADS)[:, :, 0:HD],
                              heads(ps_p[:, D:2 * D]), heads(b_l0[:, D:2 * D]), ALU.add).then_inc(ch.semaphore, ch.one())
            dve.tensor_copy(stage_i[:], perm[:, bass.ds(b, 1)]).then_inc(ch.semaphore, ch.one())
            dve.wait_ge(ch.semaphore, ch.count)
            if padding:
                dve.tensor_scalar(stage0[:], stage0[:], real[:, bass.ds(b, 1)], None, ALU.mult).then_inc(ch.semaphore, ch.one())
                dve.wait_ge(ch.semaphore, ch.count)
            dve.sem_inc(s("table_ready"), 1)
            dve.tensor_tensor(blk(own0, b, 0, D), ps_p[:, 2 * D:3 * D], b_l0[:, 2 * D:], ALU.add).then_inc(ch.semaphore, ch.one())
            dve.wait_ge(ch.semaphore, ch.count)
            dve.tensor_scalar(blk(own0, b, 0, D), blk(own0, b, 0, D), SCALE, None, ALU.mult).then_inc(ch.semaphore, ch.one())
            dve.wait_ge(ch.semaphore, ch.count)

        def dve_to_conv(dve, ch, b, wait, number, meanwhile=None, normalise=False):
            dve_project(dve, ch, meanwhile, normalise)
            of_h = blk(own1, b, 0, HV).rearrange("p (h v) -> p h v", h=HEADS)[:, :, 0:HD]
            if normalise:
                dve.tensor_scalar(of_h, heads(ps_p[:, 0:D]), rstd[:], None, ALU.mult).then_inc(ch.semaphore, ch.one())
                dve.tensor_scalar(blk(own1, b, HV, HV + REC), ps_p[:, D:D + REC], rstd[:], None, ALU.mult).then_inc(ch.semaphore, ch.one())
                dve.wait_ge(ch.semaphore, ch.count)
            else:
                dve.tensor_copy(of_h, heads(ps_p[:, 0:D])).then_inc(ch.semaphore, ch.one())
                dve.tensor_copy(blk(own1, b, HV, HV + REC), ps_p[:, D:D + REC]).then_inc(ch.semaphore, ch.one())
                dve.wait_ge(ch.semaphore, ch.count)
            wait()
            dve.tensor_scalar(stage1[:, HV:W1], blk(own1, b, HV, W1), padneg[:, bass.ds(b, 1)], None, ALU.add).then_inc(ch.semaphore, ch.one())
            dve.tensor_copy(stage1[:, 0:HV], blk(own1, b, 0, HV)).then_inc(ch.semaphore, ch.one())
            dve_table(dve, ch, b, number)

        def dve_softmax_mean(dve, ch, state, eps, to):
            by_head = state.rearrange("p (h v) -> p h v", h=HEADS)
            dve.tensor_scalar(den[:], by_head[:, :, HD], eps, None, ALU.add).then_inc(ch.semaphore, ch.one())
            dve.wait_ge(ch.semaphore, ch.count)
            dve.reciprocal(den[:], den[:]).then_inc(ch.semaphore, ch.one())
            dve.wait_ge(ch.semaphore, ch.count)
            dve.tensor_tensor(heads(to), by_head[:, :, 0:HD], den[:].unsqueeze(2).broadcast_to([P, HEADS, HD]), ALU.mult).then_inc(ch.semaphore, ch.one())
            dve.wait_ge(ch.semaphore, ch.count)

        def after_l0(dve, ch, b, wait, meanwhile):
            dve_softmax_mean(dve, ch, work[:, SLOTS, 0:HV], 1e-8, hid[:])

            def prepare():
                dve.tensor_tensor(tmp[:], blk(xs, b, 0, D), bo0[:], ALU.add).then_inc(ch.semaphore, ch.one())
                dve.wait_ge(ch.semaphore, ch.count)
                if meanwhile:
                    meanwhile()

            dve_project(dve, ch, prepare)
            dve.tensor_tensor(blk(xs, b, 0, D), ps_p[:, 0:D], tmp[:], ALU.add).then_inc(ch.semaphore, ch.one())
            dve.wait_ge(ch.semaphore, ch.count)
            dve_centre(dve, ch, blk(xs, b, 0, D))
            dve_to_conv(dve, ch, b, wait, 1, normalise=True)

        def after_conv(n):
            def run(dve, ch, b, wait, meanwhile):
                dve_softmax_mean(dve, ch, work[:, SLOTS, 0:HV], 1e-16, tmp[:])
                if n < 2:
                    dve.tensor_tensor(hid[:], tmp[:], b_g[min(n, 1)][:], ALU.add).then_inc(ch.semaphore, ch.one())
                    dve.wait_ge(ch.semaphore, ch.count)
                    dve_to_conv(dve, ch, b, wait, n + 2, meanwhile)
                    return
                dve.tensor_tensor(tmp[:], tmp[:], b_g[1][:], ALU.add).then_inc(ch.semaphore, ch.one())
                dve.wait_ge(ch.semaphore, ch.count)
                dve.tensor_reduce(col[:, 0:1], tmp[:], AX.X, ALU.max).then_inc(ch.semaphore, ch.one())
                dve.wait_ge(ch.semaphore, ch.count)
                dve.tensor_scalar(tmp[:], tmp[:], col[:, 0:1], None, ALU.subtract).then_inc(ch.semaphore, ch.one())
                dve.wait_ge(ch.semaphore, ch.count)
                dve.sem_inc(s("logits_ready"), 1)
                dve.wait_ge(s("log_sum"), 1)
                dve.sem_inc(s("log_sum"), -1)
                dve.scalar_tensor_tensor(blk(xs, b, 0, D), tmp[:], col[:, 2:3], blk(xs, b, 0, D), ALU.subtract, ALU.add).then_inc(ch.semaphore, ch.one())
                dve.wait_ge(ch.semaphore, ch.count)
                dve_centre(dve, ch, blk(xs, b, 0, D))
                dve_project(dve, ch, meanwhile, normalise=True)
                dve.tensor_scalar(blk(own2, b, 2 * D, 3 * D), hid[:], rstd[:], None, ALU.mult).then_inc(ch.semaphore, ch.one())
                wait()
                dve.scalar_tensor_tensor(blk(own2, b, 0, 2 * D), ps_p[:, 0:2 * D], rstd[:], b_l2[:, 0:2 * D], ALU.mult, ALU.add).then_inc(ch.semaphore, ch.one())
                dve.scalar_tensor_tensor(stage2[:], ps_p[:, 2 * D:3 * D], rstd[:], b_l2[:, 2 * D:], ALU.mult, ALU.add).then_inc(ch.semaphore, ch.one())
                dve.wait_ge(ch.semaphore, ch.count)
                dve.tensor_scalar(blk(own2, b, 0, D), blk(own2, b, 0, D), SCALE, None, ALU.mult).then_inc(ch.semaphore, ch.one())
                dve_table(dve, ch, b, 4)
            return run

        def act_after_conv3(act):
            act.wait_ge(s("logits_ready"), 1)
            act.sem_inc(s("logits_ready"), -1)
            act.activation(tmp2[:], tmp[:], ACT.Exp, accum_out=col[:, 1:2]).then_inc(s("act_chain"), 1)
            act.wait_ge(s("act_chain"), 1)
            act.sem_inc(s("act_chain"), -1)
            act.activation(col[:, 2:3], col[:, 1:2], ACT.Ln).then_inc(s("log_sum"), 1)
            act.preload_act_table(ACT.Exp)

        def after_l2(dve, ch, b, wait, meanwhile):
            dve.tensor_scalar(den[:], ss[:, SLOTS, :], 1e-30, None, ALU.max).then_inc(ch.semaphore, ch.one())
            dve.wait_ge(ch.semaphore, ch.count)
            dve.reciprocal(den[:], den[:]).then_inc(ch.semaphore, ch.one())
            dve.wait_ge(ch.semaphore, ch.count)
            dve.tensor_tensor(den[:], den[:], ss[:, SLOTS, :], ALU.mult).then_inc(ch.semaphore, ch.one())
            dve.wait_ge(ch.semaphore, ch.count)
            dve.tensor_tensor(heads(hid[:]), heads(blk(own2, b, D, 2 * D)), den[:].unsqueeze(2).broadcast_to([P, HEADS, HD]), ALU.mult).then_inc(ch.semaphore, ch.one())
            dve.wait_ge(ch.semaphore, ch.count)

            def prepare():
                dve.tensor_tensor(tmp[:], blk(own2, b, 2 * D, 3 * D), bo2[:], ALU.add).then_inc(ch.semaphore, ch.one())
                dve.tensor_tensor(tmp2[:], blk(xs, b, 0, D), bet[:], ALU.add).then_inc(ch.semaphore, ch.one())
                dve.wait_ge(ch.semaphore, ch.count)
                if meanwhile:
                    meanwhile()

            dve_project(dve, ch, prepare)
            dve.tensor_tensor(tmp[:], ps_p[:, 0:D], tmp[:], ALU.add).then_inc(ch.semaphore, ch.one())
            dve.wait_ge(ch.semaphore, ch.count)
            dve.bn_stats(st6[:], tmp[:]).then_inc(ch.semaphore, ch.one())
            dve.wait_ge(ch.semaphore, ch.count)
            dve.bn_aggr(mv[:], st6[:]).then_inc(ch.semaphore, ch.one())
            dve.wait_ge(ch.semaphore, ch.count)
            dve.tensor_scalar(var[:], mv[:, 1:2], EPS, None, ALU.add).then_inc(ch.semaphore, ch.one())
            dve.scalar_tensor_tensor(tmp[:], tmp[:], mv[:, 0:1], gam[:], ALU.subtract, ALU.mult).then_inc(ch.semaphore, ch.one())
            dve.wait_ge(ch.semaphore, ch.count)
            dve_seed(dve, ch)
            dve_newton(dve, ch, 2)
            dve.scalar_tensor_tensor(blk(xs, b, 0, D), tmp[:], rstd[:], tmp2[:], ALU.mult, ALU.add).then_inc(ch.semaphore, ch.one())
            dve.wait_ge(ch.semaphore, ch.count)
            dve_centre(dve, ch, blk(xs, b, 0, D))
            dve_seed(dve, ch)
            dve_newton(dve, ch, 2)
            wait()
            dve.tensor_scalar(stage2[:], hid[:], rstd[:], dis[:, bass.ds(b, 1)], ALU.mult, ALU.mult).then_inc(ch.semaphore, ch.one())
            dve.wait_ge(ch.semaphore, ch.count)
            dve.tensor_copy(blk(own0, b, 0, D), stage2[:]).then_inc(ch.semaphore, ch.one())
            dve_table(dve, ch, b, 5)

        def after_l3(dve, ch, b, wait, meanwhile):
            dve.tensor_scalar(tmp[:], land2[0][:, HALF, :], dis[:, bass.ds(b, 1)], None, ALU.mult).then_inc(ch.semaphore, ch.one())
            dve.wait_ge(ch.semaphore, ch.count)
            wait()
            dve.tensor_tensor(stage2[:], blk(xs, b, 0, D), tmp[:], ALU.add).then_inc(ch.semaphore, ch.one())
            dve_table(dve, ch, b, 6)

        def slots(ap, n):
            return ap.unsqueeze(1).broadcast_to([P, n, ap.shape[1]])

        S1 = SLOTS + 1
        now = sc[:, 0:SLOTS, :]

        def dve_weights(dve, ch):
            dve.tensor_reduce(top[:], sc[:].rearrange("p s h -> p h s"), AX.X, ALU.max).then_inc(ch.semaphore, ch.one())
            dve.wait_ge(ch.semaphore, ch.count)
            dve.tensor_tensor(sh[:], sc[:], slots(top[:], S1), ALU.subtract).then_inc(ch.semaphore, ch.one())
            dve.wait_ge(ch.semaphore, ch.count)
            dve.sem_inc(s("shifted"), 1)
            dve.wait_ge(s("exped"), 1)
            dve.sem_inc(s("exped"), -1)

        def act_weights(act):
            act.wait_ge(s("shifted"), 1)
            act.sem_inc(s("shifted"), -1)
            act.activation(sc[:, SLOTS, :], top[:], ACT.Copy)
            act.activation(wt[:], sh[:], ACT.Exp).then_inc(s("exped"), 1)

        def dve_weigh(dve, ch):
            dve.tensor_tensor(prod[:].rearrange("p s (h v) -> p s h v", h=HEADS),
                              work[:, :, 0:HV].rearrange("p s (h v) -> p s h v", h=HEADS),
                              wt[:].unsqueeze(3).broadcast_to([P, S1, HEADS, V]), ALU.mult).then_inc(ch.semaphore, ch.one())
            dve.wait_ge(ch.semaphore, ch.count)
            dve.sem_inc(s("work_free"), 1)
            dve.tensor_reduce(work[:, SLOTS, 0:HV], prod[:].rearrange("p s c -> p c s"), AX.X, ALU.add).then_inc(ch.semaphore, ch.one())
            dve.wait_ge(ch.semaphore, ch.count)

        def dve_scores(dve, ch, h, keys, queries):
            dve.tensor_tensor(kk[h][:], keys, slots(queries, HALF), ALU.mult).then_inc(ch.semaphore, ch.one())
            dve.wait_ge(ch.semaphore, ch.count)

        def dve_scores_sum(dve, ch, h):
            dve.tensor_reduce(sc[:, h * HALF:(h + 1) * HALF, :], kk[h][:].rearrange("p s (h d) -> p s h d", h=HEADS), AX.X, ALU.add).then_inc(ch.semaphore, ch.one())
            dve.wait_ge(ch.semaphore, ch.count)

        def dve_mask(dve, ch):
            dve.tensor_tensor(now, now, msk[:].unsqueeze(2).broadcast_to([P, SLOTS, HEADS]), ALU.add).then_inc(ch.semaphore, ch.one())
            dve.wait_ge(ch.semaphore, ch.count)
            dve.sem_inc(s("msk_free"), 1)

        def chunk_l0(dve, ch, b, j, landed):
            for h in range(2):
                dve.wait_ge(s(f"rel_ready{h}"), 1)
                dve.sem_inc(s(f"rel_ready{h}"), -1)
                dve_scores(dve, ch, h, ps_rel[h][:].rearrange("p (s d) -> p s d", d=D), blk(own0, b, 0, D))
                dve.sem_inc(s(f"rel_free{h}"), 1)
                dve_scores_sum(dve, ch, h)
            dve_weights(dve, ch)
            dve_weigh(dve, ch)

        def chunk_conv(dve, ch, b, j, landed):
            dve.wait_ge(s("copied"), 2)
            dve.sem_inc(s("copied"), -2)
            dve.tensor_tensor(now, work[:, 0:SLOTS, HV:W1], slots(blk(own1, b, W1, W1 + HEADS), SLOTS), ALU.add).then_inc(ch.semaphore, ch.one())
            dve.wait_ge(ch.semaphore, ch.count)
            dve.scalar_tensor_tensor(now, now, 0.2, now, ALU.mult, ALU.max).then_inc(ch.semaphore, ch.one())
            dve.wait_ge(ch.semaphore, ch.count)
            dve_weights(dve, ch)
            dve_weigh(dve, ch)

        def chunk_l2(dve, ch, b, j, landed):
            for h in range(2):
                dve.wait_ge(s("copied"), 1)
                dve.sem_inc(s("copied"), -1)
                dve_scores(dve, ch, h, work[:, h * HALF:(h + 1) * HALF, 0:D], blk(own2, b, 0, D))
                dve_scores_sum(dve, ch, h)
            dve.wait_ge(s("feat_copied"), 1)
            dve.sem_inc(s("feat_copied"), -1)
            dve.wait_ge(s("msk_in"), 16)
            dve.sem_inc(s("msk_in"), -16)
            dve.tensor_tensor(now, now, ft[:, :, 0:HEADS], ALU.add).then_inc(ch.semaphore, ch.one())
            dve.wait_ge(ch.semaphore, ch.count)
            dve.tensor_tensor(now, now, slots(cons[:, bass.ds(b, 1), :].rearrange("p o c -> p (o c)"), SLOTS), ALU.mult).then_inc(ch.semaphore, ch.one())
            dve.wait_ge(ch.semaphore, ch.count)
            dve.tensor_tensor(now, now, ft[:, :, HEADS:], ALU.add).then_inc(ch.semaphore, ch.one())
            dve.wait_ge(ch.semaphore, ch.count)
            dve.sem_inc(s("work_free"), 1)
            dve_mask(dve, ch)
            dve_weights(dve, ch)
            dve.tensor_tensor(sw[:], ss[:], wt[:], ALU.mult).then_inc(ch.semaphore, ch.one())
            dve.wait_ge(ch.semaphore, ch.count)
            dve.tensor_reduce(ss[:, SLOTS, :], sw[:].rearrange("p s h -> p h s"), AX.X, ALU.add).then_inc(ch.semaphore, ch.one())
            dve.wait_ge(ch.semaphore, ch.count)

        def chunk_l3(dve, ch, b, j, landed):
            for h in range(2):
                dve.wait_ge(landed[h], 16 * HALF * (j + 1))
                dve.tensor_reduce(land2[1 - h][:, HALF, :], land2[h][:].rearrange("p s c -> p c s"), AX.X, ALU.add).then_inc(ch.semaphore, ch.one())
                dve.wait_ge(ch.semaphore, ch.count)
                dve.sem_inc(s(f"rows_free{h}"), 1)

        def act_onehot(act):
            act.wait_ge(s("typ_in"), 32)
            act.sem_inc(s("typ_in"), -32)
            act.activation(typ_d[:], typ[:], ACT.Square, bias=neg_p[:]).then_inc(s("act_chain"), 1)
            act.wait_ge(s("act_chain"), 1)
            act.sem_inc(s("act_chain"), -1)
            act.sem_inc(s("typ_free"), 1)
            act.wait_ge(s("onehot_free"), 1)
            act.sem_inc(s("onehot_free"), -1)
            act.activation(onehot[:].rearrange("t p s -> t (p s)"), typ_d[:], ACT.Relu, bias=1.0, scale=-1.0).then_inc(s("act_chain"), 1)
            act.wait_ge(s("act_chain"), 1)
            act.sem_inc(s("act_chain"), -1)
            act.sem_inc(s("onehot_in"), 1)

        def act_copy_l0(act, n, landed):
            act.wait_ge(s("work_free"), 1)
            act.sem_inc(s("work_free"), -1)
            for h in range(2):
                act.wait_ge(landed[h], 16 * HALF * (n + 1))
                act.activation(work[:, h * HALF:(h + 1) * HALF, 0:HV], land0[h][:, :, D:W0], ACT.Copy).then_inc(s(f"rows_free{h}"), 1)

        def act_copy_conv(act, n, landed):
            act.wait_ge(s("work_free"), 1)
            act.sem_inc(s("work_free"), -1)
            for h in range(2):
                act.wait_ge(landed[h], 16 * HALF * (n + 1))
                act.activation(work[:, h * HALF:(h + 1) * HALF, :], land1[h][:], ACT.Copy).then_inc(s("act_chain"), 1)
                act.wait_ge(s("act_chain"), 1)
                act.sem_inc(s("act_chain"), -1)
                act.sem_inc(s(f"rows_free{h}"), 1)
                act.sem_inc(s("copied"), 1)

        def act_copy_l2(act, n, landed):
            act.wait_ge(s("work_free"), 1)
            act.sem_inc(s("work_free"), -1)
            for h in range(2):
                act.wait_ge(landed[h], 16 * HALF * (n + 1))
                act.activation(work[:, h * HALF:(h + 1) * HALF, 0:D], land2[h][:, 0:HALF, :], ACT.Copy).then_inc(s("act_chain"), 1)
                act.wait_ge(s("act_chain"), 1)
                act.sem_inc(s("act_chain"), -1)
                act.sem_inc(s(f"rows_free{h}"), 1)
                act.sem_inc(s("copied"), 1)
            act.wait_ge(s("feat_in"), 16 * n + 16)
            act.activation(ft[:], feat[:], ACT.Copy).then_inc(s("act_chain"), 1)
            act.wait_ge(s("act_chain"), 1)
            act.sem_inc(s("act_chain"), -1)
            act.sem_inc(s("feat_free"), 1)
            act.sem_inc(s("feat_copied"), 1)

        def start_l0(dve, ch, b):
            dve.memset(sc[:, SLOTS, :], 0.0).then_inc(ch.semaphore, ch.one())
            dve.memset(work[:, SLOTS, :], 0.0).then_inc(ch.semaphore, ch.one())
            dve.wait_ge(ch.semaphore, ch.count)

        def start_conv(dve, ch, b):
            m = sc[:, SLOTS, :]
            dve.tensor_copy(work[:, SLOTS, 0:HV], blk(own1, b, 0, HV)).then_inc(ch.semaphore, ch.one())
            dve.tensor_tensor(m, blk(own1, b, HV, W1), blk(own1, b, W1, W1 + HEADS), ALU.add).then_inc(ch.semaphore, ch.one())
            dve.wait_ge(ch.semaphore, ch.count)
            dve.scalar_tensor_tensor(m, m, 0.2, m, ALU.mult, ALU.max).then_inc(ch.semaphore, ch.one())
            dve.wait_ge(ch.semaphore, ch.count)

        def start_l2(dve, ch, b):
            dve.memset(sc[:, SLOTS, :], START).then_inc(ch.semaphore, ch.one())
            dve.memset(ss[:, SLOTS, :], 0.0).then_inc(ch.semaphore, ch.one())
            dve.wait_ge(ch.semaphore, ch.count)

        def start_l3(dve, ch, b):
            dve.tensor_copy(land2[0][:, HALF, :], blk(own0, b, 0, D)).then_inc(ch.semaphore, ch.one())
            dve.wait_ge(ch.semaphore, ch.count)

        def scatter(pool, stage, target, rows=P):
            pool.wait_ge(s("table_ready"), 1)
            pool.sem_inc(s("table_ready"), -1)
            pool.indirect_dma_start(target, bass.IndirectOffsetOnAxis(ap=stage_i[0:rows].bitcast(U32), axis=0),
                                    stage[0:rows], None).then_inc(s("table_stored"), 16)

        with nc.Block() as block:
            @block.gpsimd
            def _(pool):
                with pool.Fori(0, NB) as b:
                    scatter(pool, stage0, table[0])
                pool.wait_ge(s("table_stored"), 16 * NB)

            @block.vector
            def _(dve):
                ch = Chain(s("dve_chain"))
                dve.memset(c_hid[:], 0.0).then_inc(ch.semaphore, ch.one())
                dve.wait_ge(ch.semaphore, ch.count)
                nodes = c_hid[:, 0:NB, :]
                dve.tensor_tensor(nodes, wc1[:].unsqueeze(1).broadcast_to([P, NB, CW]),
                                  info[:, :, 4:5].broadcast_to([P, NB, CW]), ALU.mult).then_inc(ch.semaphore, ch.one())
                dve.wait_ge(ch.semaphore, ch.count)
                dve.tensor_tensor(nodes, nodes, bc1[:].unsqueeze(1).broadcast_to([P, NB, CW]), ALU.add).then_inc(ch.semaphore, ch.one())
                dve.wait_ge(ch.semaphore, ch.count)
                dve.tensor_scalar(nodes, nodes, 0.0, None, ALU.max).then_inc(ch.semaphore, ch.one())
                dve.wait_ge(ch.semaphore, ch.count)
                dve.sem_inc(s("c_hid_ready"), 1)
                for b in range(NB):
                    dve.bn_stats(st6s[:, b, :], xs[:, b, :]).then_inc(ch.semaphore, ch.one())
                dve.wait_ge(ch.semaphore, ch.count)
                for b in range(NB):
                    dve.bn_aggr(mvs[:, b, :], st6s[:, b, :]).then_inc(ch.semaphore, ch.one())
                dve.wait_ge(ch.semaphore, ch.count)
                dve.tensor_scalar(vars_[:], mvs[:, :, 1], EPS, None, ALU.add).then_inc(ch.semaphore, ch.one())
                dve.wait_ge(ch.semaphore, ch.count)
                dve_rsqrt(dve, ch, vars_[:], rstds[:], news[:], one_column=False)
                dve.wait_ge(ch.semaphore, ch.count)
                dve.sem_inc(ch.semaphore, -ch.clear())
                dve.wait_ge(s("c_z_ready"), 1)
                dve.sem_inc(s("c_z_ready"), -1)
                dve.tensor_tensor(c_z[:], bank[4][:, 0:NB * HEADS].rearrange("p (b h) -> p b h", h=HEADS),
                                  bc2[:].unsqueeze(1).broadcast_to([P, NB, HEADS]), ALU.add).then_inc(ch.semaphore, ch.one())
                dve.wait_ge(ch.semaphore, ch.count)
                dve.tensor_scalar(c_pos[:], c_z[:], 0.0, None, ALU.is_ge).then_inc(ch.semaphore, ch.one())
                dve.scalar_tensor_tensor(c_z[:], c_z[:], -1.0, c_z[:], ALU.mult, ALU.max).then_inc(ch.semaphore, ch.one())
                dve.wait_ge(ch.semaphore, ch.count)
                dve.sem_inc(s("c_arg"), 1)
                dve.wait_ge(s("c_exp"), 1)
                dve.sem_inc(s("c_exp"), -1)
                dve.tensor_tensor(c_pos[:], c_pos[:], c_e[:], ALU.max).then_inc(ch.semaphore, ch.one())
                dve.tensor_scalar(c_e[:], c_e[:], 1.0, None, ALU.add).then_inc(ch.semaphore, ch.one())
                dve.wait_ge(ch.semaphore, ch.count)
                dve.reciprocal(c_e[:], c_e[:]).then_inc(ch.semaphore, ch.one())
                dve.wait_ge(ch.semaphore, ch.count)
                dve.tensor_tensor(cons[:], c_e[:], c_pos[:], ALU.mult).then_inc(ch.semaphore, ch.one())
                dve.wait_ge(ch.semaphore, ch.count)
                dve_to_l0(dve, ch, 0, lambda: None)
                dve.wait_ge(ch.semaphore, ch.count)
                dve.sem_inc(ch.semaphore, -ch.clear())
                with dve.Fori(1, NB - 1) as b:
                    dve_to_l0(dve, ch, b, lambda: dve.wait_ge(s("table_stored"), 16 * b))
                    dve.wait_ge(ch.semaphore, ch.count)
                    dve.sem_inc(ch.semaphore, -ch.clear())
                dve_to_l0(dve, ch, NB - 1, lambda: dve.wait_ge(s("table_stored"), 16 * (NB - 1)), padding=True)
                dve.wait_ge(ch.semaphore, ch.count)
                dve.sem_inc(ch.semaphore, -ch.clear())

            @block.scalar
            def _(act):
                act.wait_ge(s("c_hid_turned"), 1)
                act.sem_inc(s("c_hid_turned"), -1)
                act.activation(c_t[:, 0:4 * P], bank[2][:, 0:4 * P], ACT.Copy)
                act.activation(c_t[:, 4 * P:], bank[3][:, 0:(NG - 4) * P], ACT.Copy).then_inc(s("c_copied"), 1)
                act.wait_ge(s("c_arg"), 1)
                act.sem_inc(s("c_arg"), -1)
                act.activation(c_e[:], c_z[:], ACT.Exp, scale=-1.0).then_inc(s("c_exp"), 1)

            @block.tensor
            def _(pe):
                pe.wait_ge(s("c_hid_ready"), 1)
                pe.sem_inc(s("c_hid_ready"), -1)
                for g in range(NG):
                    last = pe.transpose(bank[2 + g // 4][:, (g % 4) * P:(g % 4 + 1) * P],
                                        c_hid[:, g * CG:(g + 1) * CG, :].rearrange("p b w -> p (b w)"), ident[:])
                last.then_inc(s("c_hid_turned"), 1)
                pe.wait_ge(s("c_copied"), 1)
                pe.sem_inc(s("c_copied"), -1)
                for g in range(NG):
                    last = pe.matmul(bank[4][:, g * CG * HEADS:(g + 1) * CG * HEADS], c_t[:, g * P:(g + 1) * P], wc2[:], start=True, stop=True)
                last.then_inc(s("c_z_ready"), 1)
                with pe.Fori(0, NB) as b:
                    pe_project(pe, w_l0[:], 3 * D)

        def edge_pass(number, rows, source, start, chunk, after, act_copy, act_after, pe_after, stage, target,
                      types=False, mask=False, features=False, copies=False, frees=1,
                      makes_features=None, numbered=False):
            landed = [ctx.enter_context(nc.semaphore(f"rows_in{number}{h}")) for h in range(2)]
            before_this = NB * (number + 1)

            def gathers(pool, b):
                first_chunk, end = block_range(pool, b)
                with pool.Fori(first_chunk, end) as j:
                    for h in range(2):
                        pool.wait_ge(s(f"idx_in{h}"), 16)
                        pool.sem_inc(s(f"idx_in{h}"), -16)
                        pool.wait_ge(s(f"rows_free{h}"), frees)
                        pool.sem_inc(s(f"rows_free{h}"), -frees)
                        for k in range(HALF):
                            pool.indirect_dma_start(rows[h][:, k, :], None, source,
                                                    bass.IndirectOffsetOnAxis(ap=idx[h][:, k:k + 1].bitcast(U32), axis=0)).then_inc(landed[h], 16)
                    if features:
                        pool.wait_ge(s("first_in"), 16)
                        pool.sem_inc(s("first_in"), -16)
                        pool.wait_ge(s("feat_free"), 1)
                        pool.sem_inc(s("feat_free"), -1)
                        pool.indirect_dma_start(feat[:].rearrange("p s f -> p (s f)"), None, rec_ft,
                                                bass.IndirectOffsetOnAxis(ap=first[:, 0:1].bitcast(U32), axis=0)).then_inc(s("feat_in"), 16)

            with nc.Block() as block:
                @block.sync
                def _(sp):
                    if mask:
                        sp.sem_inc(s("msk_free"), 1)
                    if types:
                        sp.sem_inc(s("typ_free"), 1)

                    def loads(j, gathered):
                        def one(t, c0, c1):
                            return t[bass.ds(j, 1), :, c0:c1].rearrange("j p s -> p (j s)")
                        for h in range(2):
                            gathered(landed[h], 16 * HALF)
                            sp.dma_start(idx[h][:], one(el_idx, h * HALF, (h + 1) * HALF)).then_inc(s(f"idx_in{h}"), 16)
                            if types and h == 0:
                                sp.wait_ge(s("typ_free"), 1)
                                sp.sem_inc(s("typ_free"), -1)
                                for half in range(2):
                                    sp.dma_start(typ[half * TYPES:(half + 1) * TYPES],
                                                 el_typ[bass.ds(j, 1), half].rearrange("j p s -> (j p s)").partition_broadcast(TYPES)).then_inc(s("typ_in"), 16)
                            if features and h == 0:
                                gathered(s("feat_in"), 16)
                                sp.dma_start(first[:], one(el_idx, SLOTS, SLOTS + 2)).then_inc(s("first_in"), 16)
                        if mask:
                            sp.wait_ge(s("msk_free"), 1)
                            sp.sem_inc(s("msk_free"), -1)
                            sp.dma_start(msk[:], one(el_msk, 0, SLOTS)).then_inc(s("msk_in"), 16)

                    chunks = sp.value_load(bounds[0:1, NB:NB + 1], min_val=2, max_val=JMAX)
                    loads(0, lambda semaphore, each: None)
                    with sp.Fori(1, chunks) as j:
                        loads(j, lambda semaphore, each: sp.wait_ge(semaphore, j * each))
                    if mask:
                        sp.wait_ge(s("msk_free"), 1)
                        sp.sem_inc(s("msk_free"), -1)
                    if types:
                        sp.wait_ge(s("typ_free"), 1)
                        sp.sem_inc(s("typ_free"), -1)

                @block.gpsimd
                def _(pool):
                    gathers(pool, 0)
                    with pool.Fori(1, NB) as b:
                        gathers(pool, b)
                        scatter(pool, stage, target)
                    scatter(pool, stage, target, TAIL if target is out else P)
                    pool.wait_ge(s("table_stored"), 16 * (before_this + NB))

                @block.vector
                def _(dve):
                    ch = Chain(s("dve_chain"))
                    for h in range(2):
                        dve.sem_inc(s(f"rows_free{h}"), frees)
                    if features:
                        dve.sem_inc(s("feat_free"), 1)
                    if copies:
                        dve.sem_inc(s("work_free"), 1)

                    def block_count(b):
                        return dve.value_load(counts[0:1, bass.ds(b, 1)], min_val=2, max_val=JMAX)

                    def chunks(b, count):
                        start(dve, ch, b)
                        dve.wait_ge(ch.semaphore, ch.count)
                        dve.sem_inc(ch.semaphore, -ch.clear())
                        first_chunk, end = block_range(dve, b) if numbered else (0, count)
                        with dve.Fori(first_chunk, end) as j:
                            chunk(dve, ch, b, j, landed)
                            dve.wait_ge(ch.semaphore, ch.count)
                            dve.sem_inc(ch.semaphore, -ch.clear())

                    chunks(0, None if numbered else block_count(0))
                    with dve.Fori(1, NB) as b:
                        loaded = []
                        after(dve, ch, b - 1, lambda: dve.wait_ge(s("table_stored"), 16 * (before_this - 1) + 16 * b),
                              lambda: loaded.append(block_count(b)))
                        dve.wait_ge(ch.semaphore, ch.count)
                        dve.sem_inc(ch.semaphore, -ch.clear())
                        chunks(b, loaded[0] if loaded else None)
                    after(dve, ch, NB - 1, lambda: dve.wait_ge(s("table_stored"), 16 * (before_this + NB - 1)), None)
                    dve.wait_ge(ch.semaphore, ch.count)
                    dve.sem_inc(ch.semaphore, -ch.clear())
                    for h in range(2):
                        dve.wait_ge(s(f"rows_free{h}"), frees)
                        dve.sem_inc(s(f"rows_free{h}"), -frees)
                    if features:
                        dve.wait_ge(s("feat_free"), 1)
                        dve.sem_inc(s("feat_free"), -1)
                    if copies:
                        dve.wait_ge(s("work_free"), 1)
                        dve.sem_inc(s("work_free"), -1)

                if act_copy:
                    @block.scalar
                    def _(act):
                        act.preload_act_table(ACT.Exp)
                        def step(j):
                            if types:
                                act_onehot(act)
                            act_weights(act)
                            act_copy(act, j + 1, landed)

                        def turn(b):
                            act_copy_turned(act, 0)
                            act_attr_load(act, 0, makes_features + b + 1)

                        if types:
                            act_onehot(act)
                        act_copy(act, 0, landed)
                        if makes_features:
                            act.sem_inc(s("fts_free0"), 16)
                            act_attr_load(act, 0, makes_features)
                            first_chunk, end = block_range(act, 0)
                            with act.Fori(first_chunk, end) as j:
                                step(j)
                        with act.Fori(1 if makes_features else 0, NB - 1) as b:
                            first_chunk, end = block_range(act, b)
                            if makes_features:
                                step(first_chunk)
                                turn(b - 1)
                                with act.Fori(first_chunk + 1, end) as j:
                                    step(j)
                                act_store_features(act, 0, makes_features + b - 1)
                            else:
                                with act.Fori(first_chunk, end) as j:
                                    step(j)
                            if act_after:
                                act_after(act)
                        first_chunk, end = block_range(act, NB - 1)
                        if makes_features:
                            step(first_chunk)
                            turn(NB - 2)
                            with act.Fori(first_chunk + 1, end - 1) as j:
                                step(j)
                        else:
                            with act.Fori(first_chunk, end - 1) as j:
                                step(j)
                        act_weights(act)
                        if act_after:
                            act_after(act)
                        if makes_features:
                            act_store_features(act, 0, makes_features + NB - 2)
                            act_copy_turned(act, 0)
                            act_store_features(act, 0, makes_features + NB - 1)
                            act.wait_ge(s("fts_free0"), 16)
                            act.sem_inc(s("fts_free0"), -16)

                if pe_after:
                    @block.tensor
                    def _(pe):
                        def make_k(n, h):
                            if h == 0:
                                pe.wait_ge(s("onehot_in"), 1)
                                pe.sem_inc(s("onehot_in"), -1)
                            mine = slice(h * TYPES, (h + 1) * TYPES)
                            pe.wait_ge(s(f"rel_free{h}"), 1)
                            pe.sem_inc(s(f"rel_free{h}"), -1)
                            for k in range(HALF):
                                last = pe.matmul(ps_rel[h][:, k * D:(k + 1) * D], onehot[mine, :, k], rel[mine],
                                                 start=k == 0, stop=False, skip_group_check=True)
                            if h:
                                last.then_inc(s("onehot_free"), 1)
                            pe.wait_ge(landed[h], 16 * HALF * (n + 1))
                            pe.matmul(ps_rel[h][:].rearrange("p (s d) -> p s d", d=D), ident[:], rows[h][:, :, 0:D],
                                      start=False, stop=True, skip_group_check=True).then_inc(s("pe_chain"), 1)
                            pe.wait_ge(s("pe_chain"), 1)
                            pe.sem_inc(s("pe_chain"), -1)
                            pe.sem_inc(s(f"rel_ready{h}"), 1)
                            pe.sem_inc(s(f"rows_free{h}"), 1)

                        def block_end():
                            if makes_features:
                                pe_turn_edges(pe, 0)
                            pe_after(pe)
                            if makes_features:
                                pe_features(pe, 0)

                        if types:
                            pe.sem_inc(s("onehot_free"), 1)
                            for h in range(2):
                                pe.sem_inc(s(f"rel_free{h}"), 1)
                            for h in range(2):
                                make_k(0, h)
                        with pe.Fori(0, NB - 1) as b:
                            if types:
                                first_chunk, end = block_range(pe, b)
                                with pe.Fori(first_chunk, end - 1) as j:
                                    for h in range(2):
                                        make_k(j + 1, h)
                                make_k(end, 0)
                                pe_project(pe, wo0[:], D)
                                make_k(end, 1)
                            block_end()
                        if types:
                            first_chunk, end = block_range(pe, NB - 1)
                            with pe.Fori(first_chunk, end - 1) as j:
                                for h in range(2):
                                    make_k(j + 1, h)
                            pe_project(pe, wo0[:], D)
                        block_end()
                        if types:
                            pe.wait_ge(s("onehot_free"), 1)
                            pe.sem_inc(s("onehot_free"), -1)
                            for h in range(2):
                                pe.wait_ge(s(f"rel_free{h}"), 1)
                                pe.sem_inc(s(f"rel_free{h}"), -1)

        def pe_to_conv1(pe):
            pe_project(pe, w_g[0][:], D + REC)

        def pe_conv(pe):
            pe_project(pe, w_g[1][:], D + REC)

        edge_pass(0, land0, table[0], start_l0, chunk_l0, after_l0, act_copy_l0, None, pe_to_conv1, stage1, table[1],
                  types=True, copies=True, frees=2)
        edge_pass(1, land1, table[1], start_conv, chunk_conv, after_conv(0), act_copy_conv, None, pe_conv,
                  stage1, table[2], copies=True, makes_features=FEARLY)
        edge_pass(2, land1, table[2], start_conv, chunk_conv, after_conv(1), act_copy_conv, None, pe_conv,
                  stage1, table[3], copies=True, makes_features=FEARLY + NB)
        edge_pass(3, land1, table[3], start_conv, chunk_conv, after_conv(2), act_copy_conv, act_after_conv3,
                  lambda pe: pe_project(pe, w_l2[:], 3 * D), stage2, table[4], copies=True)
        place_c = sb("place_c", [EP, 1], I32)
        ft_c = sb("ft_c", [EP, REC])
        with nc.Block() as block:
            @block.sync
            def _(sp):
                with sp.If(is_unsorted(sp)):
                    with sp.Fori(0, EC) as c:
                        with nc.allow_non_contiguous_dma(reason="one word per edge"):
                            sp.dma_start(place_c[:], placed.rearrange("(p c) o -> p c o", p=EP)[:, bass.ds(c, 1)].rearrange("p c o -> p (c o)")).then_inc(s("ft_c_in"), 16)
                        sp.dma_start(ft_c[:], fts_d[:, bass.ds(c, 1)].rearrange("p c f -> p (c f)")).then_inc(s("ft_c_in"), 16)
                        sp.wait_ge(s("ft_c_stored"), 1)
                        sp.sem_inc(s("ft_c_stored"), -1)
                    sp.dma_start(rec_ft[0:E], ft_placed).then_inc(s("ft_copied"), 16)
                    sp.wait_ge(s("ft_copied"), 16)
                    sp.sem_inc(s("ft_copied"), -16)

            @block.gpsimd
            def _(pool):
                with pool.If(is_unsorted(pool)):
                    with pool.Fori(0, EC) as c:
                        pool.wait_ge(s("ft_c_in"), 32)
                        pool.sem_inc(s("ft_c_in"), -32)
                        pool.indirect_dma_start(ft_placed, bass.IndirectOffsetOnAxis(ap=place_c[:].bitcast(U32), axis=0),
                                                ft_c[:], None).then_inc(s("ft_placed_in"), 16)
                        pool.wait_ge(s("ft_placed_in"), 16 * c + 16)
                        pool.sem_inc(s("ft_c_stored"), 1)

        edge_pass(4, land2, table[4], start_l2, chunk_l2, after_l2, act_copy_l2, None,
                  lambda pe: pe_project(pe, wo2[:], D), stage2, table[5], mask=True, features=True, copies=True)
        edge_pass(5, land2, table[5], start_l3, chunk_l3, after_l3, None, None, None, stage2, out,
                  numbered=True)


INPUTS = ["x", "src", "dst", "edge_attr_64", "edge_type_64", "edge_weight1", "node_vec1"]
INPUTS += ["L0_gnn_" + n for n in "query_embedding relation_embeddings Wq bq Wk bk Wv bv Wo bo".split()]
INPUTS += ["L1_gnn_" + n for n in "W1 a_src1 a_dst1 b1 W2 a_src2 a_dst2 b2".split()]
INPUTS += ["L2_gnn_" + n for n in "Wq bq Wk bk Wv bv We be Wc1 bc1 Wc2 bc2 Wd1 bd1 Wd2 bd2 Wo bo gamma beta".split()]


def kernel(**inputs):
    import numpy as np
    import concourse.bacc as bacc
    from concourse.bass_utils import run_bass_kernel_spmd

    nc = bacc.Bacc("TRN2", target_bir_lowering=False, num_devices=1)
    arrays, args = {}, {}
    for name in INPUTS:
        data = np.ascontiguousarray(inputs[name])
        arrays["in_" + name] = data
        args[name] = nc.dram_tensor("in_" + name, data.shape, mybir.dt.from_np(data.dtype), kind="ExternalInput").ap()
    out = nc.dram_tensor("out_0", args["x"].shape, F32, kind="ExternalOutput").ap()
    program(nc, args, out)
    result = run_bass_kernel_spmd(nc, [arrays], core_ids=[0])
    return result.results[0]["out_0"]
```
